# Optimizing a Trainium2 kernel written in Bass

```python
import numpy as np
import jax
import jax.numpy as jnp

def _softmax(x, axis=-1):
    return jax.nn.softmax(x, axis=axis)

def _gelu(x):
    return jax.nn.gelu(x, approximate=True)

def _silu(x):
    return jax.nn.silu(x)

def _sigmoid(x):
    return jax.nn.sigmoid(x)

def _layernorm(x, axis=-1, eps=1e-05):
    m = jnp.mean(x, axis=axis, keepdims=True)
    v = jnp.var(x, axis=axis, keepdims=True)
    return (x - m) / jnp.sqrt(v + eps)

def _scatter_add(tgt, idx, src, axis=0):
    return tgt.at[idx].add(src)

def _segment_sum(src, seg, n):
    return jax.ops.segment_sum(src, seg, n)
kernel_name = 'mk_adaln_d1_jaxref_r8_110d16'

def setup_inputs(seed: int=0):
    np.random.seed(seed)
    _w = jnp.asarray

    def _L0_attn_setup():
        import jax, jax.numpy as jnp
        import numpy as np
        H = 256
        NH = 16
        NOPE = 128
        ROPE = 64
        VD = 128
        QR = 128
        KVR = 64
        ROPE_BASE = 10000.0
        EPS = 1e-06

        def rmsnorm(x, scale):
            var = jnp.mean(jnp.square(x), axis=-1, keepdims=True)
            return x * jax.lax.rsqrt(var + EPS) * scale

        def rope_cos_sin(seq_len, dim, offset=0):
            half = dim // 2
            inv_freq = 1.0 / ROPE_BASE ** (jnp.arange(half, dtype=jnp.float32) * 2.0 / dim)
            pos = jnp.arange(offset, offset + seq_len, dtype=jnp.float32)
            ang = pos[:, None] * inv_freq[None, :]
            return (jnp.cos(ang), jnp.sin(ang))

        def apply_rope_single(x, cos, sin):
            x1 = x[..., ::2]
            x2 = x[..., 1::2]
            c = cos[None, None, :, :]
            s = sin[None, None, :, :]
            rotated = jnp.stack([x1 * c - x2 * s, x1 * s + x2 * c], axis=-1)
            return rotated.reshape(x.shape)
        key = jax.random.key(seed)
        ks = jax.random.split(key, 12)
        B, S = (2, 256)
        w = lambda k, shp: jax.random.normal(k, shp, dtype=jnp.float32) * 0.02
        return {'x': jax.random.normal(ks[0], (B, S, H), dtype=jnp.float32), 'W_cq': w(ks[1], (H, QR)), 'q_scale': jnp.ones((QR,), dtype=jnp.float32), 'W_dq_nope': w(ks[2], (QR, NH * NOPE)), 'W_dq_rope': w(ks[3], (QR, NH * ROPE)), 'W_ckv': w(ks[4], (H, KVR)), 'kv_scale': jnp.ones((KVR,), dtype=jnp.float32), 'W_dk_nope': w(ks[5], (KVR, NH * NOPE)), 'W_dv': w(ks[6], (KVR, NH * VD)), 'W_krope': w(ks[7], (H, ROPE)), 'W_o': w(ks[8], (NH * VD, H))}
    _L0_attn_in = _L0_attn_setup()

    def _L0_ffn_setup():
        import jax, jax.numpy as jnp
        import numpy as np
        DIM = 256
        HID = 704
        ZERO_POINT = 128.0

        def _qlinear(x, wq, scale):
            W = (wq.astype(jnp.float32) - ZERO_POINT) * scale[:, None]
            return jnp.einsum('bsd,hd->bsh', x, W)
        key = jax.random.key(seed)
        ks = jax.random.split(key, 7)
        B, S = (4, 256)
        sg = jax.random.uniform(ks[1], (HID,)) * (0.02 / np.sqrt(DIM)) + 0.0001
        su = jax.random.uniform(ks[3], (HID,)) * (0.02 / np.sqrt(DIM)) + 0.0001
        sd = jax.random.uniform(ks[5], (DIM,)) * (0.02 / np.sqrt(HID)) + 0.0001
        return {'x': jax.random.normal(ks[0], (B, S, DIM), dtype=jnp.float32), 'wq_gate': jax.random.randint(ks[2], (HID, DIM), 0, 32, dtype=jnp.int32), 's_gate': sg, 'wq_up': jax.random.randint(ks[4], (HID, DIM), 0, 32, dtype=jnp.int32), 's_up': su, 'wq_down': jax.random.randint(ks[6], (DIM, HID), 0, 32, dtype=jnp.int32), 's_down': sd}
    _L0_ffn_in = _L0_ffn_setup()
    _L0_c = _w((lambda *s: np.random.randn(*s).astype(np.float32) * 0.05)(1, 256))
    _L0_wmod = _w((lambda *s: np.random.randn(*s).astype(np.float32) * 0.05)(256, 6 * 256) * 256 ** (-0.5))
    _d = {'L0_attn_x': _L0_attn_in['x'], 'L0_attn_W_cq': _L0_attn_in['W_cq'], 'L0_attn_q_scale': _L0_attn_in['q_scale'], 'L0_attn_W_dq_nope': _L0_attn_in['W_dq_nope'], 'L0_attn_W_dq_rope': _L0_attn_in['W_dq_rope'], 'L0_attn_W_ckv': _L0_attn_in['W_ckv'], 'L0_attn_kv_scale': _L0_attn_in['kv_scale'], 'L0_attn_W_dk_nope': _L0_attn_in['W_dk_nope'], 'L0_attn_W_dv': _L0_attn_in['W_dv'], 'L0_attn_W_krope': _L0_attn_in['W_krope'], 'L0_attn_W_o': _L0_attn_in['W_o'], 'L0_ffn_wq_gate': _L0_ffn_in['wq_gate'], 'L0_ffn_s_gate': _L0_ffn_in['s_gate'], 'L0_ffn_wq_up': _L0_ffn_in['wq_up'], 'L0_ffn_s_up': _L0_ffn_in['s_up'], 'L0_ffn_wq_down': _L0_ffn_in['wq_down'], 'L0_ffn_s_down': _L0_ffn_in['s_down'], 'L0_c': _L0_c, 'L0_wmod': _L0_wmod}
    _x0 = _d['L0_attn_x']
    _d['L0_attn_x'] = jax.random.normal(jax.random.fold_in(jax.random.key(seed), 1), (1, 2048, 256), dtype=_x0.dtype)
    del _x0
    return _d

def reference(L0_attn_x, L0_attn_W_cq, L0_attn_q_scale, L0_attn_W_dq_nope, L0_attn_W_dq_rope, L0_attn_W_ckv, L0_attn_kv_scale, L0_attn_W_dk_nope, L0_attn_W_dv, L0_attn_W_krope, L0_attn_W_o, L0_ffn_wq_gate, L0_ffn_s_gate, L0_ffn_wq_up, L0_ffn_s_up, L0_ffn_wq_down, L0_ffn_s_down, L0_c, L0_wmod):

    def _L0_attn_ref(x, W_cq, q_scale, W_dq_nope, W_dq_rope, W_ckv, kv_scale, W_dk_nope, W_dv, W_krope, W_o):
        import jax, jax.numpy as jnp
        import numpy as np
        H = 256
        NH = 16
        NOPE = 128
        ROPE = 64
        VD = 128
        QR = 128
        KVR = 64
        ROPE_BASE = 10000.0
        EPS = 1e-06

        def rmsnorm(x, scale):
            var = jnp.mean(jnp.square(x), axis=-1, keepdims=True)
            return x * jax.lax.rsqrt(var + EPS) * scale

        def rope_cos_sin(seq_len, dim, offset=0):
            half = dim // 2
            inv_freq = 1.0 / ROPE_BASE ** (jnp.arange(half, dtype=jnp.float32) * 2.0 / dim)
            pos = jnp.arange(offset, offset + seq_len, dtype=jnp.float32)
            ang = pos[:, None] * inv_freq[None, :]
            return (jnp.cos(ang), jnp.sin(ang))

        def apply_rope_single(x, cos, sin):
            x1 = x[..., ::2]
            x2 = x[..., 1::2]
            c = cos[None, None, :, :]
            s = sin[None, None, :, :]
            rotated = jnp.stack([x1 * c - x2 * s, x1 * s + x2 * c], axis=-1)
            return rotated.reshape(x.shape)
        B, S, _ = x.shape
        norm_q = rmsnorm(x @ W_cq, q_scale)
        q_nope = (norm_q @ W_dq_nope).reshape(B, S, NH, NOPE)
        q_rope = (norm_q @ W_dq_rope).reshape(B, S, NH, ROPE)
        norm_kv = rmsnorm(x @ W_ckv, kv_scale)
        k_nope = (norm_kv @ W_dk_nope).reshape(B, S, NH, NOPE)
        value = (norm_kv @ W_dv).reshape(B, S, NH, VD)
        k_rope = (x @ W_krope).reshape(B, S, 1, ROPE)
        q_nope = q_nope.transpose(0, 2, 1, 3)
        q_rope = q_rope.transpose(0, 2, 1, 3)
        k_nope = k_nope.transpose(0, 2, 1, 3)
        k_rope = k_rope.transpose(0, 2, 1, 3)
        value = value.transpose(0, 2, 1, 3)
        cos, sin = rope_cos_sin(S, ROPE, offset=0)
        q_rope = apply_rope_single(q_rope, cos, sin)
        k_rope = apply_rope_single(k_rope, cos, sin) / NH
        full_head_dim = NOPE + ROPE
        query = jnp.concatenate([q_nope, q_rope], axis=-1)
        key = jnp.concatenate([k_nope, jnp.broadcast_to(k_rope, k_nope.shape[:-1] + (ROPE,))], axis=-1)
        scale = 1.0 / jnp.sqrt(jnp.asarray(full_head_dim, dtype=x.dtype))
        scores = jnp.einsum('bhqd,bhkd->bhqk', query, key) * scale
        causal = jnp.tril(jnp.ones((S, S), dtype=jnp.bool_))
        scores = jnp.where(causal[None, None, :, :], scores, -1000000000.0)
        attn = jax.nn.softmax(scores, axis=-1)
        out = jnp.einsum('bhqk,bhkd->bhqd', attn, value)
        out = out.transpose(0, 2, 1, 3).reshape(B, S, NH * VD)
        return out @ W_o

    def _L0_ffn_ref(x, wq_gate, s_gate, wq_up, s_up, wq_down, s_down):
        import jax, jax.numpy as jnp
        import numpy as np
        DIM = 256
        HID = 704
        ZERO_POINT = 128.0

        def _qlinear(x, wq, scale):
            W = (wq.astype(jnp.float32) - ZERO_POINT) * scale[:, None]
            return jnp.einsum('bsd,hd->bsh', x, W)
        gate = _qlinear(x, wq_gate, s_gate)
        gate = jax.nn.silu(gate)
        up = _qlinear(x, wq_up, s_up)
        return _qlinear(gate * up, wq_down, s_down)
    x = L0_attn_x
    mod = (_silu(L0_c) @ L0_wmod).reshape(L0_c.shape[0], 6, 1, -1)
    sa, ca, ga, sb, cb, gb = (mod[:, 0], mod[:, 1], mod[:, 2], mod[:, 3], mod[:, 4], mod[:, 5])
    ga = (2 * (ga >= 0) - 1) * jnp.maximum(jnp.abs(ga), 0.25)
    gb = (2 * (gb >= 0) - 1) * jnp.maximum(jnp.abs(gb), 0.25)
    h = _layernorm(x, axis=-1) * (1 + ca) + sa
    x = x + ga * _L0_attn_ref(h, L0_attn_W_cq, L0_attn_q_scale, L0_attn_W_dq_nope, L0_attn_W_dq_rope, L0_attn_W_ckv, L0_attn_kv_scale, L0_attn_W_dk_nope, L0_attn_W_dv, L0_attn_W_krope, L0_attn_W_o)
    h = _layernorm(x, axis=-1) * (1 + cb) + sb
    x = x + gb * _L0_ffn_ref(h, L0_ffn_wq_gate, L0_ffn_s_gate, L0_ffn_wq_up, L0_ffn_s_up, L0_ffn_wq_down, L0_ffn_s_down)
    return x

_drawn_inputs = setup_inputs


def setup_inputs(seed=0):
    import zlib

    import numpy as np

    out = dict(_drawn_inputs(seed))
    spreads = {'L0_attn_q_scale': (1.0, 0.6), 'L0_attn_kv_scale': (1.0, 0.6)}
    factors = {'L0_attn_W_cq': 8.0,
     'L0_attn_W_dq_nope': 8.0,
     'L0_attn_W_dq_rope': 8.0,
     'L0_attn_W_ckv': 8.0,
     'L0_attn_W_dk_nope': 8.0,
     'L0_attn_W_dv': 8.0,
     'L0_attn_W_krope': 8.0,
     'L0_attn_W_o': 8.0,
     'L0_ffn_s_gate': 8.0,
     'L0_ffn_s_up': 8.0,
     'L0_ffn_s_down': 8.0,
     'L0_c': 8.0,
     'L0_wmod': 8.0}
    for name, (base, spread) in spreads.items():
        noise = np.random.default_rng([zlib.crc32(name.encode()), seed]).standard_normal(out[name].shape)
        drawn = base * np.exp(spread * noise) if base else spread * noise
        out[name] = jnp.asarray(drawn.astype(out[name].dtype))
    for name, factor in factors.items():
        out[name] = (out[name] * factor).astype(out[name].dtype)
    return out
```

```python
from contextlib import ExitStack

import numpy as np

import concourse.bass as bass
from concourse import mybir

F32 = mybir.dt.float32
F32R = mybir.dt.float32r
BF16 = mybir.dt.bfloat16
F16 = mybir.dt.float16
I32 = mybir.dt.int32
ALU = mybir.AluOpType
ACT = mybir.ActivationFunctionType
AX_X = mybir.AxisListType.X

P = 128
S = 2048
D = 256
DF = D // P
NH = 16
NOPE, ROPE, VD = 128, 64, 128
QR, KVR = 128, 64
HALF = ROPE // 2
HID, HIDP = 704, 768
HT = HIDP // P
ZERO_POINT = 128.0
NT = S // P
CH = 512
NC = S // CH
TPC = CH // P
RMS_EPS, LN_EPS = 1e-6, 1e-5
SCORE_SCALE = float((NOPE + ROPE) ** -0.5)
MASKED = -1e30
PSCALE = 1024.0

UNITS = [(i * P + P + CH - 1) // CH for i in range(NT)]
FIRST = [sum(UNITS[:i]) for i in range(NT)]
NU = sum(UNITS)
TILE_OF = [i for i in range(NT) for _ in range(UNITS[i])]
LEAD_S = 5
LEAD_E = 2
QP_AFTER = {2: 0, 8: 1, 20: 2, 35: 3}
PSLOTS = 5
assert NU % LEAD_S == 0 and NU % PSLOTS == 0

USE_T, USE_Q = {}, {}
for _g in range(NU):
    USE_T[_g] = len(USE_T) + len(USE_Q)
    if _g in QP_AFTER:
        USE_Q[QP_AFTER[_g]] = len(USE_T) + len(USE_Q)
USES = len(USE_T) + len(USE_Q)
MULTI = sum(u for u in UNITS if u > 1)
assert USES % 2 == 0


def width(g):
    i = TILE_OF[g]
    return min(CH, (i + 1) * P - (g - FIRST[i]) * CH)


def multi_before(g):
    return sum(1 for j in range(g + 1) if UNITS[TILE_OF[j]] > 1)


def pv_pieces():
    at = {}
    for c in range(NC - 1):
        for r in range(TPC):
            n = TPC * (c + 1) + r
            at[FIRST[n] + (1 if r == 0 else 0)] = (c, list(range((c + 1) * r, (c + 1) * (r + 1))))
    return at


PV_AT = pv_pieces()
O_AFTER = {FIRST[TPC * c + 7] + 1: c for c in range(NC - 1)}


def adaln_block(nc, x, w_cq, q_scale, w_qn, w_qr, w_ckv, kv_scale, w_kn, w_v, w_kr, w_o,
                wq_gate, s_gate, wq_up, s_up, wq_down, s_down, cond, w_mod,
                ident_in, mask_in, cos_q, sin_q, cos_k, sin_k, out):
    rl_dram = nc.dram_tensor("rl_scratch", [S], F32).ap()
    ot_dram = nc.dram_tensor("ot_scratch", [NH * KVR, S], F32).ap()

    with ExitStack() as whole:
        def alloc(ctx, name, shape, dt):
            return ctx.enter_context(nc.sbuf_tensor(name, shape, dt))

        def sem(name, ctx=whole):
            return ctx.enter_context(nc.semaphore(name))

        ident = alloc(whole, "ident", [P, P], F32)
        identb = alloc(whole, "identb", [P, P], BF16)
        maskb = alloc(whole, "maskb", [P, P], BF16)
        mod = alloc(whole, "mod", [P, 12], F32)
        eps = alloc(whole, "eps", [P, 2], F32)
        kvs = alloc(whole, "kvs", [KVR, 1], F32)
        SA, CA, GA, SB, CB, GB = (mod[:, 2 * k:2 * k + 2] for k in range(6))

        pv_done = sem("pv_done")
        o_taken = sem("o_taken")
        on_ready = sem("on_ready")

        att = ExitStack()
        k_hi = alloc(att, "k_hi", [P, S], F32R)
        k_lo = alloc(att, "k_lo", [P, S], F32R)
        nq_hi = alloc(att, "nq_hi", [P, S], F32R)
        nq_lo = alloc(att, "nq_lo", [P, S], F32R)
        vals = alloc(att, "vals", [P, NT, 2 * KVR], F16)
        wq_hi = alloc(att, "wq_hi", [P, NH + 2, P], F32R)
        wq_lo = alloc(att, "wq_lo", [P, NH + 2, P], F32R)
        lsum = alloc(att, "lsum", [P, NT, 4], F32)

        g = dict(locals())
        prepare(nc, g, alloc)
        attend(nc, g, alloc)
        att.close()
        finish(nc, g, alloc)


def prepare(nc, g, alloc):
    (x, w_cq, q_scale, w_qn, w_qr, w_ckv, kv_scale, w_kn, w_kr, cond, w_mod, ident_in, mask_in, cos_k, sin_k) = (
        g[k] for k in ("x", "w_cq", "q_scale", "w_qn", "w_qr", "w_ckv", "kv_scale", "w_kn", "w_kr", "cond",
                       "w_mod", "ident_in", "mask_in", "cos_k", "sin_k"))
    ident, identb, maskb, mod, eps, kvs = (g[k] for k in ("ident", "identb", "maskb", "mod", "eps", "kvs"))
    SA, CA = g["SA"], g["CA"]
    k_hi, k_lo, nq_hi, nq_lo, vals = (g[k] for k in ("k_hi", "k_lo", "nq_hi", "nq_lo", "vals"))
    wq_hi, wq_lo, lsum = g["wq_hi"], g["wq_lo"], g["lsum"]

    with ExitStack() as ctx:
        def sb(name, shape, dt=F32):
            return alloc(ctx, name, shape, dt)

        def sem(name):
            return ctx.enter_context(nc.semaphore(name))

        xs = sb("xs", [P, NT, D])
        xn = sb("xn", [P, NT, D])
        st = sb("st", [P, NT, 6])
        mv = sb("mv", [P, NT, 2])
        sd = sb("sd", [P, NT])
        rstd = sb("rstd", [P, NT])
        h32 = sb("h32", [P, 2, DF, CH])
        h_hi = sb("h_hi", [P, 2, DF, CH], F32R)
        h_lo = sb("h_lo", [P, 2, DF, CH], F32R)
        wx = sb("wx", [P, DF, D])
        wkr = sb("wkr", [P, DF, ROPE])
        wx_hi = sb("wx_hi", [P, DF, D], F32R)
        wx_lo = sb("wx_lo", [P, DF, D], F32R)
        z = sb("z", [P, NT, D])
        ss = sb("ss", [P, 2, NT])
        sdz = sb("sdz", [P, 2, NT])
        rz = sb("rz", [P, 2, NT])
        sq, nqn = xs[:, :, 0:P], xs[:, :, P:D]
        kk = sb("kk", [P, NT, P])
        ck = sb("ck", [P, NT, HALF])
        sk = sb("sk", [P, NT, HALF])
        r1 = sb("r1", [P, 4, NT, HALF])
        wqn = sb("wqn", [P, NH, NOPE])
        wqr = sb("wqr", [P, NH, HALF, 2])
        wkn = sb("wkn", [KVR, NH, NOPE])
        wqT = sb("wqT", [P, NH, QR])
        wkT = sb("wkT", [P, NH, KVR])
        wqa = sb("wqa", [P, NH, P])
        qs = sb("qs", [P, 1])
        cs = sb("cs", [P, 2])
        wm = sb("wm", [P, 2, 6 * D])
        sc = sb("sc", [P, 2])
        mk32 = sb("mk32", [P, P])
        gt = sb("gt", [P, 2, 4])
        banks = [ctx.enter_context(nc.psum_tensor(f"prep{b}", [P, CH], F32)) for b in range(8)]

        jobs = [("wqT", k) for k in range(4)] + [("wkT", k) for k in range(2)]
        jobs += [("mod", 0)]
        for c in range(NC):
            jobs += [("xT", c, f) for f in range(DF)]
            if c == 0:
                jobs += [("A", k) for k in range(2)]
            if c:
                jobs += [("z", c - 1, k) for k in range(2)]
        jobs += [("z", NC - 1, k) for k in range(2)]
        for c in range(NC):
            jobs += [("nT", c), ("kT", c)]
        index = {j: n for n, j in enumerate(jobs)}

        pe_done = sem("pe_done")
        freed = [sem(f"freed{b}") for b in range(8)]
        dve_chain, act_chain = sem("dve_chain"), sem("act_chain")
        s_small, s_wqk, s_wx, s_wm, s_tab = sem("s_small"), sem("s_wqk"), sem("s_wx"), sem("s_wm"), sem("s_tab")
        s_x = [sem(f"s_x{c}") for c in range(NC)]
        consts_ready = sem("consts_ready")
        wkn_ready = sem("wkn_ready")
        var_ready = sem("var_ready")
        sd_ready = sem("sd_ready")
        xn_ready = sem("xn_ready")
        silu_ready = sem("silu_ready")
        mod_ready = sem("mod_ready")
        wx_ready = sem("wx_ready")
        h_split = sem("h_split")
        ss_ready = sem("ss_ready")
        sdz_ready = sem("sdz_ready")
        nk_ready = sem("nk_ready")
        hi_ready = sem("hi_ready")

        def bank(job):
            return banks[index[job] % 8]

        def job_done(eng, job):
            eng.wait_ge(pe_done, index[job] + 1)

        def taken(eng, job):
            eng.wait_ge(freed[index[job] % 8], index[job] // 8 + 1)

        class Order:

            def __init__(self, eng, chain):
                self.eng, self.chain, self.count, self.last = eng, chain, {}, None

            def did(self, ins, signal=None):
                s = signal if signal is not None else self.chain
                self.count[id(s)] = self.count.get(id(s), 0) + 1
                ins.then_inc(s, 1)
                self.last = (s, self.count[id(s)])

            def own(self):
                self.eng.wait_ge(*self.last)

        def free(ins, job):
            ins.then_inc(freed[index[job] % 8], 1)

        block = ctx.enter_context(nc.Block())

        @block.sync
        def _(sp):
            sp.dma_start(ident[:, :], ident_in).then_inc(s_small, 16)
            sp.dma_start(mk32[:, :], mask_in).then_inc(s_small, 16)
            sp.dma_start(qs[:, :], q_scale.rearrange("(p a) -> p a", a=1)).then_inc(s_small, 16)
            sp.dma_start(kvs[:, :], kv_scale.rearrange("(p a) -> p a", a=1)).then_inc(s_small, 16)
            for k in range(2):
                sp.dma_start(cs[:, k:k + 1], cond[0, k * P:(k + 1) * P].rearrange("(p a) -> p a", a=1)).then_inc(s_small, 16)
            xv = x.rearrange("a (t p) d -> p (a t) d", p=P)
            for c in range(NC):
                sp.dma_start(xs[:, c * TPC:(c + 1) * TPC, :], xv[:, c * TPC:(c + 1) * TPC, :]).then_inc(s_x[c], 16)
            sp.dma_start(wm[:, :, :], w_mod.rearrange("(k p) n -> p k n", p=P)).then_inc(s_wm, 16)

        @block.gpsimd
        def _(pool):
            pool.dma_start(wkn[:, :, :], w_kn.rearrange("r (h n) -> r h n", h=NH)).then_inc(s_wqk, 16)
            pool.dma_start(wqn[:, :, :], w_qn.rearrange("r (h n) -> r h n", h=NH)).then_inc(s_wqk, 16)
            pool.dma_start(wqr[:, :, :, :], w_qr.rearrange("r (h i e) -> r h i e", h=NH, e=2)).then_inc(s_wqk, 16)
            pool.dma_start(wx[:, :, 0:QR], w_cq.rearrange("(k p) n -> p k n", p=P)).then_inc(s_wx, 16)
            pool.dma_start(wx[:, :, QR:QR + KVR], w_ckv.rearrange("(k p) n -> p k n", p=P)).then_inc(s_wx, 16)
            pool.dma_start(wkr[:, :, :], w_kr.rearrange("(k p) n -> p k n", p=P)).then_inc(s_wx, 16)
            pool.dma_start(ck[:, :, :], cos_k.rearrange("(t p) i -> p t i", p=P)).then_inc(s_tab, 16)
            pool.dma_start(sk[:, :, :], sin_k.rearrange("(t p) i -> p t i", p=P)).then_inc(s_tab, 16)

        @block.vector
        def _(dve):
            o = Order(dve, dve_chain)
            did, own = o.did, o.own
            dve.memset(eps[:, 0:1], LN_EPS).then_inc(g["pv_done"], 2)
            dve.memset(eps[:, 1:2], RMS_EPS).then_inc(g["o_taken"], 1)
            dve.memset(lsum[:, :, :], 0.0).then_inc(g["on_ready"], NC)
            did(dve.memset(wq_hi[:, NH:NH + 2, :].bitcast(mybir.dt.uint32), 0))
            did(dve.memset(wq_lo[:, NH:NH + 2, :].bitcast(mybir.dt.uint32), 0))
            dve.wait_ge(s_small, 16 * 6)
            did(dve.tensor_copy(identb[:, :], ident[:, :]))
            did(dve.tensor_copy(maskb[:, :], mk32[:, :]), consts_ready)
            did(dve.tensor_scalar(qs[:, :], qs[:, :], SCORE_SCALE, None, ALU.mult))
            dve.wait_ge(s_wqk, 48)
            did(dve.tensor_scalar(wkn[:, :, :], wkn[:, :, :], kvs[:, 0:1], None, ALU.mult), wkn_ready)
            for c in range(NC):
                dve.wait_ge(s_x[c], 16)
                for t in range(c * TPC, (c + 1) * TPC):
                    did(dve.bn_stats(st[:, t, :], xs[:, t, :]))
            own()
            for t in range(NT):
                did(dve.bn_aggr(mv[:, t, :], st[:, t, :]), var_ready)
            dve.wait_ge(s_wx, 48)
            did(dve.tensor_copy(wx[:, :, QR + KVR:QR + KVR + HALF], wkr[:, :, 0::2]))
            did(dve.tensor_copy(wx[:, :, QR + KVR + HALF:D], wkr[:, :, 1::2]))
            own()
            did(dve.tensor_copy(wx_hi[:, :, :], wx[:, :, :]))
            own()
            did(dve.tensor_tensor(wx_lo[:, :, :], wx[:, :, :], wx_hi[:, :, :].bitcast(F32), ALU.subtract), wx_ready)
            dve.wait_ge(sd_ready, 1)
            did(dve.reciprocal(rstd[:, :], sd[:, :]))
            own()
            for t in range(NT):
                did(dve.tensor_scalar(xn[:, t, :], xs[:, t, :], mv[:, t, 0:1], rstd[:, t:t + 1],
                                      ALU.subtract, ALU.mult), xn_ready if t % TPC == TPC - 1 else None)
            job_done(dve, ("mod", 0))
            free(dve.tensor_copy(mod[:, :], bank(("mod", 0))[:, 0:12]), ("mod", 0))
            taken(dve, ("mod", 0))
            gates = mod[:, :].rearrange("p (s k f) -> p s k f", s=2, k=3)[:, :, 2, :]
            sign, size = gt[:, :, 0:2], gt[:, :, 2:4]
            did(dve.tensor_scalar(sign, gates, 0.0, 2.0, ALU.is_ge, ALU.mult))
            did(dve.tensor_scalar(size, gates, -1.0, None, ALU.mult))
            own()
            did(dve.tensor_scalar(sign, sign, -1.0, None, ALU.add))
            did(dve.tensor_tensor(size, gates, size, ALU.max))
            own()
            did(dve.tensor_scalar(size, size, 0.25, None, ALU.max))
            for base in (2, 8):
                did(dve.tensor_scalar(mod[:, base:base + 2], mod[:, base:base + 2], 1.0, None, ALU.add))
            own()
            did(dve.tensor_tensor(gates, sign, size, ALU.mult), mod_ready)

            for c in range(NC):
                if c >= 2:
                    job_done(dve, ("z", c - 2, 1))
                for f in range(DF):
                    taken(dve, ("xT", c, f))
                    did(dve.tensor_copy(h_hi[:, c % 2, f, :], h32[:, c % 2, f, :]))
                    own()
                    did(dve.tensor_tensor(h_lo[:, c % 2, f, :], h32[:, c % 2, f, :],
                                          h_hi[:, c % 2, f, :].bitcast(F32), ALU.subtract), h_split)
                if c == 0:
                    for k in range(2):
                        job_done(dve, ("A", k))
                        free(dve.tensor_scalar(wqa[:, 8 * k:8 * k + 8, 0:KVR],
                                               bank(("A", k))[:, :].rearrange("p (h j) -> p h j", h=8),
                                               qs[:, 0:1], None, ALU.mult), ("A", k))
                    for e in range(2):
                        did(dve.tensor_scalar(wqa[:, :, KVR + HALF * e:KVR + HALF * e + HALF], wqr[:, :, :, e],
                                              qs[:, 0:1], None, ALU.mult))
                    for k in range(2):
                        taken(dve, ("A", k))
                    own()
                    did(dve.tensor_copy(wq_hi[:, 0:NH, :], wqa[:, :, :]))
                    own()
                    did(dve.tensor_tensor(wq_lo[:, 0:NH, :], wqa[:, :, :], wq_hi[:, 0:NH, :].bitcast(F32),
                                          ALU.subtract))

            for c in range(NC):
                for k in range(2):
                    taken(dve, ("z", c, k))
            did(dve.tensor_tensor(sq[:, :, :], z[:, :, 0:QR], z[:, :, 0:QR], ALU.mult))
            own()
            did(dve.tensor_reduce(ss[:, 0, :], sq[:, :, :], AX_X, ALU.add))
            own()
            did(dve.tensor_tensor(sq[:, :, 0:KVR], z[:, :, QR:QR + KVR], z[:, :, QR:QR + KVR], ALU.mult))
            own()
            did(dve.tensor_reduce(ss[:, 1, :], sq[:, :, 0:KVR], AX_X, ALU.add))
            own()
            did(dve.tensor_scalar(ss[:, 0, :], ss[:, 0, :], 1.0 / QR, None, ALU.mult))
            did(dve.tensor_scalar(ss[:, 1, :], ss[:, 1, :], 1.0 / KVR, None, ALU.mult), ss_ready)
            dve.wait_ge(s_tab, 32)
            even, odd = z[:, :, QR + KVR:QR + KVR + HALF], z[:, :, QR + KVR + HALF:D]
            for k, (a, b) in enumerate(((even, ck), (odd, sk), (even, sk), (odd, ck))):
                did(dve.tensor_tensor(r1[:, k, :, :], a, b[:, :, :], ALU.mult))
            own()
            did(dve.tensor_tensor(kk[:, :, KVR:KVR + HALF], r1[:, 0, :, :], r1[:, 1, :, :], ALU.subtract))
            did(dve.tensor_tensor(kk[:, :, KVR + HALF:P], r1[:, 2, :, :], r1[:, 3, :, :], ALU.add))
            dve.wait_ge(sdz_ready, 1)
            did(dve.reciprocal(rz[:, :, :], sdz[:, :, :]))
            own()
            for t in range(NT):
                did(dve.tensor_scalar(nqn[:, t, :], z[:, t, 0:QR], rz[:, 0, t:t + 1], None, ALU.mult))
                did(dve.tensor_scalar(kk[:, t, 0:KVR], z[:, t, QR:QR + KVR], rz[:, 1, t:t + 1], None, ALU.mult),
                    nk_ready if t % TPC == TPC - 1 else None)
            own()
            did(dve.tensor_copy(vals[:, :, 0:KVR], kk[:, :, 0:KVR]))
            own()
            did(dve.tensor_tensor(vals[:, :, KVR:2 * KVR], kk[:, :, 0:KVR], vals[:, :, 0:KVR], ALU.subtract))
            for c in range(NC):
                for k, (kind, hi, lo) in enumerate((("nT", nq_hi, nq_lo), ("kT", k_hi, k_lo))):
                    cols = slice(c * CH, (c + 1) * CH)
                    dve.wait_ge(hi_ready, 2 * c + k + 1)
                    free(dve.tensor_tensor(lo[:, cols], bank((kind, c))[:, :], hi[:, cols].bitcast(F32),
                                           ALU.subtract), (kind, c))

        @block.scalar
        def _(act):
            act.wait_ge(s_small, 16 * 6)
            act.activation(sc[:, :], cs[:, :], ACT.Silu).then_inc(silu_ready, 1)
            for k in range(4):
                job_done(act, ("wqT", k))
                free(act.activation(wqT[:, 4 * k:4 * k + 4, :].rearrange("p h n -> p (h n)"),
                                    bank(("wqT", k))[:, :], ACT.Copy), ("wqT", k))
            for k in range(2):
                job_done(act, ("wkT", k))
                free(act.activation(wkT[:, 8 * k:8 * k + 8, :].rearrange("p h n -> p (h n)"),
                                    bank(("wkT", k))[:, :], ACT.Copy), ("wkT", k))
            act.wait_ge(var_ready, NT)
            act.activation(sd[:, :], mv[:, :, 1], ACT.Sqrt, bias=eps[:, 0:1]).then_inc(sd_ready, 1)
            act.wait_ge(mod_ready, 1)

            def take_z(c):
                for k in range(2):
                    job_done(act, ("z", c, k))
                    t = c * TPC + 2 * k
                    free(act.activation(z[:, t:t + 2, :].rearrange("p t n -> p (t n)"), bank(("z", c, k))[:, :],
                                        ACT.Copy), ("z", c, k))

            for c in range(NC):
                for f in range(DF):
                    job_done(act, ("xT", c, f))
                    if c >= 2:
                        act.wait_ge(h_split, 2 * (c - 2) + f + 1)
                    free(act.activation(h32[:, c % 2, f, :], bank(("xT", c, f))[:, :], ACT.Identity,
                                        bias=SA[:, f:f + 1], scale=CA[:, f:f + 1]), ("xT", c, f))
                if c:
                    take_z(c - 1)
            take_z(NC - 1)
            act.wait_ge(ss_ready, 1)
            act.activation(sdz[:, :, :].rearrange("p a t -> p (a t)"), ss[:, :, :].rearrange("p a t -> p (a t)"),
                           ACT.Sqrt, bias=eps[:, 1:2]).then_inc(sdz_ready, 1)
            for c in range(NC):
                for kind, hi in (("nT", nq_hi), ("kT", k_hi)):
                    job_done(act, (kind, c))
                    act.activation(hi[:, c * CH:(c + 1) * CH], bank((kind, c))[:, :], ACT.Copy).then_inc(hi_ready, 1)

        @block.tensor
        def _(pe):
            pe.wait_ge(s_small, 16 * 6)
            for n, job in enumerate(jobs):
                kind, b = job[0], bank(job)
                if n >= 8:
                    pe.wait_ge(freed[n % 8], n // 8)
                if kind == "wqT":
                    pe.wait_ge(s_wqk, 48)
                    for k in range(4):
                        last = pe.transpose(b[:, k * P:(k + 1) * P], wqn[:, 4 * job[1] + k, :], ident[:, :])
                elif kind == "wkT":
                    pe.wait_ge(wkn_ready, 1)
                    for k in range(8):
                        last = pe.transpose(b[:, k * KVR:(k + 1) * KVR], wkn[:, 8 * job[1] + k, :], ident[0:KVR, 0:KVR])
                elif kind == "mod":
                    pe.wait_ge(s_wm, 16)
                    pe.wait_ge(silu_ready, 1)
                    for m in range(12):
                        for k in range(2):
                            last = pe.matmul(b[:, m:m + 1], wm[:, k, m * P:(m + 1) * P], sc[:, k:k + 1],
                                             start=(k == 0), stop=(k == 1))
                elif kind == "A":
                    if job[1] == 0:
                        for k in range(2):
                            taken(pe, ("wkT", k))
                        for k in range(4):
                            taken(pe, ("wqT", k))
                    for k in range(8):
                        h = 8 * job[1] + k
                        last = pe.matmul(b[:, k * KVR:(k + 1) * KVR], wqT[:, h, :], wkT[:, h, :], start=True, stop=True)
                elif kind == "xT":
                    c, f = job[1:]
                    pe.wait_ge(xn_ready, c + 1)
                    for k in range(TPC):
                        last = pe.transpose(b[:, k * P:(k + 1) * P], xn[:, c * TPC + k, f * P:(f + 1) * P], ident[:, :])
                elif kind == "z":
                    c, half = job[1:]
                    pe.wait_ge(h_split, 2 * c + 2)
                    pe.wait_ge(wx_ready, 1)
                    for k in range(2):
                        tok = slice((2 * half + k) * P, (2 * half + k + 1) * P)
                        passes = [(a, w, f) for f in range(DF) for a, w in ((h_hi, wx_hi), (h_hi, wx_lo), (h_lo, wx_hi))]
                        for q, (a, w, f) in enumerate(passes):
                            last = pe.matmul(b[:, k * D:(k + 1) * D], a[:, c % 2, f, tok], w[:, f, :],
                                             start=(q == 0), stop=(q == len(passes) - 1))
                else:
                    c = job[1]
                    pe.wait_ge(nk_ready, c + 1)
                    src = nqn if kind == "nT" else kk
                    for k in range(TPC):
                        last = pe.transpose(b[:, k * P:(k + 1) * P], src[:, c * TPC + k, :], ident[:, :])
                last.then_inc(pe_done, 1)


def attend(nc, g, alloc):
    k_hi, k_lo, nq_hi, nq_lo, vals = (g[k] for k in ("k_hi", "k_lo", "nq_hi", "nq_lo", "vals"))
    wq_hi, wq_lo, lsum = g["wq_hi"], g["wq_lo"], g["lsum"]
    ident, identb, maskb = g["ident"], g["identb"], g["maskb"]
    cos_q, sin_q, rl_dram, ot_dram = g["cos_q"], g["sin_q"], g["rl_dram"], g["ot_dram"]
    pv_done, o_taken, on_ready = g["pv_done"], g["o_taken"], g["on_ready"]

    with ExitStack() as ctx:
        def sb(name, shape, dt=F32):
            return alloc(ctx, name, shape, dt)

        def sem(name):
            return ctx.enter_context(nc.semaphore(name))

        wh_hi = sb("wh_hi", [P, P], F32R)
        wh_lo = sb("wh_lo", [P, P], F32R)
        q_hi = sb("q_hi", [P, S], F32R)
        q_lo = sb("q_lo", [P, S], F32R)
        y = sb("y", [P, CH])
        w = sb("w", [P, CH])
        zeros = sb("zeros", [P, CH])
        cosr = sb("cosr", [P, S])
        sinr = sb("sinr", [P, S])
        prob = sb("prob", [P, PSLOTS, CH])
        pt = [[sb(f"pt{b}{part}", [P, n, CH], F16) for part in ("hi", "lo")] for b, n in ((0, 12), (1, 16))]
        mx = sb("mx", [P, NT, 4])
        nm = sb("nm", [P, NT])
        l = sb("l", [P, NT])
        rl = sb("rl", [P, 32])
        rlT = sb("rlT", [P, 32])
        tmp = sb("tmp", [KVR, CH])
        oraw = sb("oraw", [KVR, S])
        rb = sb("rb", [KVR, S])
        on = sb("on", [KVR, S])
        sbank = [ctx.enter_context(nc.psum_tensor(f"scores{b}", [P, CH], F32)) for b in range(LEAD_S)]
        tbank = [ctx.enter_context(nc.psum_tensor(f"turned{b}", [P, CH], F32)) for b in range(2)]
        obank = ctx.enter_context(nc.psum_tensor("outputs", [P, CH], F32))

        s_tab = sem("s_tabq")
        wh_ready = sem("wh_ready")
        qp_done = sem("qp_done")
        lat_taken = sem("lat_taken")
        rope_ready = sem("rope_ready")
        q_ready = sem("q_ready")
        pool_chain = sem("pool_chain")
        scored = sem("scored")
        unit_max = sem("unit_max")
        max_ready = sem("max_ready")
        exp_done = sem("exp_done")
        turned = sem("turned")
        hi_ready = sem("pthi_ready")
        t_free = sem("t_free")
        tmp_ready = sem("tmp_ready")
        l_chain = sem("l_chain")
        rl_ready = sem("rl_ready")
        rl_stored = sem("rl_stored")
        rb_loaded = sem("rb_loaded")
        ot_stored = sem("ot_stored")

        def after(h, per_head, k):
            return h * per_head + k

        ident_in = g["ident_in"]
        block = ctx.enter_context(nc.Block())

        @block.tensor
        def _(pe):
            def project(h, c, use):
                b, cols = tbank[use % 2], slice(c * CH, (c + 1) * CH)
                pe.matmul(b[:, :], wh_hi[:, :], nq_hi[:, cols], start=True, stop=False)
                pe.matmul(b[:, :], wh_hi[:, :], nq_lo[:, cols], start=False, stop=False)
                pe.matmul(b[:, :], wh_lo[:, :], nq_hi[:, cols], start=False, stop=True).then_inc(qp_done, 1)

            def score(u):
                i, n = TILE_OF[u], width(u)
                b, k0 = sbank[u % LEAD_S], (u - FIRST[i]) * CH
                q, k = slice(i * P, (i + 1) * P), slice(k0, k0 + n)
                pe.matmul(b[:, 0:n], q_hi[:, q], k_hi[:, k], start=True, stop=False)
                pe.matmul(b[:, 0:n], q_hi[:, q], k_lo[:, k], start=False, stop=False)
                if u == FIRST[i] + UNITS[i] - 1:
                    pe.matmul(b[:, n - P:n], identb[:, :], maskb[:, :], start=False, stop=False)
                pe.matmul(b[:, 0:n], q_lo[:, q], k_hi[:, k], start=False, stop=True).then_inc(scored, 1)

            def values(c, blocks):
                for j in blocks:
                    q0 = max(0, j - TPC * c) * P
                    for part in range(2):
                        first, last = j == 0 and part == 0, j == TPC * c + TPC - 1 and part == 1
                        ins = pe.matmul(obank[:, q0:CH], vals[:, j, :], pt[c % 2][part][:, j, q0:CH],
                                        start=first, stop=last)
                        if last:
                            ins.then_inc(pv_done, 1)

            pe.wait_ge(wh_ready, 1)
            for c in range(NC):
                if c >= 2:
                    pe.wait_ge(t_free, c - 1)
                project(0, c, c)
            pe.wait_ge(q_ready, 2)
            for u in range(LEAD_S):
                score(u)
            with pe.Fori(0, NH) as h:
                for u in range(NU):
                    use = NC + USE_T[u]
                    if u in PV_AT:
                        c, blocks = PV_AT[u]
                        if blocks[0] == 0:
                            last = FIRST[TPC * c + 3] + UNITS[TPC * c + 3] - 1
                            pe.wait_ge(t_free, after(h, USES, NC + USE_T[last] + 1))
                            pe.wait_ge(o_taken, after(h, NC, c + 1))
                        values(c, blocks)
                    pe.wait_ge(exp_done, after(h, NU, u + 1))
                    pe.wait_ge(t_free, after(h, USES, use - 1))
                    for k in range(width(u) // P):
                        ins = pe.transpose(tbank[use % 2][:, k * P:(k + 1) * P],
                                           prob[:, u % PSLOTS, k * P:(k + 1) * P], ident[:, :])
                    ins.then_inc(turned, 1)
                    n = (u + LEAD_S) % NU
                    if n == FIRST[TILE_OF[n]] and TILE_OF[n] % TPC == 0:
                        pe.wait_ge(q_ready, after(h, NC, (NC if u + LEAD_S >= NU else 0) + TILE_OF[n] // TPC + 1))
                    score(n)
                    if u in QP_AFTER:
                        c = QP_AFTER[u]
                        use = NC + USE_Q[c]
                        if c == 0:
                            pe.wait_ge(wh_ready, after(h, 1, 2))
                        pe.wait_ge(t_free, after(h, USES, use - 1))
                        project(h + 1, c, use)
                c = NC - 1
                pe.wait_ge(t_free, after(h, USES, NC + USE_T[NU - 1] + 1))
                pe.wait_ge(o_taken, after(h, NC, c + 1))
                values(c, range(NT))

        @block.vector
        def _(dve):
            def rotate(h, c, use, index):
                b, cols = tbank[use % 2], slice(c * CH, (c + 1) * CH)
                e, o = slice(KVR, KVR + HALF), slice(KVR + HALF, P)
                dve.wait_ge(qp_done, index + 1)
                if not (isinstance(index, int) and index == 0):
                    dve.wait_ge(q_ready, index)
                dve.tensor_tensor(y[KVR:P, :], b[KVR:P, :], cosr[KVR:P, cols], ALU.mult).then_inc(rope_ready, 1)
                dve.tensor_tensor(w[e, :], b[o, :], sinr[o, cols], ALU.mult).then_inc(rope_ready, 1)
                dve.wait_ge(lat_taken, index + 1)
                dve.tensor_tensor(w[o, :], b[e, :], sinr[e, cols], ALU.mult).then_inc(t_free, 1)

            def maximum(h, u):
                i, n, k = TILE_OF[u], width(u), u - FIRST[TILE_OF[u]]
                dve.wait_ge(scored, after(h, NU, u + 1))
                if UNITS[i] == 1:
                    dve.tensor_reduce(nm[:, i:i + 1], sbank[u % LEAD_S][:, 0:n], AX_X, ALU.max,
                                      negate=True).then_inc(max_ready, 1)
                    return
                dve.tensor_reduce(mx[:, i, k:k + 1], sbank[u % LEAD_S][:, 0:n], AX_X, ALU.max).then_inc(unit_max, 1)
                if k == UNITS[i] - 1:
                    dve.wait_ge(unit_max, after(h, MULTI, multi_before(u)))
                    dve.tensor_reduce(nm[:, i:i + 1], mx[:, i, 0:UNITS[i]], AX_X, ALU.max,
                                      negate=True).then_inc(max_ready, 1)

            def take_outputs(h, c):
                dve.wait_ge(on_ready, after(h, NC, NC))
                dve.wait_ge(tmp_ready, after(h, NC, c + 1))
                dve.scalar_tensor_tensor(out=oraw[:, c * CH:(c + 1) * CH], in0=obank[0:KVR, :], scalar=1.0 / PSCALE,
                                         in1=tmp[:, :], op0=ALU.mult, op1=ALU.add).then_inc(o_taken, 1)

            dve.memset(rl[:, :], 0.0).then_inc(l_chain, 1)
            dve.wait_ge(s_tab, 32)
            for c in range(NC):
                rotate(0, c, c, c)
            for u in range(LEAD_S):
                maximum(0, u)
            with dve.Fori(0, NH) as h:
                for u in range(NU):
                    use = NC + USE_T[u]
                    i, n, j0 = TILE_OF[u], width(u) // P, (u - FIRST[TILE_OF[u]]) * TPC
                    hi, lo = (pt[(i // TPC) % 2][part][:, j0:j0 + n, (i % TPC) * P:(i % TPC + 1) * P]
                              for part in range(2))
                    dve.wait_ge(hi_ready, after(h, NU, u + 1))
                    dve.scalar_tensor_tensor(
                        out=lo, in0=tbank[use % 2][:, 0:n * P].rearrange("p (j q) -> p j q", q=P), scalar=PSCALE,
                        in1=hi, op0=ALU.mult, op1=ALU.subtract).then_inc(t_free, 1)
                    if u + LEAD_S < NU:
                        maximum(h, u + LEAD_S)
                    else:
                        if u + LEAD_S == NU:
                            dve.wait_ge(exp_done, after(h, NU, FIRST[12]))
                            dve.tensor_reduce(l[:, 0:12], lsum[:, 0:12, :], AX_X, ALU.add).then_inc(l_chain, 1)
                        maximum(h + 1, u + LEAD_S - NU)
                    if u in QP_AFTER:
                        c = QP_AFTER[u]
                        rotate(h + 1, c, NC + USE_Q[c], after(h, NC, NC + c))
                    if u in O_AFTER:
                        take_outputs(h, O_AFTER[u])
                dve.tensor_reduce(l[:, 12:NT], lsum[:, 12:NT, :], AX_X, ALU.add).then_inc(l_chain, 1)
                dve.wait_ge(l_chain, after(h, 3, 3))
                dve.reciprocal(rl[:, 0:NT], l[:, :]).then_inc(l_chain, 1)
                dve.wait_ge(l_chain, after(h, 3, 4))
                dve.wait_ge(ot_stored, 16)
                dve.transpose(rlT[:, :], rl[:, :]).then_inc(rl_ready, 1)
                take_outputs(h, NC - 1)

        @block.scalar
        def _(act):
            def take_latent(index, c, use):
                act.wait_ge(qp_done, index + 1)
                if not (isinstance(index, int) and index == 0):
                    act.wait_ge(q_ready, index)
                act.activation(y[0:KVR, :], tbank[use % 2][0:KVR, :], ACT.Copy).then_inc(lat_taken, 1)

            def exponentials(h, u):
                i, n = TILE_OF[u], width(u)
                if u == FIRST[i]:
                    act.wait_ge(max_ready, after(h, NT, i + 1))
                k = u - FIRST[i]
                act.activation(prob[:, u % PSLOTS, 0:n], sbank[u % LEAD_S][:, 0:n], ACT.Exp, bias=nm[:, i:i + 1],
                               accum_out=lsum[:, i, k:k + 1]).then_inc(exp_done, 1)

            def low_rows(h, c):
                act.wait_ge(pv_done, after(h, NC, 2 + c + 1))
                act.wait_ge(o_taken, after(h, NC, 1 + c))
                act.activation(tmp[:, :], obank[KVR:P, :], ACT.Copy, scale=1.0 / PSCALE).then_inc(tmp_ready, 1)

            for c in range(NC):
                take_latent(c, c, c)
            for u in range(LEAD_E):
                exponentials(0, u)
            with act.Fori(0, NH) as h:
                for u in range(NU):
                    use = NC + USE_T[u]
                    i, n, j0 = TILE_OF[u], width(u) // P, (u - FIRST[TILE_OF[u]]) * TPC
                    act.wait_ge(turned, after(h, NU, u + 1))
                    if u == FIRST[i] and i % TPC == 0:
                        act.wait_ge(pv_done, after(h, NC, i // TPC + 1))
                    act.activation(pt[(i // TPC) % 2][0][:, j0:j0 + n, (i % TPC) * P:(i % TPC + 1) * P],
                                   tbank[use % 2][:, 0:n * P].rearrange("p (j q) -> p j q", q=P), ACT.Copy,
                                   scale=PSCALE).then_inc(hi_ready, 1)
                    if u in QP_AFTER:
                        c = QP_AFTER[u]
                        take_latent(after(h, NC, NC + c), c, NC + USE_Q[c])
                    if u in O_AFTER:
                        low_rows(h, O_AFTER[u])
                    if u + LEAD_E < NU:
                        exponentials(h, u + LEAD_E)
                    else:
                        exponentials(h + 1, u + LEAD_E - NU)
                low_rows(h, NC - 1)

        @block.gpsimd
        def _(pool):
            def load_weights(h):
                pool.tensor_copy(wh_hi[:, :], wq_hi[:, h, :]).then_inc(pool_chain, 1)
                pool.tensor_copy(wh_lo[:, :], wq_lo[:, h, :]).then_inc(wh_ready, 1)

            def parts(c, use_count, count):
                cols = slice(c * CH, (c + 1) * CH)
                pool.wait_ge(t_free, use_count)
                pool.tensor_tensor(y[KVR:P, :], y[KVR:P, :], w[KVR:P, :], ALU.add).then_inc(pool_chain, 1)
                pool.wait_ge(pool_chain, count + 1)
                pool.tensor_tensor(q_hi[:, cols], y[:, :], zeros[:, :], ALU.add).then_inc(pool_chain, 1)
                pool.wait_ge(pool_chain, count + 2)
                pool.tensor_tensor(q_lo[:, cols], y[:, :], q_hi[:, cols].bitcast(F32), ALU.subtract).then_inc(q_ready, 1)

            chain = 1 + 2 * NC
            pool.memset(zeros[:, :], 0.0).then_inc(pool_chain, 1)
            load_weights(0)
            for c in range(NC):
                parts(c, c + 1, 2 + 2 * c)
            load_weights(1)
            with pool.Fori(0, NH) as h:
                for c in range(NC):
                    parts(c, after(h, USES, NC + USE_Q[c] + 1), after(h, chain, 3 + 2 * NC + 2 * c))
                load_weights(h + 2)
                pool.wait_ge(rb_loaded, after(h, 16, 16))
                for c in range(NC):
                    cols = slice(c * CH, (c + 1) * CH)
                    pool.wait_ge(o_taken, after(h, NC, 1 + c + 1))
                    pool.tensor_tensor(on[:, cols], oraw[:, cols], rb[:, cols], ALU.mult).then_inc(on_ready, 1)

        @block.sync
        def _(sp):
            sp.dma_start(cosr[KVR:P, :], cos_q).then_inc(s_tab, 16)
            sp.dma_start(sinr[KVR:P, :], sin_q).then_inc(s_tab, 16)
            sp.dma_start(rlT[:, :], ident_in[:, 0:32]).then_inc(ot_stored, 16)
            with sp.Fori(0, NH) as h:
                row = sp.snap(h * KVR)
                sp.wait_ge(rl_ready, after(h, 1, 1))
                for a in range(4):
                    sp.dma_start(rl_dram.rearrange("(t p) -> t p", p=P)[:, 32 * a:32 * a + 32],
                                 rlT[32 * a:32 * a + NT, :]).then_inc(rl_stored, 16)
                sp.wait_ge(rl_stored, after(h, 64, 64))
                sp.wait_ge(ot_stored, after(h, 16, 16))
                sp.dma_start(rb[:, :], rl_dram.rearrange("(a s) -> a s", a=1).to_broadcast([KVR, S])).then_inc(rb_loaded, 16)
                sp.wait_ge(on_ready, after(h, NC, 2 * NC))
                sp.dma_start(ot_dram[bass.ds(row, KVR), :], on[:, :]).then_inc(ot_stored, 16)
            sp.wait_ge(ot_stored, 16 * (NH + 1))


def finish(nc, g, alloc):
    with ExitStack() as ctx:
        def sb(name, shape, dt=F32):
            return alloc(ctx, name, shape, dt)

        g["b_hi"] = sb("b_hi", [P, NH // 2, D], F32R)
        g["b_lo"] = sb("b_lo", [P, NH // 2, D], F32R)
        g["gu_hi"] = sb("gu_hi", [P, 2, DF, HIDP], F32R)
        g["gu_lo"] = sb("gu_lo", [P, 2, DF, HIDP], F32R)
        g["dn_hi"] = sb("dn_hi", [P, HT, D], F32R)
        g["dn_lo"] = sb("dn_lo", [P, HT, D], F32R)
        last_weights(nc, g, alloc)
        last_layers(nc, g, alloc)


def last_weights(nc, g, alloc):
    w_v, w_o, ident, kvs = g["w_v"], g["w_o"], g["ident"], g["kvs"]
    b_hi, b_lo, gu_hi, gu_lo, dn_hi, dn_lo = (g[k] for k in ("b_hi", "b_lo", "gu_hi", "gu_lo", "dn_hi", "dn_lo"))
    full = HID // P
    rest = HID - full * P

    with ExitStack() as ctx:
        def sb(name, shape, dt=F32):
            return alloc(ctx, name, shape, dt)

        def sem(name):
            return ctx.enter_context(nc.semaphore(name))

        wv = sb("wv", [KVR, NH, VD])
        wo = sb("wo", [P, NH, D])
        wvT = sb("wvT", [P, NH, KVR])
        wgi = sb("wgi", [P, 2, HT, D], I32)
        wdi = sb("wdi", [P, DF, HID], I32)
        wg = sb("wg", [P, 2, HT, D])
        wd = sb("wd", [P, DF, HIDP])
        sg = sb("sg", [P, 2, HT])
        sdn = sb("sdn", [P, DF])
        banks = [ctx.enter_context(nc.psum_tensor(f"lw{b}", [P, CH], F32)) for b in range(8)]

        jobs = [("vT", k) for k in range(2)] + [("B", k) for k in range(4)]
        jobs += [("gu", a, f, k) for a in range(2) for f in range(DF) for k in range(2)] + [("dn", k) for k in range(3)]
        index = {j: n for n, j in enumerate(jobs)}
        dest = {}
        for k in range(4):
            dest[("B", k)] = [x[:, 2 * k:2 * k + 2, :].rearrange("p a n -> p (a n)") for x in (b_hi, b_lo)]
        for a in range(2):
            for f in range(DF):
                for k, (lo, hi) in enumerate(((0, CH), (CH, HIDP))):
                    dest[("gu", a, f, k)] = [x[:, a, f, lo:hi] for x in (gu_hi, gu_lo)]
        for k in range(3):
            dest[("dn", k)] = [x[:, 2 * k:2 * k + 2, :].rearrange("p a n -> p (a n)") for x in (dn_hi, dn_lo)]

        s_v, s_o, s_i, s_d, s_sg = sem("s_v"), sem("s_o"), sem("s_i"), sem("s_d"), sem("s_sg")
        pe_done = sem("lw_done")
        hi_done = sem("lw_hi")
        taken = sem("lw_taken")
        vt_taken = sem("vt_taken")
        wv_ready = sem("wv_ready")
        w_ready = sem("w_ready")
        zeroed = sem("zeroed")

        block = ctx.enter_context(nc.Block())

        @block.sync
        def _(sp):
            sp.dma_start(wv[:, :, :], w_v.rearrange("r (h n) -> r h n", h=NH)).then_inc(s_v, 16)
            sp.dma_start(wo[:, :, :], w_o.rearrange("(h n) m -> n h m", h=NH)).then_inc(s_o, 16)
            for a, wq in enumerate((g["wq_gate"], g["wq_up"])):
                sp.dma_start(wgi[:, a, 0:full, :], wq[0:full * P, :].rearrange("(m p) d -> p m d", p=P)).then_inc(s_i, 16)
                sp.dma_start(wgi[0:rest, a, full, :], wq[full * P:HID, :]).then_inc(s_i, 16)

        @block.gpsimd
        def _(pool):
            pool.dma_start(wdi[:, :, :], g["wq_down"].rearrange("(f p) n -> p f n", p=P)).then_inc(s_d, 16)
            for f in range(DF):
                pool.dma_start(sdn[:, f:f + 1], g["s_down"][f * P:(f + 1) * P].rearrange("(p a) -> p a", a=1)).then_inc(s_d, 16)
            for a, s in enumerate((g["s_gate"], g["s_up"])):
                for m in range(full):
                    pool.dma_start(sg[:, a, m:m + 1], s[m * P:(m + 1) * P].rearrange("(p a) -> p a", a=1)).then_inc(s_sg, 16)
                pool.dma_start(sg[0:rest, a, full:full + 1], s[full * P:HID].rearrange("(p a) -> p a", a=1)).then_inc(s_sg, 16)

        @block.vector
        def _(dve):
            dve.memset(wg[:, :, full, :], 0.0).then_inc(zeroed, 1)
            dve.memset(wd[:, :, HID:HIDP], 0.0).then_inc(zeroed, 1)
            dve.wait_ge(s_v, 16)
            dve.tensor_scalar(wv[:, :, :], wv[:, :, :], kvs[:, 0:1], None, ALU.mult).then_inc(wv_ready, 1)
            dve.wait_ge(s_i, 64)
            dve.wait_ge(s_sg, 16 * 2 * HT)
            dve.wait_ge(zeroed, 2)
            for a in range(2):
                for m in range(HT):
                    rows = P if m < full else rest
                    dve.tensor_scalar(wg[0:rows, a, m, :], wgi[0:rows, a, m, :], ZERO_POINT, sg[0:rows, a, m:m + 1],
                                      ALU.subtract, ALU.mult).then_inc(w_ready, 1)
            dve.wait_ge(s_d, 48)
            for f in range(DF):
                dve.tensor_scalar(wd[:, f, 0:HID], wdi[:, f, :], ZERO_POINT, sdn[:, f:f + 1],
                                  ALU.subtract, ALU.mult).then_inc(w_ready, 1)
            for n, job in enumerate(jobs):
                if job[0] == "vT":
                    continue
                hi, lo = dest[job]
                dve.wait_ge(hi_done, n - 1)
                dve.tensor_tensor(lo, banks[n % 8][:, 0:hi.shape[-1]], hi.bitcast(F32), ALU.subtract).then_inc(taken, 1)

        @block.scalar
        def _(act):
            for n, job in enumerate(jobs):
                act.wait_ge(pe_done, n + 1)
                if job[0] == "vT":
                    act.activation(wvT[:, 8 * n:8 * n + 8, :].rearrange("p h n -> p (h n)"), banks[n][:, :],
                                   ACT.Copy).then_inc(vt_taken, 1)
                else:
                    hi = dest[job][0]
                    act.activation(hi, banks[n % 8][:, 0:hi.shape[-1]], ACT.Copy).then_inc(hi_done, 1)

        @block.tensor
        def _(pe):
            for n, job in enumerate(jobs):
                b = banks[n % 8]
                if 8 <= n < 10:
                    pe.wait_ge(vt_taken, n - 7)
                elif n >= 10:
                    pe.wait_ge(taken, n - 9)
                if job[0] == "vT":
                    pe.wait_ge(wv_ready, 1)
                    for k in range(8):
                        last = pe.transpose(b[:, k * KVR:(k + 1) * KVR], wv[:, 8 * job[1] + k, :], ident[0:KVR, 0:KVR])
                elif job[0] == "B":
                    pe.wait_ge(vt_taken, 2)
                    pe.wait_ge(s_o, 16)
                    for k in range(4):
                        h = 4 * job[1] + k
                        r = (h % 2) * KVR
                        last = pe.matmul(b[r:r + KVR, (k // 2) * D:(k // 2 + 1) * D], wvT[:, h, :], wo[:, h, :],
                                         start=True, stop=True)
                elif job[0] == "gu":
                    _, a, f, k = job
                    pe.wait_ge(w_ready, HT * (a + 1))
                    for m in range(4 * k, min(4 * k + 4, HT)):
                        last = pe.transpose(b[:, (m - 4 * k) * P:(m - 4 * k + 1) * P], wg[:, a, m, f * P:(f + 1) * P],
                                            ident[:, :])
                else:
                    pe.wait_ge(w_ready, 2 * HT + DF)
                    for k in range(4):
                        m, f = 2 * job[1] + k // 2, k % 2
                        last = pe.transpose(b[:, k * P:(k + 1) * P], wd[:, f, m * P:(m + 1) * P], ident[:, :])
                last.then_inc(pe_done, 1)


def last_layers(nc, g, alloc):
    x, out, ot_dram, ident, eps = g["x"], g["out"], g["ot_dram"], g["ident"], g["eps"]
    GA, SB, CB, GB = g["GA"], g["SB"], g["CB"], g["GB"]
    b_hi, b_lo, gu_hi, gu_lo, dn_hi, dn_lo = (g[k] for k in ("b_hi", "b_lo", "gu_hi", "gu_lo", "dn_hi", "dn_lo"))
    NP = NH // 2

    events = [("X", 0), ("T", 0)]
    for c in range(NC):
        for m in range(HT):
            events.append(("GU", c, m))
            if m == 1 and c:
                events.append(("O", c - 1))
            if m == 2 and c + 1 < NC:
                events.append(("X", c + 1))
            if m == 3 and c + 1 < NC:
                events.append(("T", c + 1))
            if m:
                events.append(("DN", c, m - 1))
        events.append(("DN", c, HT - 1))
    events.append(("O", NC - 1))

    with ExitStack() as ctx:
        def sb(name, shape, dt=F32):
            return alloc(ctx, name, shape, dt)

        def sem(name):
            return ctx.enter_context(nc.semaphore(name))

        xs = sb("x1", [P, NT, D])
        st, mv, sd, rstd = sb("st2", [P, NT, 6]), sb("mv2", [P, NT, 2]), sb("sd2", [P, NT]), sb("rstd2", [P, NT])
        half = ExitStack()
        ot = alloc(half, "ot", [P, 2, NP, CH], F32)
        o_hi = alloc(half, "o_hi", [P, NP, CH], F32R)
        o_lo = alloc(half, "o_lo", [P, NP, CH], F32R)
        yT = alloc(half, "yT", [P, 2, DF, CH], F32)
        banks = [ctx.enter_context(nc.psum_tensor(f"ll{b}", [P, CH], F32)) for b in range(8)]

        s_ot, s_x = [sem(f"s_ot{c}") for c in range(NC)], sem("s_x1")
        hi_done, o_split, pair_used = sem("o_hi_done"), sem("o_split"), sem("pair_used")
        y_ready, y_turned, x1_ready = sem("y_ready"), sem("y_turned"), sem("x1_ready")
        st_ready, mv_ready, sd2_ready = sem("st_ready"), sem("mv_ready"), sem("sd2_ready")
        rstd_ready = sem("rstd_ready")

        with nc.Block() as block:
            @block.sync
            def _(sp):
                src = ot_dram.rearrange("(a p) s -> p a s", p=P)
                for c in range(NC):
                    if c >= 2:
                        sp.wait_ge(o_split, NP * (c - 1))
                    sp.dma_start(ot[:, c % 2, :, :], src[:, :, c * CH:(c + 1) * CH]).then_inc(s_ot[c], 16)

            @block.scalar
            def _(act):
                act.dma_start(xs[:, :, :], x.rearrange("a (t p) d -> p (a t) d", p=P)).then_inc(s_x, 16)
                for c in range(NC):
                    act.wait_ge(pair_used, NP * (c + 1))
                    if c >= 2:
                        act.wait_ge(y_turned, 2 * (c - 1))
                    for f in range(DF):
                        act.activation(yT[:, c % 2, f, :], banks[2 * (c % 2) + f][:, :], ACT.Copy,
                                       scale=GA[:, f:f + 1]).then_inc(y_ready, 1)
                act.wait_ge(mv_ready, NT)
                act.activation(sd[:, :], mv[:, :, 1], ACT.Sqrt, bias=eps[:, 0:1]).then_inc(sd2_ready, 1)

            @block.vector
            def _(dve):
                def residual(c):
                    for f in range(DF):
                        dve.wait_ge(y_turned, 2 * c + f + 1)
                        cols = xs[:, TPC * c:TPC * (c + 1), f * P:(f + 1) * P]
                        dve.tensor_tensor(cols, banks[4 + f][:, :].rearrange("p (t n) -> p t n", n=P), cols,
                                          ALU.add).then_inc(x1_ready, 1)
                    dve.wait_ge(x1_ready, 2 * (c + 1))
                    for t in range(TPC * c, TPC * (c + 1)):
                        dve.bn_stats(st[:, t, :], xs[:, t, :]).then_inc(st_ready, 1)
                    dve.wait_ge(st_ready, TPC * (c + 1))
                    for t in range(TPC * c, TPC * (c + 1)):
                        dve.bn_aggr(mv[:, t, :], st[:, t, :]).then_inc(mv_ready, 1)

                for c in range(NC):
                    dve.wait_ge(s_ot[c], 16)
                    for a in range(NP):
                        if c:
                            dve.wait_ge(pair_used, NP * (c - 1) + a + 1)
                        dve.tensor_copy(o_hi[:, a, :], ot[:, c % 2, a, :]).then_inc(hi_done, 1)
                        dve.wait_ge(hi_done, NP * c + a + 1)
                        dve.tensor_tensor(o_lo[:, a, :], ot[:, c % 2, a, :], o_hi[:, a, :].bitcast(F32),
                                          ALU.subtract).then_inc(o_split, 1)
                    if c == 0:
                        dve.wait_ge(s_x, 16)
                    else:
                        residual(c - 1)
                residual(NC - 1)
                dve.wait_ge(sd2_ready, 1)
                dve.reciprocal(rstd[:, :], sd[:, :]).then_inc(rstd_ready, 1)

            @block.tensor
            def _(pe):
                def turn(c):
                    for f in range(DF):
                        pe.wait_ge(y_ready, 2 * c + f + 1)
                        if c:
                            pe.wait_ge(x1_ready, 2 * (c - 1) + f + 1)
                        for k in range(TPC):
                            last = pe.transpose(banks[4 + f][:, k * P:(k + 1) * P],
                                                yT[:, c % 2, f, k * P:(k + 1) * P], ident[:, :])
                        last.then_inc(y_turned, 1)

                for c in range(NC):
                    if c >= 2:
                        pe.wait_ge(y_ready, 2 * (c - 1))
                    for a in range(NP):
                        pe.wait_ge(o_split, NP * c + a + 1)
                        for q, (w, o) in enumerate(((b_hi, o_hi), (b_hi, o_lo), (b_lo, o_hi))):
                            for f in range(DF):
                                last = pe.matmul(banks[2 * (c % 2) + f][:, :], w[:, a, f * P:(f + 1) * P], o[:, a, :],
                                                 start=(a == 0 and q == 0), stop=(a == NP - 1 and q == 2))
                        last.then_inc(pair_used, 1)
                    if c:
                        turn(c - 1)
                turn(NC - 1)
        half.close()

        xn = sb("xn2", [P, TPC, D])
        h32 = sb("h2", [P, DF, CH])
        h_hi, h_lo = sb("h2_hi", [P, 2, DF, CH], F32R), sb("h2_lo", [P, 2, DF, CH], F32R)
        sl = sb("sl", [P, 2, CH])
        a32 = sb("a32", [P, 2, CH])
        a_hi, a_lo = sb("a_hi", [P, 2, CH], F32R), sb("a_lo", [P, 2, CH], F32R)
        fT = sb("fT", [P, DF, CH])
        res = sb("res", [P, 2, TPC, D])

        xn_ready, t_done, t_taken, h_hi_done, h_split = (sem(n) for n in ("x2n", "x2t", "x2taken", "h2hi", "h2split"))
        gu_done, silu_done, prod_done, a_hi_done, a_split = (sem(n) for n in ("gud", "silud", "prodd", "ahid", "asplit"))
        dn_done, f_taken, o_turned, o_added = (sem(n) for n in ("dnd", "ftaken", "oturned", "oadded"))
        stored = [sem(f"stored{c}") for c in range(NC)]

        with nc.Block() as block:
            @block.sync
            def _(sp):
                for c in range(NC):
                    sp.wait_ge(o_added, 2 * (c + 1))
                    sp.dma_start(out[0, c * CH:(c + 1) * CH, :].rearrange("(t p) d -> p t d", p=P),
                                 res[:, c % 2, :, :]).then_inc(stored[c], 16)
                for c in range(NC):
                    sp.wait_ge(stored[c], 16)

            @block.vector
            def _(dve):
                for e in events:
                    kind, c = e[0], e[1]
                    if kind == "X":
                        if c:
                            dve.wait_ge(t_done, 2 * c)
                        for k in range(TPC):
                            t = TPC * c + k
                            dve.tensor_scalar(xn[:, k, :], xs[:, t, :], mv[:, t, 0:1], rstd[:, t:t + 1],
                                              ALU.subtract, ALU.mult).then_inc(xn_ready, 1)
                    elif kind == "T":
                        if c >= 2:
                            dve.wait_ge(gu_done, HT * (c - 1))
                        for f in range(DF):
                            dve.wait_ge(t_taken, 2 * c + f + 1)
                            dve.tensor_copy(h_hi[:, c % 2, f, :], h32[:, f, :]).then_inc(h_hi_done, 1)
                            dve.wait_ge(h_hi_done, 2 * c + f + 1)
                            dve.tensor_tensor(h_lo[:, c % 2, f, :], h32[:, f, :], h_hi[:, c % 2, f, :].bitcast(F32),
                                              ALU.subtract).then_inc(h_split, 1)
                    elif kind == "GU":
                        n = HT * c + e[2]
                        dve.wait_ge(silu_done, n + 1)
                        if n >= 2:
                            dve.wait_ge(a_split, n - 1)
                        dve.tensor_tensor(a32[:, n % 2, :], banks[2 * (n % 2) + 1][:, :], sl[:, n % 2, :],
                                          ALU.mult).then_inc(prod_done, 1)
                        if n >= 2:
                            dve.wait_ge(dn_done, n - 1)
                        dve.wait_ge(prod_done, n + 1)
                        dve.tensor_copy(a_hi[:, n % 2, :], a32[:, n % 2, :]).then_inc(a_hi_done, 1)
                        dve.wait_ge(a_hi_done, n + 1)
                        dve.tensor_tensor(a_lo[:, n % 2, :], a32[:, n % 2, :], a_hi[:, n % 2, :].bitcast(F32),
                                          ALU.subtract).then_inc(a_split, 1)
                    elif kind == "O":
                        if c >= 2:
                            dve.wait_ge(stored[c - 2], 16)
                        for f in range(DF):
                            dve.wait_ge(o_turned, 2 * c + f + 1)
                            cols = slice(f * P, (f + 1) * P)
                            dve.tensor_tensor(res[:, c % 2, :, cols],
                                              banks[4 + f][:, :].rearrange("p (t n) -> p t n", n=P),
                                              xs[:, TPC * c:TPC * (c + 1), cols], ALU.add).then_inc(o_added, 1)

            @block.scalar
            def _(act):
                for e in events:
                    kind, c = e[0], e[1]
                    if kind == "T":
                        for f in range(DF):
                            act.wait_ge(t_done, 2 * c + f + 1)
                            if c:
                                act.wait_ge(h_split, 2 * (c - 1) + f + 1)
                            act.activation(h32[:, f, :], banks[4 + f][:, :], ACT.Identity, bias=SB[:, f:f + 1],
                                           scale=CB[:, f:f + 1]).then_inc(t_taken, 1)
                    elif kind == "GU":
                        n = HT * c + e[2]
                        act.wait_ge(gu_done, n + 1)
                        if n >= 2:
                            act.wait_ge(prod_done, n - 1)
                        act.activation(sl[:, n % 2, :], banks[2 * (n % 2)][:, :], ACT.Silu).then_inc(silu_done, 1)
                    elif kind == "DN" and e[2] == HT - 1:
                        act.wait_ge(dn_done, HT * (c + 1))
                        if c:
                            act.wait_ge(o_turned, 2 * c)
                        for f in range(DF):
                            act.activation(fT[:, f, :], banks[6 + f][:, :], ACT.Copy, scale=GB[:, f:f + 1]).then_inc(f_taken, 1)

            @block.tensor
            def _(pe):
                for at, e in enumerate(events):
                    kind, c = e[0], e[1]
                    if kind == "T":
                        pe.wait_ge(xn_ready, TPC * (c + 1))
                        if c >= 2:
                            pe.wait_ge(o_added, 2 * (c - 1))
                        elif c == 1:
                            pe.wait_ge(t_taken, 2)
                        for f in range(DF):
                            for k in range(TPC):
                                last = pe.transpose(banks[4 + f][:, k * P:(k + 1) * P], xn[:, k, f * P:(f + 1) * P],
                                                    ident[:, :])
                            last.then_inc(t_done, 1)
                    elif kind == "O":
                        pe.wait_ge(f_taken, 2 * (c + 1))
                        pe.wait_ge(t_taken, 2 * min(c + 2, NC))
                        for f in range(DF):
                            if c == NC - 1:
                                pe.wait_ge(o_added, 2 * c)
                            for k in range(TPC):
                                last = pe.transpose(banks[4 + f][:, k * P:(k + 1) * P], fT[:, f, k * P:(k + 1) * P],
                                                    ident[:, :])
                            last.then_inc(o_turned, 1)
                    elif kind == "GU":
                        n = HT * c + e[2]
                        if e[2] == 0:
                            pe.wait_ge(h_split, 2 * (c + 1))
                        if n >= 2:
                            pe.wait_ge(prod_done, n - 1)
                        cols = slice(e[2] * P, (e[2] + 1) * P)
                        for a in range(2):
                            passes = [(w, h, f) for f in range(DF)
                                      for w, h in ((gu_hi, h_hi), (gu_hi, h_lo), (gu_lo, h_hi))]
                            for q, (w, h, f) in enumerate(passes):
                                last = pe.matmul(banks[2 * (n % 2) + a][:, :], w[:, a, f, cols], h[:, c % 2, f, :],
                                                 start=(q == 0), stop=(q == len(passes) - 1))
                        last.then_inc(gu_done, 1)
                    elif kind == "DN":
                        n = HT * c + e[2]
                        pe.wait_ge(a_split, n + 1)
                        if e[2] == 0 and c:
                            pe.wait_ge(f_taken, 2 * c)
                        for f in range(DF):
                            cols = slice(f * P, (f + 1) * P)
                            for q, (w, a) in enumerate(((dn_hi, a_hi), (dn_hi, a_lo), (dn_lo, a_hi))):
                                last = pe.matmul(banks[6 + f][:, :], w[:, e[2], cols], a[:, n % 2, :],
                                                 start=(e[2] == 0 and q == 0), stop=(e[2] == HT - 1 and q == 2))
                        last.then_inc(dn_done, 1)


_INS = ["L0_attn_x", "L0_attn_W_cq", "L0_attn_q_scale", "L0_attn_W_dq_nope", "L0_attn_W_dq_rope", "L0_attn_W_ckv",
        "L0_attn_kv_scale", "L0_attn_W_dk_nope", "L0_attn_W_dv", "L0_attn_W_krope", "L0_attn_W_o",
        "L0_ffn_wq_gate", "L0_ffn_s_gate", "L0_ffn_wq_up", "L0_ffn_s_up", "L0_ffn_wq_down", "L0_ffn_s_down",
        "L0_c", "L0_wmod"]


def shape_constants():
    f = np.float32
    inv = (f(1.0) / np.power(f(10000.0), np.arange(HALF, dtype=f) * f(2.0) / f(ROPE))).astype(f)
    ang = np.arange(S, dtype=f)[:, None] * inv[None, :]
    cos, sin = np.cos(ang).astype(f), np.sin(ang).astype(f)
    return {
        "ident": np.eye(P, dtype=f),
        "mask": np.where(np.arange(P)[None, :] > np.arange(P)[:, None], f(MASKED), f(0)).astype(f),
        "cos_q": np.ascontiguousarray(np.concatenate([cos.T, cos.T])),
        "sin_q": np.ascontiguousarray(np.concatenate([sin.T, -sin.T])),
        "cos_k": cos / f(NH),
        "sin_k": sin / f(NH),
    }


def kernel(**inputs):
    import concourse.bacc as _bacc
    from concourse.bass_utils import run_bass_kernel_spmd as _run

    nc = _bacc.Bacc("TRN2", target_bir_lowering=False, num_devices=1)
    arrays, args = {}, []
    given = {n: np.ascontiguousarray(inputs[n]) for n in _INS} | shape_constants()
    for name, a in given.items():
        arrays[f"in_{name}_dram"] = a
        args.append(nc.dram_tensor(f"in_{name}_dram", a.shape, mybir.dt.from_np(a.dtype), kind="ExternalInput").ap())
    out = nc.dram_tensor("out_dram", (1, S, D), F32, kind="ExternalOutput").ap()
    adaln_block(nc, *args, out)
    r = _run(nc, [arrays], core_ids=[0])
    return r.results[0]["out_dram"]
```

```python
from contextlib import ExitStack

import numpy as np

import concourse.bass as bass
from concourse import mybir

F32 = mybir.dt.float32
F32R = mybir.dt.float32r
BF16 = mybir.dt.bfloat16
F16 = mybir.dt.float16
I32 = mybir.dt.int32
ALU = mybir.AluOpType
ACT = mybir.ActivationFunctionType
AX_X = mybir.AxisListType.X

P = 128
S = 2048
D = 256
DF = D // P
NH = 16
NOPE, ROPE, VD = 128, 64, 128
QR, KVR = 128, 64
HALF = ROPE // 2
HID, HIDP = 704, 768
HT = HIDP // P
ZERO_POINT = 128.0
NT = S // P
CH = 512
NC = S // CH
TPC = CH // P
RMS_EPS, LN_EPS = 1e-6, 1e-5
SCORE_SCALE = float((NOPE + ROPE) ** -0.5)
MASKED = -1e30
PSCALE = 1024.0

UNITS = [(i * P + P + CH - 1) // CH for i in range(NT)]
FIRST = [sum(UNITS[:i]) for i in range(NT)]
NU = sum(UNITS)
TILE_OF = [i for i in range(NT) for _ in range(UNITS[i])]
SBANKS = 5
WBANKS = 3
LEAD_S = 6
LEAD_E = 3
assert NU % SBANKS == 0

START = 6
QP_AFTER = {11: 0, 25: 1, 33: 2, 41: 3}
PV_BEFORE = {7: 0, 20: 1, 31: 2, 42: 3}
SUMS_EARLY, SUMS_LATE = NU - LEAD_S, NU


def width(v):
    i = TILE_OF[v % NU]
    return min(CH, (i + 1) * P - (v % NU - FIRST[i]) * CH)


def chunk_of(v):
    return TILE_OF[v % NU] // TPC + NC * (v // NU)


def starts_chunk(v):
    return TILE_OF[v % NU] % TPC == 0 and v % NU == FIRST[TILE_OF[v % NU]]


def multi_before(v):
    return sum(1 for j in range(v + 1) if UNITS[TILE_OF[j % NU]] > 1)


MULTI = multi_before(NU - 1)


def bank_order():
    uses = [("q", c - NC) for c in range(NC)]
    for v in range(START + NU):
        if v >= START and v in PV_BEFORE:
            uses.append(("o", PV_BEFORE[v]))
        uses.append(("t", v))
        if v >= START and v in QP_AFTER:
            uses.append(("q", QP_AFTER[v]))
    return uses


USES = bank_order()
BANK = {use: n % WBANKS for n, use in enumerate(USES)}
BEFORE = {use: USES[n - WBANKS] for n, use in enumerate(USES) if n >= WBANKS}
assert (NU + 2 * NC) % WBANKS == 0
assert all(USES[-k] == ("t", START + NU - k) for k in range(1, WBANKS + 1))


def adaln_block(nc, x, w_cq, q_scale, w_qn, w_qr, w_ckv, kv_scale, w_kn, w_v, w_kr, w_o,
                wq_gate, s_gate, wq_up, s_up, wq_down, s_down, cond, w_mod,
                ident_in, mask_in, cos_q, sin_q, cos_k, sin_k, out):
    rl_dram = nc.dram_tensor("rl_scratch", [S], F32).ap()
    ot_dram = nc.dram_tensor("ot_scratch", [NH * KVR, S], F32).ap()

    with ExitStack() as whole:
        def alloc(ctx, name, shape, dt):
            return ctx.enter_context(nc.sbuf_tensor(name, shape, dt))

        def sem(name, ctx=whole):
            return ctx.enter_context(nc.semaphore(name))

        ident = alloc(whole, "ident", [P, P], F32)
        identb = alloc(whole, "identb", [P, P], BF16)
        maskb = alloc(whole, "maskb", [P, P], BF16)
        mod = alloc(whole, "mod", [P, 12], F32)
        eps = alloc(whole, "eps", [P, 2], F32)
        kvs = alloc(whole, "kvs", [KVR, 1], F32)
        SA, CA, GA, SB, CB, GB = (mod[:, 2 * k:2 * k + 2] for k in range(6))

        pv_done = sem("pv_done")
        o_taken = sem("o_taken")
        on_ready = sem("on_ready")

        att = ExitStack()
        k_hi = alloc(att, "k_hi", [P, S], F32R)
        k_lo = alloc(att, "k_lo", [P, S], F32R)
        nq_hi = alloc(att, "nq_hi", [P, S], F32R)
        nq_lo = alloc(att, "nq_lo", [P, S], F32R)
        vals = alloc(att, "vals", [P, NT, 2 * KVR], F16)
        wq_hi = alloc(att, "wq_hi", [P, NH + 2, P], F32R)
        wq_lo = alloc(att, "wq_lo", [P, NH + 2, P], F32R)
        lsum = alloc(att, "lsum", [P, NT, 4], F32)

        g = dict(locals())
        prepare(nc, g, alloc)
        attend(nc, g, alloc)
        att.close()
        finish(nc, g, alloc)


def prepare(nc, g, alloc):
    (x, w_cq, q_scale, w_qn, w_qr, w_ckv, kv_scale, w_kn, w_kr, cond, w_mod, ident_in, mask_in, cos_k, sin_k) = (
        g[k] for k in ("x", "w_cq", "q_scale", "w_qn", "w_qr", "w_ckv", "kv_scale", "w_kn", "w_kr", "cond",
                       "w_mod", "ident_in", "mask_in", "cos_k", "sin_k"))
    ident, identb, maskb, mod, eps, kvs = (g[k] for k in ("ident", "identb", "maskb", "mod", "eps", "kvs"))
    SA, CA = g["SA"], g["CA"]
    k_hi, k_lo, nq_hi, nq_lo, vals = (g[k] for k in ("k_hi", "k_lo", "nq_hi", "nq_lo", "vals"))
    wq_hi, wq_lo, lsum = g["wq_hi"], g["wq_lo"], g["lsum"]

    with ExitStack() as ctx:
        def sb(name, shape, dt=F32):
            return alloc(ctx, name, shape, dt)

        def sem(name):
            return ctx.enter_context(nc.semaphore(name))

        xs = sb("xs", [P, NT, D])
        xn = sb("xn", [P, NT, D])
        st = sb("st", [P, NT, 6])
        mv = sb("mv", [P, NT, 2])
        sd = sb("sd", [P, NT])
        rstd = sb("rstd", [P, NT])
        h32 = sb("h32", [P, 2, DF, CH])
        h_hi = sb("h_hi", [P, 2, DF, CH], F32R)
        h_lo = sb("h_lo", [P, 2, DF, CH], F32R)
        wx = sb("wx", [P, DF, D])
        wkr = sb("wkr", [P, DF, ROPE])
        wx_hi = sb("wx_hi", [P, DF, D], F32R)
        wx_lo = sb("wx_lo", [P, DF, D], F32R)
        z = sb("z", [P, NT, D])
        ss = sb("ss", [P, 2, NT])
        sdz = sb("sdz", [P, 2, NT])
        rz = sb("rz", [P, 2, NT])
        sq, nqn = xs[:, :, 0:P], xs[:, :, P:D]
        kk = sb("kk", [P, NT, P])
        ck = sb("ck", [P, NT, HALF])
        sk = sb("sk", [P, NT, HALF])
        r1 = sb("r1", [P, 4, NT, HALF])
        wqn = sb("wqn", [P, NH, NOPE])
        wqr = sb("wqr", [P, NH, HALF, 2])
        wkn = sb("wkn", [KVR, NH, NOPE])
        wqT = sb("wqT", [P, NH, QR])
        wkT = sb("wkT", [P, NH, KVR])
        wqa = sb("wqa", [P, NH, P])
        qs = sb("qs", [P, 1])
        cs = sb("cs", [P, 2])
        wm = sb("wm", [P, 2, 6 * D])
        sc = sb("sc", [P, 2])
        mk32 = sb("mk32", [P, P])
        gt = sb("gt", [P, 2, 4])
        banks = [ctx.enter_context(nc.psum_tensor(f"prep{b}", [P, CH], F32)) for b in range(8)]

        jobs = [("wqT", k) for k in range(4)] + [("wkT", k) for k in range(2)]
        jobs += [("mod", 0)]
        for c in range(NC):
            jobs += [("xT", c, f) for f in range(DF)]
            if c == 0:
                jobs += [("A", k) for k in range(2)]
            if c:
                jobs += [("z", c - 1, k) for k in range(2)]
        jobs += [("z", NC - 1, k) for k in range(2)]
        for c in range(NC):
            jobs += [("nT", c), ("kT", c)]
        index = {j: n for n, j in enumerate(jobs)}

        pe_done = sem("pe_done")
        freed = [sem(f"freed{b}") for b in range(8)]
        dve_chain, act_chain = sem("dve_chain"), sem("act_chain")
        s_small, s_wqk, s_wx, s_wm, s_tab = sem("s_small"), sem("s_wqk"), sem("s_wx"), sem("s_wm"), sem("s_tab")
        s_x = [sem(f"s_x{c}") for c in range(NC)]
        consts_ready = sem("consts_ready")
        wkn_ready = sem("wkn_ready")
        var_ready = sem("var_ready")
        sd_ready = sem("sd_ready")
        xn_ready = sem("xn_ready")
        silu_ready = sem("silu_ready")
        mod_ready = sem("mod_ready")
        wx_ready = sem("wx_ready")
        h_split = sem("h_split")
        ss_ready = sem("ss_ready")
        sdz_ready = sem("sdz_ready")
        nk_ready = sem("nk_ready")
        hi_ready = sem("hi_ready")

        def bank(job):
            return banks[index[job] % 8]

        def job_done(eng, job):
            eng.wait_ge(pe_done, index[job] + 1)

        def taken(eng, job):
            eng.wait_ge(freed[index[job] % 8], index[job] // 8 + 1)

        class Order:

            def __init__(self, eng, chain):
                self.eng, self.chain, self.count, self.last = eng, chain, {}, None

            def did(self, ins, signal=None):
                s = signal if signal is not None else self.chain
                self.count[id(s)] = self.count.get(id(s), 0) + 1
                ins.then_inc(s, 1)
                self.last = (s, self.count[id(s)])

            def own(self):
                self.eng.wait_ge(*self.last)

        def free(ins, job):
            ins.then_inc(freed[index[job] % 8], 1)

        block = ctx.enter_context(nc.Block())

        @block.sync
        def _(sp):
            sp.dma_start(ident[:, :], ident_in).then_inc(s_small, 16)
            sp.dma_start(mk32[:, :], mask_in).then_inc(s_small, 16)
            sp.dma_start(qs[:, :], q_scale.rearrange("(p a) -> p a", a=1)).then_inc(s_small, 16)
            sp.dma_start(kvs[:, :], kv_scale.rearrange("(p a) -> p a", a=1)).then_inc(s_small, 16)
            for k in range(2):
                sp.dma_start(cs[:, k:k + 1], cond[0, k * P:(k + 1) * P].rearrange("(p a) -> p a", a=1)).then_inc(s_small, 16)
            xv = x.rearrange("a (t p) d -> p (a t) d", p=P)
            for c in range(NC):
                sp.dma_start(xs[:, c * TPC:(c + 1) * TPC, :], xv[:, c * TPC:(c + 1) * TPC, :]).then_inc(s_x[c], 16)
            sp.dma_start(wm[:, :, :], w_mod.rearrange("(k p) n -> p k n", p=P)).then_inc(s_wm, 16)

        @block.gpsimd
        def _(pool):
            pool.dma_start(wkn[:, :, :], w_kn.rearrange("r (h n) -> r h n", h=NH)).then_inc(s_wqk, 16)
            pool.dma_start(wqn[:, :, :], w_qn.rearrange("r (h n) -> r h n", h=NH)).then_inc(s_wqk, 16)
            pool.dma_start(wqr[:, :, :, :], w_qr.rearrange("r (h i e) -> r h i e", h=NH, e=2)).then_inc(s_wqk, 16)
            pool.dma_start(wx[:, :, 0:QR], w_cq.rearrange("(k p) n -> p k n", p=P)).then_inc(s_wx, 16)
            pool.dma_start(wx[:, :, QR:QR + KVR], w_ckv.rearrange("(k p) n -> p k n", p=P)).then_inc(s_wx, 16)
            pool.dma_start(wkr[:, :, :], w_kr.rearrange("(k p) n -> p k n", p=P)).then_inc(s_wx, 16)
            pool.dma_start(ck[:, :, :], cos_k.rearrange("(t p) i -> p t i", p=P)).then_inc(s_tab, 16)
            pool.dma_start(sk[:, :, :], sin_k.rearrange("(t p) i -> p t i", p=P)).then_inc(s_tab, 16)

        @block.vector
        def _(dve):
            o = Order(dve, dve_chain)
            did, own = o.did, o.own
            dve.memset(eps[:, 0:1], LN_EPS).then_inc(g["pv_done"], 2)
            dve.memset(eps[:, 1:2], RMS_EPS).then_inc(g["o_taken"], 1)
            dve.memset(lsum[:, :, :], 0.0).then_inc(g["on_ready"], NC)
            did(dve.memset(wq_hi[:, NH:NH + 2, :].bitcast(mybir.dt.uint32), 0))
            did(dve.memset(wq_lo[:, NH:NH + 2, :].bitcast(mybir.dt.uint32), 0))
            dve.wait_ge(s_small, 16 * 6)
            did(dve.tensor_copy(identb[:, :], ident[:, :]))
            did(dve.tensor_copy(maskb[:, :], mk32[:, :]), consts_ready)
            did(dve.tensor_scalar(qs[:, :], qs[:, :], SCORE_SCALE, None, ALU.mult))
            dve.wait_ge(s_wqk, 48)
            did(dve.tensor_scalar(wkn[:, :, :], wkn[:, :, :], kvs[:, 0:1], None, ALU.mult), wkn_ready)
            for c in range(NC):
                dve.wait_ge(s_x[c], 16)
                for t in range(c * TPC, (c + 1) * TPC):
                    did(dve.bn_stats(st[:, t, :], xs[:, t, :]))
            own()
            for t in range(NT):
                did(dve.bn_aggr(mv[:, t, :], st[:, t, :]), var_ready)
            dve.wait_ge(s_wx, 48)
            did(dve.tensor_copy(wx[:, :, QR + KVR:QR + KVR + HALF], wkr[:, :, 0::2]))
            did(dve.tensor_copy(wx[:, :, QR + KVR + HALF:D], wkr[:, :, 1::2]))
            own()
            did(dve.tensor_copy(wx_hi[:, :, :], wx[:, :, :]))
            own()
            did(dve.tensor_tensor(wx_lo[:, :, :], wx[:, :, :], wx_hi[:, :, :].bitcast(F32), ALU.subtract), wx_ready)
            dve.wait_ge(sd_ready, 1)
            did(dve.reciprocal(rstd[:, :], sd[:, :]))
            own()
            for t in range(NT):
                did(dve.tensor_scalar(xn[:, t, :], xs[:, t, :], mv[:, t, 0:1], rstd[:, t:t + 1],
                                      ALU.subtract, ALU.mult), xn_ready if t % TPC == TPC - 1 else None)
            job_done(dve, ("mod", 0))
            free(dve.tensor_copy(mod[:, :], bank(("mod", 0))[:, 0:12]), ("mod", 0))
            taken(dve, ("mod", 0))
            gates = mod[:, :].rearrange("p (s k f) -> p s k f", s=2, k=3)[:, :, 2, :]
            sign, size = gt[:, :, 0:2], gt[:, :, 2:4]
            did(dve.tensor_scalar(sign, gates, 0.0, 2.0, ALU.is_ge, ALU.mult))
            did(dve.tensor_scalar(size, gates, -1.0, None, ALU.mult))
            own()
            did(dve.tensor_scalar(sign, sign, -1.0, None, ALU.add))
            did(dve.tensor_tensor(size, gates, size, ALU.max))
            own()
            did(dve.tensor_scalar(size, size, 0.25, None, ALU.max))
            for base in (2, 8):
                did(dve.tensor_scalar(mod[:, base:base + 2], mod[:, base:base + 2], 1.0, None, ALU.add))
            own()
            did(dve.tensor_tensor(gates, sign, size, ALU.mult), mod_ready)

            for c in range(NC):
                if c >= 2:
                    job_done(dve, ("z", c - 2, 1))
                for f in range(DF):
                    taken(dve, ("xT", c, f))
                    did(dve.tensor_copy(h_hi[:, c % 2, f, :], h32[:, c % 2, f, :]))
                    own()
                    did(dve.tensor_tensor(h_lo[:, c % 2, f, :], h32[:, c % 2, f, :],
                                          h_hi[:, c % 2, f, :].bitcast(F32), ALU.subtract), h_split)
                if c == 0:
                    for k in range(2):
                        job_done(dve, ("A", k))
                        free(dve.tensor_scalar(wqa[:, 8 * k:8 * k + 8, 0:KVR],
                                               bank(("A", k))[:, :].rearrange("p (h j) -> p h j", h=8),
                                               qs[:, 0:1], None, ALU.mult), ("A", k))
                    for e in range(2):
                        did(dve.tensor_scalar(wqa[:, :, KVR + HALF * e:KVR + HALF * e + HALF], wqr[:, :, :, e],
                                              qs[:, 0:1], None, ALU.mult))
                    for k in range(2):
                        taken(dve, ("A", k))
                    own()
                    did(dve.tensor_copy(wq_hi[:, 0:NH, :], wqa[:, :, :]))
                    own()
                    did(dve.tensor_tensor(wq_lo[:, 0:NH, :], wqa[:, :, :], wq_hi[:, 0:NH, :].bitcast(F32),
                                          ALU.subtract))

            for c in range(NC):
                for k in range(2):
                    taken(dve, ("z", c, k))
            did(dve.tensor_tensor(sq[:, :, :], z[:, :, 0:QR], z[:, :, 0:QR], ALU.mult))
            own()
            did(dve.tensor_reduce(ss[:, 0, :], sq[:, :, :], AX_X, ALU.add))
            own()
            did(dve.tensor_tensor(sq[:, :, 0:KVR], z[:, :, QR:QR + KVR], z[:, :, QR:QR + KVR], ALU.mult))
            own()
            did(dve.tensor_reduce(ss[:, 1, :], sq[:, :, 0:KVR], AX_X, ALU.add))
            own()
            did(dve.tensor_scalar(ss[:, 0, :], ss[:, 0, :], 1.0 / QR, None, ALU.mult))
            did(dve.tensor_scalar(ss[:, 1, :], ss[:, 1, :], 1.0 / KVR, None, ALU.mult), ss_ready)
            dve.wait_ge(s_tab, 32)
            even, odd = z[:, :, QR + KVR:QR + KVR + HALF], z[:, :, QR + KVR + HALF:D]
            for k, (a, b) in enumerate(((even, ck), (odd, sk), (even, sk), (odd, ck))):
                did(dve.tensor_tensor(r1[:, k, :, :], a, b[:, :, :], ALU.mult))
            own()
            did(dve.tensor_tensor(kk[:, :, KVR:KVR + HALF], r1[:, 0, :, :], r1[:, 1, :, :], ALU.subtract))
            did(dve.tensor_tensor(kk[:, :, KVR + HALF:P], r1[:, 2, :, :], r1[:, 3, :, :], ALU.add))
            dve.wait_ge(sdz_ready, 1)
            did(dve.reciprocal(rz[:, :, :], sdz[:, :, :]))
            own()
            for t in range(NT):
                did(dve.tensor_scalar(nqn[:, t, :], z[:, t, 0:QR], rz[:, 0, t:t + 1], None, ALU.mult))
                did(dve.tensor_scalar(kk[:, t, 0:KVR], z[:, t, QR:QR + KVR], rz[:, 1, t:t + 1], None, ALU.mult),
                    nk_ready if t % TPC == TPC - 1 else None)
            own()
            did(dve.tensor_copy(vals[:, :, 0:KVR], kk[:, :, 0:KVR]))
            own()
            did(dve.tensor_tensor(vals[:, :, KVR:2 * KVR], kk[:, :, 0:KVR], vals[:, :, 0:KVR], ALU.subtract))
            for c in range(NC):
                for k, (kind, hi, lo) in enumerate((("nT", nq_hi, nq_lo), ("kT", k_hi, k_lo))):
                    cols = slice(c * CH, (c + 1) * CH)
                    dve.wait_ge(hi_ready, 2 * c + k + 1)
                    free(dve.tensor_tensor(lo[:, cols], bank((kind, c))[:, :], hi[:, cols].bitcast(F32),
                                           ALU.subtract), (kind, c))

        @block.scalar
        def _(act):
            act.wait_ge(s_small, 16 * 6)
            act.activation(sc[:, :], cs[:, :], ACT.Silu).then_inc(silu_ready, 1)
            for k in range(4):
                job_done(act, ("wqT", k))
                free(act.activation(wqT[:, 4 * k:4 * k + 4, :].rearrange("p h n -> p (h n)"),
                                    bank(("wqT", k))[:, :], ACT.Copy), ("wqT", k))
            for k in range(2):
                job_done(act, ("wkT", k))
                free(act.activation(wkT[:, 8 * k:8 * k + 8, :].rearrange("p h n -> p (h n)"),
                                    bank(("wkT", k))[:, :], ACT.Copy), ("wkT", k))
            act.wait_ge(var_ready, NT)
            act.activation(sd[:, :], mv[:, :, 1], ACT.Sqrt, bias=eps[:, 0:1]).then_inc(sd_ready, 1)
            act.wait_ge(mod_ready, 1)

            def take_z(c):
                for k in range(2):
                    job_done(act, ("z", c, k))
                    t = c * TPC + 2 * k
                    free(act.activation(z[:, t:t + 2, :].rearrange("p t n -> p (t n)"), bank(("z", c, k))[:, :],
                                        ACT.Copy), ("z", c, k))

            for c in range(NC):
                for f in range(DF):
                    job_done(act, ("xT", c, f))
                    if c >= 2:
                        act.wait_ge(h_split, 2 * (c - 2) + f + 1)
                    free(act.activation(h32[:, c % 2, f, :], bank(("xT", c, f))[:, :], ACT.Identity,
                                        bias=SA[:, f:f + 1], scale=CA[:, f:f + 1]), ("xT", c, f))
                if c:
                    take_z(c - 1)
            take_z(NC - 1)
            act.wait_ge(ss_ready, 1)
            act.activation(sdz[:, :, :].rearrange("p a t -> p (a t)"), ss[:, :, :].rearrange("p a t -> p (a t)"),
                           ACT.Sqrt, bias=eps[:, 1:2]).then_inc(sdz_ready, 1)
            for c in range(NC):
                for kind, hi in (("nT", nq_hi), ("kT", k_hi)):
                    job_done(act, (kind, c))
                    act.activation(hi[:, c * CH:(c + 1) * CH], bank((kind, c))[:, :], ACT.Copy).then_inc(hi_ready, 1)

        @block.tensor
        def _(pe):
            pe.wait_ge(s_small, 16 * 6)
            for n, job in enumerate(jobs):
                kind, b = job[0], bank(job)
                if n >= 8:
                    pe.wait_ge(freed[n % 8], n // 8)
                if kind == "wqT":
                    pe.wait_ge(s_wqk, 48)
                    for k in range(4):
                        last = pe.transpose(b[:, k * P:(k + 1) * P], wqn[:, 4 * job[1] + k, :], ident[:, :])
                elif kind == "wkT":
                    pe.wait_ge(wkn_ready, 1)
                    for k in range(8):
                        last = pe.transpose(b[:, k * KVR:(k + 1) * KVR], wkn[:, 8 * job[1] + k, :], ident[0:KVR, 0:KVR])
                elif kind == "mod":
                    pe.wait_ge(s_wm, 16)
                    pe.wait_ge(silu_ready, 1)
                    for m in range(12):
                        for k in range(2):
                            last = pe.matmul(b[:, m:m + 1], wm[:, k, m * P:(m + 1) * P], sc[:, k:k + 1],
                                             start=(k == 0), stop=(k == 1))
                elif kind == "A":
                    if job[1] == 0:
                        for k in range(2):
                            taken(pe, ("wkT", k))
                        for k in range(4):
                            taken(pe, ("wqT", k))
                    for k in range(8):
                        h = 8 * job[1] + k
                        last = pe.matmul(b[:, k * KVR:(k + 1) * KVR], wqT[:, h, :], wkT[:, h, :], start=True, stop=True)
                elif kind == "xT":
                    c, f = job[1:]
                    pe.wait_ge(xn_ready, c + 1)
                    for k in range(TPC):
                        last = pe.transpose(b[:, k * P:(k + 1) * P], xn[:, c * TPC + k, f * P:(f + 1) * P], ident[:, :])
                elif kind == "z":
                    c, half = job[1:]
                    pe.wait_ge(h_split, 2 * c + 2)
                    pe.wait_ge(wx_ready, 1)
                    for k in range(2):
                        tok = slice((2 * half + k) * P, (2 * half + k + 1) * P)
                        passes = [(a, w, f) for f in range(DF) for a, w in ((h_hi, wx_hi), (h_hi, wx_lo), (h_lo, wx_hi))]
                        for q, (a, w, f) in enumerate(passes):
                            last = pe.matmul(b[:, k * D:(k + 1) * D], a[:, c % 2, f, tok], w[:, f, :],
                                             start=(q == 0), stop=(q == len(passes) - 1))
                else:
                    c = job[1]
                    pe.wait_ge(nk_ready, c + 1)
                    src = nqn if kind == "nT" else kk
                    for k in range(TPC):
                        last = pe.transpose(b[:, k * P:(k + 1) * P], src[:, c * TPC + k, :], ident[:, :])
                last.then_inc(pe_done, 1)


def attend(nc, g, alloc):
    k_hi, k_lo, nq_hi, nq_lo, vals = (g[k] for k in ("k_hi", "k_lo", "nq_hi", "nq_lo", "vals"))
    wq_hi, wq_lo, lsum = g["wq_hi"], g["wq_lo"], g["lsum"]
    ident, identb, maskb = g["ident"], g["identb"], g["maskb"]
    cos_q, sin_q, rl_dram, ot_dram = g["cos_q"], g["sin_q"], g["rl_dram"], g["ot_dram"]
    pv_done, o_taken, on_ready = g["pv_done"], g["o_taken"], g["on_ready"]

    with ExitStack() as ctx:
        def sb(name, shape, dt=F32):
            return alloc(ctx, name, shape, dt)

        def sem(name):
            return ctx.enter_context(nc.semaphore(name))

        wh_hi = sb("wh_hi", [P, P], F32R)
        wh_lo = sb("wh_lo", [P, P], F32R)
        q_hi = sb("q_hi", [P, S], F32R)
        q_lo = sb("q_lo", [P, S], F32R)
        y = sb("y", [P, CH])
        yc = sb("yc", [P, CH])
        ys = sb("ys", [P, CH])
        zeros = sb("zeros", [P, CH])
        shared = [sb(f"shared{k}", [P, S]) for k in range(2)]
        rb, cosr = shared[0][0:KVR, :], shared[0]
        on, sinr = shared[1][0:KVR, :], shared[1]
        oraw = sb("oraw", [KVR, S])
        tmp = sb("tmp", [KVR, CH])
        prob = sb("prob", [P, SBANKS, CH])
        pt = [[sb(f"pt{b}{part}", [P, n, CH], F16) for part in ("hi", "lo")] for b, n in ((0, 12), (1, 16))]
        mx = sb("mx", [P, NT, 4])
        nm = sb("nm", [P, NT])
        l = sb("l", [P, NT])
        rl = sb("rl", [P, 32])
        rlT = sb("rlT", [P, 32])
        sbank = [ctx.enter_context(nc.psum_tensor(f"scores{b}", [P, CH], F32)) for b in range(SBANKS)]
        wbank = [ctx.enter_context(nc.psum_tensor(f"work{b}", [P, CH], F32)) for b in range(WBANKS)]

        s_tab = sem("s_tabq")
        wh_ready = sem("wh_ready")
        qp_done = sem("qp_done")
        q_taken = sem("q_taken")
        q_ready = sem("q_ready")
        pool_chain = sem("pool_chain")
        scored = sem("scored")
        unit_max = sem("unit_max")
        max_ready = sem("max_ready")
        exp_done = sem("exp_done")
        turned = sem("turned")
        hi_ready = sem("pthi_ready")
        lo_ready = sem("ptlo_ready")
        tmp_ready = sem("tmp_ready")
        l_chain = sem("l_chain")
        rl_ready = sem("rl_ready")
        rl_stored = sem("rl_stored")
        rb_loaded = sem("rb_loaded")
        ot_stored = sem("ot_stored")

        def after(h, per_head, k):
            return h * per_head + k

        def transposed(v, part):
            i, n = TILE_OF[v % NU], width(v) // P
            j0, r = (v % NU - FIRST[i]) * TPC, i % TPC
            return pt[(i // TPC) % 2][part][:, j0:j0 + n, r * P:(r + 1) * P]

        def turned_bank(v):
            return wbank[BANK[("t", v)]][:, 0:width(v)].rearrange("p (j q) -> p j q", q=P)

        def outputs(c):
            return wbank[BANK[("o", c)]]

        ident_in = g["ident_in"]
        block = ctx.enter_context(nc.Block())

        @block.tensor
        def _(pe):
            def bank_free(h, use):
                kind, n = BEFORE[use]
                if kind == "t":
                    pe.wait_ge(lo_ready, after(h, NU, n + 1))
                elif kind == "q":
                    pe.wait_ge(q_taken, after(h, NC, NC + n + 1))
                else:
                    pe.wait_ge(o_taken, after(h, NC, 1 + n + 1))

            def project(b, c):
                cols = slice(c * CH, (c + 1) * CH)
                pe.matmul(b[:, :], wh_hi[:, :], nq_hi[:, cols], start=True, stop=False)
                pe.matmul(b[:, :], wh_hi[:, :], nq_lo[:, cols], start=False, stop=False)
                pe.matmul(b[:, :], wh_lo[:, :], nq_hi[:, cols], start=False, stop=True).then_inc(qp_done, 1)

            def score(h, v):
                u, n = v % NU, width(v)
                i = TILE_OF[u]
                if starts_chunk(v):
                    pe.wait_ge(q_ready, after(h, NC, chunk_of(v) + 1))
                if v >= SBANKS:
                    pe.wait_ge(exp_done, after(h, NU, v - SBANKS + 1))
                b, k0 = sbank[u % SBANKS], (u - FIRST[i]) * CH
                q, k = slice(i * P, (i + 1) * P), slice(k0, k0 + n)
                pe.matmul(b[:, 0:n], q_hi[:, q], k_hi[:, k], start=True, stop=False)
                pe.matmul(b[:, 0:n], q_hi[:, q], k_lo[:, k], start=False, stop=False)
                if u == FIRST[i] + UNITS[i] - 1:
                    pe.matmul(b[:, n - P:n], identb[:, :], maskb[:, :], start=False, stop=False)
                pe.matmul(b[:, 0:n], q_lo[:, q], k_hi[:, k], start=False, stop=True).then_inc(scored, 1)

            def values(h, c):
                last = FIRST[TPC * c + 3] + UNITS[TPC * c + 3] - 1
                pe.wait_ge(lo_ready, after(h, NU, last + 1))
                bank_free(h, ("o", c))
                for j in range(TPC * (c + 1)):
                    q0 = max(0, j - TPC * c) * P
                    for part in range(2):
                        ins = pe.matmul(outputs(c)[:, q0:CH], vals[:, j, :], pt[c % 2][part][:, j, q0:CH],
                                        start=(j == 0 and part == 0), stop=(j == TPC * c + TPC - 1 and part == 1))
                ins.then_inc(pv_done, 1)

            def step(h, v):
                if v >= START and v in PV_BEFORE:
                    values(h, PV_BEFORE[v])
                bank_free(h, ("t", v))
                for k in range(width(v) // P):
                    ins = pe.transpose(wbank[BANK[("t", v)]][:, k * P:(k + 1) * P],
                                       prob[:, v % SBANKS, k * P:(k + 1) * P], ident[:, :])
                ins.then_inc(turned, 1)
                score(h, v + LEAD_S)
                if v >= START and v in QP_AFTER:
                    c = QP_AFTER[v]
                    if c == 0:
                        pe.wait_ge(wh_ready, after(h, 1, 2))
                    bank_free(h, ("q", c))
                    project(wbank[BANK[("q", c)]], c)

            pe.wait_ge(wh_ready, 1)
            for c in range(NC):
                if c >= WBANKS:
                    pe.wait_ge(q_taken, c - WBANKS + 1)
                project(wbank[c % WBANKS], c)
            for v in range(LEAD_S):
                score(0, v)
            for v in range(START):
                step(0, v)
            with pe.Fori(0, NH) as h:
                for v in range(START, START + NU):
                    step(h, v)

        @block.vector
        def _(dve):
            def maximum(h, v):
                i, n = TILE_OF[v % NU], width(v)
                k, b = v % NU - FIRST[i], sbank[v % SBANKS][:, 0:n]
                dve.wait_ge(scored, after(h, NU, v + 1))
                if UNITS[i] == 1:
                    dve.tensor_reduce(nm[:, i:i + 1], b, AX_X, ALU.max, negate=True).then_inc(max_ready, 1)
                    return
                dve.tensor_reduce(mx[:, i, k:k + 1], b, AX_X, ALU.max).then_inc(unit_max, 1)
                if k == UNITS[i] - 1:
                    dve.wait_ge(unit_max, after(h, MULTI, multi_before(v)))
                    dve.tensor_reduce(nm[:, i:i + 1], mx[:, i, 0:UNITS[i]], AX_X, ALU.max,
                                      negate=True).then_inc(max_ready, 1)

            def low_parts(h, v):
                dve.wait_ge(hi_ready, after(h, NU, v + 1))
                dve.scalar_tensor_tensor(out=transposed(v, 1), in0=turned_bank(v), scalar=PSCALE,
                                         in1=transposed(v, 0), op0=ALU.mult, op1=ALU.subtract).then_inc(lo_ready, 1)

            def take_outputs(h, c):
                dve.wait_ge(on_ready, after(h, NC, c + 1))
                dve.wait_ge(tmp_ready, after(h, NC, c + 1))
                dve.scalar_tensor_tensor(out=oraw[:, c * CH:(c + 1) * CH], in0=outputs(c)[0:KVR, :], scalar=1.0 / PSCALE,
                                         in1=tmp[:, :], op0=ALU.mult, op1=ALU.add).then_inc(o_taken, 1)

            def step(h, v):
                if v == SUMS_EARLY:
                    dve.wait_ge(exp_done, after(h, NU, FIRST[12]))
                    dve.tensor_reduce(l[:, 0:12], lsum[:, 0:12, :], AX_X, ALU.add).then_inc(l_chain, 1)
                maximum(h, v + LEAD_S)
                low_parts(h, v)
                if v == SUMS_LATE:
                    dve.wait_ge(exp_done, after(h, NU, NU))
                    dve.tensor_reduce(l[:, 12:NT], lsum[:, 12:NT, :], AX_X, ALU.add).then_inc(l_chain, 1)
                    dve.wait_ge(l_chain, after(h, 3, 3))
                    dve.reciprocal(rl[:, 0:NT], l[:, :]).then_inc(l_chain, 1)
                    dve.wait_ge(l_chain, after(h, 3, 4))
                    dve.wait_ge(ot_stored, after(h, 16, 16))
                    dve.transpose(rlT[:, :], rl[:, :]).then_inc(rl_ready, 1)
                if v >= START and v in PV_BEFORE:
                    take_outputs(h, PV_BEFORE[v])

            dve.memset(rl[:, :], 0.0).then_inc(l_chain, 1)
            for v in range(LEAD_S):
                maximum(0, v)
            for v in range(START):
                step(0, v)
            with dve.Fori(0, NH) as h:
                for v in range(START, START + NU):
                    step(h, v)

        @block.scalar
        def _(act):
            def take_query(b, before):
                act.wait_ge(qp_done, before + 1)
                if not (isinstance(before, int) and before == 0):
                    act.wait_ge(q_ready, before)
                act.activation(y[:, :], b[:, :], ACT.Copy).then_inc(q_taken, 1)

            def exponentials(h, v):
                i, n = TILE_OF[v % NU], width(v)
                k = v % NU - FIRST[i]
                if k == 0:
                    act.wait_ge(max_ready, after(h, NT, i + 1 + NT * (v // NU)))
                act.activation(prob[:, v % SBANKS, 0:n], sbank[v % SBANKS][:, 0:n], ACT.Exp, bias=nm[:, i:i + 1],
                               accum_out=lsum[:, i, k:k + 1]).then_inc(exp_done, 1)

            def low_rows(h, c):
                act.wait_ge(pv_done, after(h, NC, 2 + c + 1))
                act.wait_ge(o_taken, after(h, NC, 1 + c))
                act.activation(tmp[:, :], outputs(c)[KVR:P, :], ACT.Copy, scale=1.0 / PSCALE).then_inc(tmp_ready, 1)

            def step(h, v):
                act.wait_ge(turned, after(h, NU, v + 1))
                if starts_chunk(v):
                    act.wait_ge(pv_done, after(h, NC, chunk_of(v) + 1))
                act.activation(transposed(v, 0), turned_bank(v), ACT.Copy, scale=PSCALE).then_inc(hi_ready, 1)
                if v >= START and v in QP_AFTER:
                    c = QP_AFTER[v]
                    take_query(wbank[BANK[("q", c)]], after(h, NC, NC + c))
                if v >= START and v in PV_BEFORE:
                    low_rows(h, PV_BEFORE[v])
                exponentials(h, v + LEAD_E)

            for c in range(NC):
                take_query(wbank[c % WBANKS], c)
            for v in range(LEAD_E):
                exponentials(0, v)
            for v in range(START):
                step(0, v)
            with act.Fori(0, NH) as h:
                for v in range(START, START + NU):
                    step(h, v)

        @block.gpsimd
        def _(pool):
            def load_weights(h):
                pool.tensor_copy(wh_hi[:, :], wq_hi[:, h, :]).then_inc(pool_chain, 1)
                pool.tensor_copy(wh_lo[:, :], wq_lo[:, h, :]).then_inc(wh_ready, 1)

            def parts(c, taken, chain):
                cols = slice(c * CH, (c + 1) * CH)
                rot, e, o = slice(KVR, P), slice(KVR, KVR + HALF), slice(KVR + HALF, P)
                pool.wait_ge(q_taken, taken)
                pool.tensor_tensor(yc[rot, :], y[rot, :], cosr[rot, cols], ALU.mult).then_inc(pool_chain, 1)
                pool.wait_ge(pool_chain, chain + 1)
                pool.tensor_tensor(ys[e, :], y[o, :], sinr[o, cols], ALU.mult).then_inc(pool_chain, 1)
                pool.wait_ge(pool_chain, chain + 2)
                pool.tensor_tensor(ys[o, :], y[e, :], sinr[e, cols], ALU.mult).then_inc(pool_chain, 1)
                pool.wait_ge(pool_chain, chain + 3)
                pool.tensor_tensor(y[rot, :], yc[rot, :], ys[rot, :], ALU.add).then_inc(pool_chain, 1)
                pool.wait_ge(pool_chain, chain + 4)
                pool.tensor_tensor(q_hi[:, cols], y[:, :], zeros[:, :], ALU.add).then_inc(pool_chain, 1)
                pool.wait_ge(pool_chain, chain + 5)
                pool.tensor_tensor(q_lo[:, cols], y[:, :], q_hi[:, cols].bitcast(F32), ALU.subtract).then_inc(q_ready, 1)

            chain = 5 * NC + 1
            pool.memset(zeros[:, :], 0.0).then_inc(pool_chain, 1)
            load_weights(0)
            pool.wait_ge(s_tab, 32)
            for c in range(NC):
                parts(c, c + 1, 2 + 5 * c)
            load_weights(1)
            with pool.Fori(0, NH) as h:
                for c in range(NC):
                    parts(c, after(h, NC, NC + c + 1), after(h, chain, 3 + 5 * NC + 5 * c))
                load_weights(h + 2)
                pool.wait_ge(rb_loaded, after(h, 16, 16))
                for c in range(NC):
                    cols = slice(c * CH, (c + 1) * CH)
                    pool.wait_ge(o_taken, after(h, NC, 1 + c + 1))
                    pool.tensor_tensor(on[:, cols], oraw[:, cols], rb[:, cols], ALU.mult).then_inc(on_ready, 1)

        @block.sync
        def _(sp):
            sp.dma_start(cosr[KVR:P, :], cos_q).then_inc(s_tab, 16)
            sp.dma_start(sinr[KVR:P, :], sin_q).then_inc(s_tab, 16)
            sp.dma_start(rlT[:, :], ident_in[:, 0:32]).then_inc(ot_stored, 16)
            with sp.Fori(0, NH) as h:
                row = sp.snap(h * KVR)
                sp.wait_ge(rl_ready, after(h, 1, 1))
                for a in range(4):
                    sp.dma_start(rl_dram.rearrange("(t p) -> t p", p=P)[:, 32 * a:32 * a + 32],
                                 rlT[32 * a:32 * a + NT, :]).then_inc(rl_stored, 16)
                sp.wait_ge(rl_stored, after(h, 64, 64))
                sp.wait_ge(ot_stored, after(h, 16, 16))
                sp.dma_start(rb, rl_dram.rearrange("(a s) -> a s", a=1).to_broadcast([KVR, S])).then_inc(rb_loaded, 16)
                sp.wait_ge(on_ready, after(h, NC, 2 * NC))
                sp.dma_start(ot_dram[bass.ds(row, KVR), :], on).then_inc(ot_stored, 16)
            sp.wait_ge(ot_stored, 16 * (NH + 1))


def finish(nc, g, alloc):
    with ExitStack() as ctx:
        def sb(name, shape, dt=F32):
            return alloc(ctx, name, shape, dt)

        g["b_hi"] = sb("b_hi", [P, NH // 2, D], F32R)
        g["b_lo"] = sb("b_lo", [P, NH // 2, D], F32R)
        g["gu_hi"] = sb("gu_hi", [P, 2, DF, HIDP], F32R)
        g["gu_lo"] = sb("gu_lo", [P, 2, DF, HIDP], F32R)
        g["dn_hi"] = sb("dn_hi", [P, HT, D], F32R)
        g["dn_lo"] = sb("dn_lo", [P, HT, D], F32R)
        last_weights(nc, g, alloc)
        last_layers(nc, g, alloc)


def last_weights(nc, g, alloc):
    w_v, w_o, ident, kvs = g["w_v"], g["w_o"], g["ident"], g["kvs"]
    b_hi, b_lo, gu_hi, gu_lo, dn_hi, dn_lo = (g[k] for k in ("b_hi", "b_lo", "gu_hi", "gu_lo", "dn_hi", "dn_lo"))
    full = HID // P
    rest = HID - full * P

    with ExitStack() as ctx:
        def sb(name, shape, dt=F32):
            return alloc(ctx, name, shape, dt)

        def sem(name):
            return ctx.enter_context(nc.semaphore(name))

        wv = sb("wv", [KVR, NH, VD])
        wo = sb("wo", [P, NH, D])
        wvT = sb("wvT", [P, NH, KVR])
        wgi = sb("wgi", [P, 2, HT, D], I32)
        wdi = sb("wdi", [P, DF, HID], I32)
        wg = sb("wg", [P, 2, HT, D])
        wd = sb("wd", [P, DF, HIDP])
        sg = sb("sg", [P, 2, HT])
        sdn = sb("sdn", [P, DF])
        banks = [ctx.enter_context(nc.psum_tensor(f"lw{b}", [P, CH], F32)) for b in range(8)]

        jobs = [("vT", k) for k in range(2)] + [("B", k) for k in range(4)]
        jobs += [("gu", a, f, k) for a in range(2) for f in range(DF) for k in range(2)] + [("dn", k) for k in range(3)]
        index = {j: n for n, j in enumerate(jobs)}
        dest = {}
        for k in range(4):
            dest[("B", k)] = [x[:, 2 * k:2 * k + 2, :].rearrange("p a n -> p (a n)") for x in (b_hi, b_lo)]
        for a in range(2):
            for f in range(DF):
                for k, (lo, hi) in enumerate(((0, CH), (CH, HIDP))):
                    dest[("gu", a, f, k)] = [x[:, a, f, lo:hi] for x in (gu_hi, gu_lo)]
        for k in range(3):
            dest[("dn", k)] = [x[:, 2 * k:2 * k + 2, :].rearrange("p a n -> p (a n)") for x in (dn_hi, dn_lo)]

        s_v, s_o, s_i, s_d, s_sg = sem("s_v"), sem("s_o"), sem("s_i"), sem("s_d"), sem("s_sg")
        pe_done = sem("lw_done")
        hi_done = sem("lw_hi")
        taken = sem("lw_taken")
        vt_taken = sem("vt_taken")
        wv_ready = sem("wv_ready")
        w_ready = sem("w_ready")
        zeroed = sem("zeroed")

        block = ctx.enter_context(nc.Block())

        @block.sync
        def _(sp):
            sp.dma_start(wv[:, :, :], w_v.rearrange("r (h n) -> r h n", h=NH)).then_inc(s_v, 16)
            sp.dma_start(wo[:, :, :], w_o.rearrange("(h n) m -> n h m", h=NH)).then_inc(s_o, 16)
            for a, wq in enumerate((g["wq_gate"], g["wq_up"])):
                sp.dma_start(wgi[:, a, 0:full, :], wq[0:full * P, :].rearrange("(m p) d -> p m d", p=P)).then_inc(s_i, 16)
                sp.dma_start(wgi[0:rest, a, full, :], wq[full * P:HID, :]).then_inc(s_i, 16)

        @block.gpsimd
        def _(pool):
            pool.dma_start(wdi[:, :, :], g["wq_down"].rearrange("(f p) n -> p f n", p=P)).then_inc(s_d, 16)
            for f in range(DF):
                pool.dma_start(sdn[:, f:f + 1], g["s_down"][f * P:(f + 1) * P].rearrange("(p a) -> p a", a=1)).then_inc(s_d, 16)
            for a, s in enumerate((g["s_gate"], g["s_up"])):
                for m in range(full):
                    pool.dma_start(sg[:, a, m:m + 1], s[m * P:(m + 1) * P].rearrange("(p a) -> p a", a=1)).then_inc(s_sg, 16)
                pool.dma_start(sg[0:rest, a, full:full + 1], s[full * P:HID].rearrange("(p a) -> p a", a=1)).then_inc(s_sg, 16)

        @block.vector
        def _(dve):
            dve.memset(wg[:, :, full, :], 0.0).then_inc(zeroed, 1)
            dve.memset(wd[:, :, HID:HIDP], 0.0).then_inc(zeroed, 1)
            dve.wait_ge(s_v, 16)
            dve.tensor_scalar(wv[:, :, :], wv[:, :, :], kvs[:, 0:1], None, ALU.mult).then_inc(wv_ready, 1)
            dve.wait_ge(s_i, 64)
            dve.wait_ge(s_sg, 16 * 2 * HT)
            dve.wait_ge(zeroed, 2)
            for a in range(2):
                for m in range(HT):
                    rows = P if m < full else rest
                    dve.tensor_scalar(wg[0:rows, a, m, :], wgi[0:rows, a, m, :], ZERO_POINT, sg[0:rows, a, m:m + 1],
                                      ALU.subtract, ALU.mult).then_inc(w_ready, 1)
            dve.wait_ge(s_d, 48)
            for f in range(DF):
                dve.tensor_scalar(wd[:, f, 0:HID], wdi[:, f, :], ZERO_POINT, sdn[:, f:f + 1],
                                  ALU.subtract, ALU.mult).then_inc(w_ready, 1)
            for n, job in enumerate(jobs):
                if job[0] == "vT":
                    continue
                hi, lo = dest[job]
                dve.wait_ge(hi_done, n - 1)
                dve.tensor_tensor(lo, banks[n % 8][:, 0:hi.shape[-1]], hi.bitcast(F32), ALU.subtract).then_inc(taken, 1)

        @block.scalar
        def _(act):
            for n, job in enumerate(jobs):
                act.wait_ge(pe_done, n + 1)
                if job[0] == "vT":
                    act.activation(wvT[:, 8 * n:8 * n + 8, :].rearrange("p h n -> p (h n)"), banks[n][:, :],
                                   ACT.Copy).then_inc(vt_taken, 1)
                else:
                    hi = dest[job][0]
                    act.activation(hi, banks[n % 8][:, 0:hi.shape[-1]], ACT.Copy).then_inc(hi_done, 1)

        @block.tensor
        def _(pe):
            for n, job in enumerate(jobs):
                b = banks[n % 8]
                if 8 <= n < 10:
                    pe.wait_ge(vt_taken, n - 7)
                elif n >= 10:
                    pe.wait_ge(taken, n - 9)
                if job[0] == "vT":
                    pe.wait_ge(wv_ready, 1)
                    for k in range(8):
                        last = pe.transpose(b[:, k * KVR:(k + 1) * KVR], wv[:, 8 * job[1] + k, :], ident[0:KVR, 0:KVR])
                elif job[0] == "B":
                    pe.wait_ge(vt_taken, 2)
                    pe.wait_ge(s_o, 16)
                    for k in range(4):
                        h = 4 * job[1] + k
                        r = (h % 2) * KVR
                        last = pe.matmul(b[r:r + KVR, (k // 2) * D:(k // 2 + 1) * D], wvT[:, h, :], wo[:, h, :],
                                         start=True, stop=True)
                elif job[0] == "gu":
                    _, a, f, k = job
                    pe.wait_ge(w_ready, HT * (a + 1))
                    for m in range(4 * k, min(4 * k + 4, HT)):
                        last = pe.transpose(b[:, (m - 4 * k) * P:(m - 4 * k + 1) * P], wg[:, a, m, f * P:(f + 1) * P],
                                            ident[:, :])
                else:
                    pe.wait_ge(w_ready, 2 * HT + DF)
                    for k in range(4):
                        m, f = 2 * job[1] + k // 2, k % 2
                        last = pe.transpose(b[:, k * P:(k + 1) * P], wd[:, f, m * P:(m + 1) * P], ident[:, :])
                last.then_inc(pe_done, 1)


def last_layers(nc, g, alloc):
    x, out, ot_dram, ident, eps = g["x"], g["out"], g["ot_dram"], g["ident"], g["eps"]
    GA, SB, CB, GB = g["GA"], g["SB"], g["CB"], g["GB"]
    b_hi, b_lo, gu_hi, gu_lo, dn_hi, dn_lo = (g[k] for k in ("b_hi", "b_lo", "gu_hi", "gu_lo", "dn_hi", "dn_lo"))
    NP = NH // 2

    events = [("X", 0), ("T", 0)]
    for c in range(NC):
        for m in range(HT):
            events.append(("GU", c, m))
            if m == 1 and c:
                events.append(("O", c - 1))
            if m == 2 and c + 1 < NC:
                events.append(("X", c + 1))
            if m == 3 and c + 1 < NC:
                events.append(("T", c + 1))
            if m:
                events.append(("DN", c, m - 1))
        events.append(("DN", c, HT - 1))
    events.append(("O", NC - 1))

    with ExitStack() as ctx:
        def sb(name, shape, dt=F32):
            return alloc(ctx, name, shape, dt)

        def sem(name):
            return ctx.enter_context(nc.semaphore(name))

        xs = sb("x1", [P, NT, D])
        st, mv, sd, rstd = sb("st2", [P, NT, 6]), sb("mv2", [P, NT, 2]), sb("sd2", [P, NT]), sb("rstd2", [P, NT])
        half = ExitStack()
        ot = alloc(half, "ot", [P, 2, NP, CH], F32)
        o_hi = alloc(half, "o_hi", [P, NP, CH], F32R)
        o_lo = alloc(half, "o_lo", [P, NP, CH], F32R)
        yT = alloc(half, "yT", [P, 2, DF, CH], F32)
        banks = [ctx.enter_context(nc.psum_tensor(f"ll{b}", [P, CH], F32)) for b in range(8)]

        s_ot, s_x = [sem(f"s_ot{c}") for c in range(NC)], sem("s_x1")
        hi_done, o_split, pair_used = sem("o_hi_done"), sem("o_split"), sem("pair_used")
        y_ready, y_turned, x1_ready = sem("y_ready"), sem("y_turned"), sem("x1_ready")
        st_ready, mv_ready, sd2_ready = sem("st_ready"), sem("mv_ready"), sem("sd2_ready")
        rstd_ready = sem("rstd_ready")

        with nc.Block() as block:
            @block.sync
            def _(sp):
                src = ot_dram.rearrange("(a p) s -> p a s", p=P)
                for c in range(NC):
                    if c >= 2:
                        sp.wait_ge(o_split, NP * (c - 1))
                    sp.dma_start(ot[:, c % 2, :, :], src[:, :, c * CH:(c + 1) * CH]).then_inc(s_ot[c], 16)

            @block.scalar
            def _(act):
                act.dma_start(xs[:, :, :], x.rearrange("a (t p) d -> p (a t) d", p=P)).then_inc(s_x, 16)
                for c in range(NC):
                    act.wait_ge(pair_used, NP * (c + 1))
                    if c >= 2:
                        act.wait_ge(y_turned, 2 * (c - 1))
                    for f in range(DF):
                        act.activation(yT[:, c % 2, f, :], banks[2 * (c % 2) + f][:, :], ACT.Copy,
                                       scale=GA[:, f:f + 1]).then_inc(y_ready, 1)
                act.wait_ge(mv_ready, NT)
                act.activation(sd[:, :], mv[:, :, 1], ACT.Sqrt, bias=eps[:, 0:1]).then_inc(sd2_ready, 1)

            @block.vector
            def _(dve):
                def residual(c):
                    for f in range(DF):
                        dve.wait_ge(y_turned, 2 * c + f + 1)
                        cols = xs[:, TPC * c:TPC * (c + 1), f * P:(f + 1) * P]
                        dve.tensor_tensor(cols, banks[4 + f][:, :].rearrange("p (t n) -> p t n", n=P), cols,
                                          ALU.add).then_inc(x1_ready, 1)
                    dve.wait_ge(x1_ready, 2 * (c + 1))
                    for t in range(TPC * c, TPC * (c + 1)):
                        dve.bn_stats(st[:, t, :], xs[:, t, :]).then_inc(st_ready, 1)
                    dve.wait_ge(st_ready, TPC * (c + 1))
                    for t in range(TPC * c, TPC * (c + 1)):
                        dve.bn_aggr(mv[:, t, :], st[:, t, :]).then_inc(mv_ready, 1)

                for c in range(NC):
                    dve.wait_ge(s_ot[c], 16)
                    for a in range(NP):
                        if c:
                            dve.wait_ge(pair_used, NP * (c - 1) + a + 1)
                        dve.tensor_copy(o_hi[:, a, :], ot[:, c % 2, a, :]).then_inc(hi_done, 1)
                        dve.wait_ge(hi_done, NP * c + a + 1)
                        dve.tensor_tensor(o_lo[:, a, :], ot[:, c % 2, a, :], o_hi[:, a, :].bitcast(F32),
                                          ALU.subtract).then_inc(o_split, 1)
                    if c == 0:
                        dve.wait_ge(s_x, 16)
                    else:
                        residual(c - 1)
                residual(NC - 1)
                dve.wait_ge(sd2_ready, 1)
                dve.reciprocal(rstd[:, :], sd[:, :]).then_inc(rstd_ready, 1)

            @block.tensor
            def _(pe):
                def turn(c):
                    for f in range(DF):
                        pe.wait_ge(y_ready, 2 * c + f + 1)
                        if c:
                            pe.wait_ge(x1_ready, 2 * (c - 1) + f + 1)
                        for k in range(TPC):
                            last = pe.transpose(banks[4 + f][:, k * P:(k + 1) * P],
                                                yT[:, c % 2, f, k * P:(k + 1) * P], ident[:, :])
                        last.then_inc(y_turned, 1)

                for c in range(NC):
                    if c >= 2:
                        pe.wait_ge(y_ready, 2 * (c - 1))
                    for a in range(NP):
                        pe.wait_ge(o_split, NP * c + a + 1)
                        for q, (w, o) in enumerate(((b_hi, o_hi), (b_hi, o_lo), (b_lo, o_hi))):
                            for f in range(DF):
                                last = pe.matmul(banks[2 * (c % 2) + f][:, :], w[:, a, f * P:(f + 1) * P], o[:, a, :],
                                                 start=(a == 0 and q == 0), stop=(a == NP - 1 and q == 2))
                        last.then_inc(pair_used, 1)
                    if c:
                        turn(c - 1)
                turn(NC - 1)
        half.close()

        xn = sb("xn2", [P, TPC, D])
        h32 = sb("h2", [P, DF, CH])
        h_hi, h_lo = sb("h2_hi", [P, 2, DF, CH], F32R), sb("h2_lo", [P, 2, DF, CH], F32R)
        sl = sb("sl", [P, 2, CH])
        a32 = sb("a32", [P, 2, CH])
        a_hi, a_lo = sb("a_hi", [P, 2, CH], F32R), sb("a_lo", [P, 2, CH], F32R)
        fT = sb("fT", [P, DF, CH])
        res = sb("res", [P, 2, TPC, D])

        xn_ready, t_done, t_taken, h_hi_done, h_split = (sem(n) for n in ("x2n", "x2t", "x2taken", "h2hi", "h2split"))
        gu_done, silu_done, prod_done, a_hi_done, a_split = (sem(n) for n in ("gud", "silud", "prodd", "ahid", "asplit"))
        dn_done, f_taken, o_turned, o_added = (sem(n) for n in ("dnd", "ftaken", "oturned", "oadded"))
        stored = [sem(f"stored{c}") for c in range(NC)]

        with nc.Block() as block:
            @block.sync
            def _(sp):
                for c in range(NC):
                    sp.wait_ge(o_added, 2 * (c + 1))
                    sp.dma_start(out[0, c * CH:(c + 1) * CH, :].rearrange("(t p) d -> p t d", p=P),
                                 res[:, c % 2, :, :]).then_inc(stored[c], 16)
                for c in range(NC):
                    sp.wait_ge(stored[c], 16)

            @block.vector
            def _(dve):
                for e in events:
                    kind, c = e[0], e[1]
                    if kind == "X":
                        if c:
                            dve.wait_ge(t_done, 2 * c)
                        for k in range(TPC):
                            t = TPC * c + k
                            dve.tensor_scalar(xn[:, k, :], xs[:, t, :], mv[:, t, 0:1], rstd[:, t:t + 1],
                                              ALU.subtract, ALU.mult).then_inc(xn_ready, 1)
                    elif kind == "T":
                        if c >= 2:
                            dve.wait_ge(gu_done, HT * (c - 1))
                        for f in range(DF):
                            dve.wait_ge(t_taken, 2 * c + f + 1)
                            dve.tensor_copy(h_hi[:, c % 2, f, :], h32[:, f, :]).then_inc(h_hi_done, 1)
                            dve.wait_ge(h_hi_done, 2 * c + f + 1)
                            dve.tensor_tensor(h_lo[:, c % 2, f, :], h32[:, f, :], h_hi[:, c % 2, f, :].bitcast(F32),
                                              ALU.subtract).then_inc(h_split, 1)
                    elif kind == "GU":
                        n = HT * c + e[2]
                        dve.wait_ge(silu_done, n + 1)
                        if n >= 2:
                            dve.wait_ge(a_split, n - 1)
                        dve.tensor_tensor(a32[:, n % 2, :], banks[2 * (n % 2) + 1][:, :], sl[:, n % 2, :],
                                          ALU.mult).then_inc(prod_done, 1)
                        if n >= 2:
                            dve.wait_ge(dn_done, n - 1)
                        dve.wait_ge(prod_done, n + 1)
                        dve.tensor_copy(a_hi[:, n % 2, :], a32[:, n % 2, :]).then_inc(a_hi_done, 1)
                        dve.wait_ge(a_hi_done, n + 1)
                        dve.tensor_tensor(a_lo[:, n % 2, :], a32[:, n % 2, :], a_hi[:, n % 2, :].bitcast(F32),
                                          ALU.subtract).then_inc(a_split, 1)
                    elif kind == "O":
                        if c >= 2:
                            dve.wait_ge(stored[c - 2], 16)
                        for f in range(DF):
                            dve.wait_ge(o_turned, 2 * c + f + 1)
                            cols = slice(f * P, (f + 1) * P)
                            dve.tensor_tensor(res[:, c % 2, :, cols],
                                              banks[4 + f][:, :].rearrange("p (t n) -> p t n", n=P),
                                              xs[:, TPC * c:TPC * (c + 1), cols], ALU.add).then_inc(o_added, 1)

            @block.scalar
            def _(act):
                for e in events:
                    kind, c = e[0], e[1]
                    if kind == "T":
                        for f in range(DF):
                            act.wait_ge(t_done, 2 * c + f + 1)
                            if c:
                                act.wait_ge(h_split, 2 * (c - 1) + f + 1)
                            act.activation(h32[:, f, :], banks[4 + f][:, :], ACT.Identity, bias=SB[:, f:f + 1],
                                           scale=CB[:, f:f + 1]).then_inc(t_taken, 1)
                    elif kind == "GU":
                        n = HT * c + e[2]
                        act.wait_ge(gu_done, n + 1)
                        if n >= 2:
                            act.wait_ge(prod_done, n - 1)
                        act.activation(sl[:, n % 2, :], banks[2 * (n % 2)][:, :], ACT.Silu).then_inc(silu_done, 1)
                    elif kind == "DN" and e[2] == HT - 1:
                        act.wait_ge(dn_done, HT * (c + 1))
                        if c:
                            act.wait_ge(o_turned, 2 * c)
                        for f in range(DF):
                            act.activation(fT[:, f, :], banks[6 + f][:, :], ACT.Copy, scale=GB[:, f:f + 1]).then_inc(f_taken, 1)

            @block.tensor
            def _(pe):
                for at, e in enumerate(events):
                    kind, c = e[0], e[1]
                    if kind == "T":
                        pe.wait_ge(xn_ready, TPC * (c + 1))
                        if c >= 2:
                            pe.wait_ge(o_added, 2 * (c - 1))
                        elif c == 1:
                            pe.wait_ge(t_taken, 2)
                        for f in range(DF):
                            for k in range(TPC):
                                last = pe.transpose(banks[4 + f][:, k * P:(k + 1) * P], xn[:, k, f * P:(f + 1) * P],
                                                    ident[:, :])
                            last.then_inc(t_done, 1)
                    elif kind == "O":
                        pe.wait_ge(f_taken, 2 * (c + 1))
                        pe.wait_ge(t_taken, 2 * min(c + 2, NC))
                        for f in range(DF):
                            if c == NC - 1:
                                pe.wait_ge(o_added, 2 * c)
                            for k in range(TPC):
                                last = pe.transpose(banks[4 + f][:, k * P:(k + 1) * P], fT[:, f, k * P:(k + 1) * P],
                                                    ident[:, :])
                            last.then_inc(o_turned, 1)
                    elif kind == "GU":
                        n = HT * c + e[2]
                        if e[2] == 0:
                            pe.wait_ge(h_split, 2 * (c + 1))
                        if n >= 2:
                            pe.wait_ge(prod_done, n - 1)
                        cols = slice(e[2] * P, (e[2] + 1) * P)
                        for a in range(2):
                            passes = [(w, h, f) for f in range(DF)
                                      for w, h in ((gu_hi, h_hi), (gu_hi, h_lo), (gu_lo, h_hi))]
                            for q, (w, h, f) in enumerate(passes):
                                last = pe.matmul(banks[2 * (n % 2) + a][:, :], w[:, a, f, cols], h[:, c % 2, f, :],
                                                 start=(q == 0), stop=(q == len(passes) - 1))
                        last.then_inc(gu_done, 1)
                    elif kind == "DN":
                        n = HT * c + e[2]
                        pe.wait_ge(a_split, n + 1)
                        if e[2] == 0 and c:
                            pe.wait_ge(f_taken, 2 * c)
                        for f in range(DF):
                            cols = slice(f * P, (f + 1) * P)
                            for q, (w, a) in enumerate(((dn_hi, a_hi), (dn_hi, a_lo), (dn_lo, a_hi))):
                                last = pe.matmul(banks[6 + f][:, :], w[:, e[2], cols], a[:, n % 2, :],
                                                 start=(e[2] == 0 and q == 0), stop=(e[2] == HT - 1 and q == 2))
                        last.then_inc(dn_done, 1)


_INS = ["L0_attn_x", "L0_attn_W_cq", "L0_attn_q_scale", "L0_attn_W_dq_nope", "L0_attn_W_dq_rope", "L0_attn_W_ckv",
        "L0_attn_kv_scale", "L0_attn_W_dk_nope", "L0_attn_W_dv", "L0_attn_W_krope", "L0_attn_W_o",
        "L0_ffn_wq_gate", "L0_ffn_s_gate", "L0_ffn_wq_up", "L0_ffn_s_up", "L0_ffn_wq_down", "L0_ffn_s_down",
        "L0_c", "L0_wmod"]


def shape_constants():
    f = np.float32
    inv = (f(1.0) / np.power(f(10000.0), np.arange(HALF, dtype=f) * f(2.0) / f(ROPE))).astype(f)
    ang = np.arange(S, dtype=f)[:, None] * inv[None, :]
    cos, sin = np.cos(ang).astype(f), np.sin(ang).astype(f)
    return {
        "ident": np.eye(P, dtype=f),
        "mask": np.where(np.arange(P)[None, :] > np.arange(P)[:, None], f(MASKED), f(0)).astype(f),
        "cos_q": np.ascontiguousarray(np.concatenate([cos.T, cos.T])),
        "sin_q": np.ascontiguousarray(np.concatenate([sin.T, -sin.T])),
        "cos_k": cos / f(NH),
        "sin_k": sin / f(NH),
    }


def kernel(**inputs):
    import concourse.bacc as _bacc
    from concourse.bass_utils import run_bass_kernel_spmd as _run

    nc = _bacc.Bacc("TRN2", target_bir_lowering=False, num_devices=1)
    arrays, args = {}, []
    given = {n: np.ascontiguousarray(inputs[n]) for n in _INS} | shape_constants()
    for name, a in given.items():
        arrays[f"in_{name}_dram"] = a
        args.append(nc.dram_tensor(f"in_{name}_dram", a.shape, mybir.dt.from_np(a.dtype), kind="ExternalInput").ap())
    out = nc.dram_tensor("out_dram", (1, S, D), F32, kind="ExternalOutput").ap()
    adaln_block(nc, *args, out)
    r = _run(nc, [arrays], core_ids=[0])
    return r.results[0]["out_dram"]
```

```python
from contextlib import ExitStack

import numpy as np

import concourse.bass as bass
from concourse import mybir

F32 = mybir.dt.float32
F32R = mybir.dt.float32r
BF16 = mybir.dt.bfloat16
F16 = mybir.dt.float16
I32 = mybir.dt.int32
ALU = mybir.AluOpType
ACT = mybir.ActivationFunctionType
AX_X = mybir.AxisListType.X

P = 128
S = 2048
D = 256
DF = D // P
NH = 16
NOPE, ROPE, VD = 128, 64, 128
QR, KVR = 128, 64
HALF = ROPE // 2
HID, HIDP = 704, 768
HT = HIDP // P
ZERO_POINT = 128.0
NT = S // P
CH = 512
NC = S // CH
TPC = CH // P
RMS_EPS, LN_EPS = 1e-6, 1e-5
SCORE_SCALE = float((NOPE + ROPE) ** -0.5)
MASKED = -1e30
PSCALE = 1024.0

UNITS = [(i * P + P + CH - 1) // CH for i in range(NT)]
FIRST = [sum(UNITS[:i]) for i in range(NT)]
NU = sum(UNITS)
TILE_OF = [i for i in range(NT) for _ in range(UNITS[i])]
SBANKS = 5
WBANKS = 3
LEAD_S = {1: [6], 2: [7, 6], 3: [5, 5, 5], 4: [7, 6, 6, 7]}
LEAD_M = {1: [5], 2: [6, 6], 3: [5, 6, 5], 4: [7, 6, 6, 6]}
LEAD_E = {1: [3], 2: [4, 3], 3: [2, 3, 3], 4: [3, 4, 3, 4]}
MAXIMA_LAST = {3: [1, 2], 4: [1]}
assert NU % SBANKS == 0

START = 6
QP_AFTER = {9: 0, 17: 1, 26: 2, 38: 3}
DVE_CHUNKS = 2
PV_BEFORE = {7: 0, 23: 1, 34: 2, 42: 3}


def width(v):
    i = TILE_OF[v % NU]
    return min(CH, (i + 1) * P - (v % NU - FIRST[i]) * CH)


def chunk_of(v):
    return TILE_OF[v % NU] // TPC + NC * (v // NU)


def starts_chunk(v):
    return TILE_OF[v % NU] % TPC == 0 and v % NU == FIRST[TILE_OF[v % NU]]


def place(v):
    i = TILE_OF[v % NU]
    return UNITS[i], v % NU - FIRST[i]


def reached(lead, v):
    return max(w + lead[place(w)[0]][place(w)[1]] for w in range(v - 3, v + 1))


def ahead(lead, v, last=False):
    return [n for n in range(reached(lead, v - 1) + 1, reached(lead, v) + 1) if n < NU or not last]


SUMS_EARLY = next(v for v in range(NU) if NU in ahead(LEAD_M, v))
SUMS_LATE = NU


def multi_before(v):
    return sum(1 for j in range(v + 1) if UNITS[TILE_OF[j % NU]] > 1)


MULTI = multi_before(NU - 1)


def bank_order():
    uses = [("q", c - NC) for c in range(NC)]
    for v in range(START + NU):
        if v >= START and v in PV_BEFORE:
            uses.append(("o", PV_BEFORE[v]))
        uses.append(("t", v))
        if v >= START and v in QP_AFTER:
            uses.append(("q", QP_AFTER[v]))
    return uses


USES = bank_order()
BANK = {use: n % WBANKS for n, use in enumerate(USES)}
BEFORE = {use: USES[n - WBANKS] for n, use in enumerate(USES) if n >= WBANKS}
assert (NU + 2 * NC) % WBANKS == 0
assert all(USES[-k] == ("t", START + NU - k) for k in range(1, WBANKS + 1))


def adaln_block(nc, x, w_cq, q_scale, w_qn, w_qr, w_ckv, kv_scale, w_kn, w_v, w_kr, w_o,
                wq_gate, s_gate, wq_up, s_up, wq_down, s_down, cond, w_mod,
                ident_in, mask_in, cos_q, sin_q, cos_k, sin_k, out):
    rl_dram = nc.dram_tensor("rl_scratch", [S], F32).ap()
    ot_dram = nc.dram_tensor("ot_scratch", [NH * KVR, S], F32).ap()

    with ExitStack() as whole:
        def alloc(ctx, name, shape, dt):
            return ctx.enter_context(nc.sbuf_tensor(name, shape, dt))

        def sem(name, ctx=whole):
            return ctx.enter_context(nc.semaphore(name))

        ident = alloc(whole, "ident", [P, P], F32)
        identb = alloc(whole, "identb", [P, P], BF16)
        maskb = alloc(whole, "maskb", [P, P], BF16)
        mod = alloc(whole, "mod", [P, 12], F32)
        eps = alloc(whole, "eps", [P, 2], F32)
        kvs = alloc(whole, "kvs", [P, 1], F32)
        b_hi = alloc(whole, "b_hi", [P, NH // 2, D], F32R)
        b_lo = alloc(whole, "b_lo", [P, NH // 2, D], F32R)
        wgi = alloc(whole, "wgi", [P, 2, HT, D], I32)
        wdi = alloc(whole, "wdi", [P, DF, HID], I32)
        sg = alloc(whole, "sg", [P, 2, HT], F32)
        sdn = alloc(whole, "sdn", [P, DF], F32)
        s_ffn = sem("s_ffn")
        SA, CA, GA, SB, CB, GB = (mod[:, 2 * k:2 * k + 2] for k in range(6))

        pv_done = sem("pv_done")
        o_taken = sem("o_taken")
        on_ready = sem("on_ready")

        ot_stored = sem("ot_stored")

        att = ExitStack()
        k_hi = alloc(att, "k_hi", [P, S], F32R)
        k_lo = alloc(att, "k_lo", [P, S], F32R)
        nq_hi = alloc(att, "nq_hi", [P, S], F32R)
        nq_lo = alloc(att, "nq_lo", [P, S], F32R)
        vals = alloc(att, "vals", [P, NT, 2 * KVR], F16)
        wq_hi = alloc(att, "wq_hi", [P, NH + 1, P], F32R)
        wq_lo = alloc(att, "wq_lo", [P, NH + 1, P], F32R)
        lsum = alloc(att, "lsum", [P, NT, 4], F32)
        cosr = alloc(att, "cosr", [P, S], F32)
        sinr = alloc(att, "sinr", [P, S], F32)
        s_rot = sem("s_rot")

        g = dict(locals())
        prepare(nc, g, alloc)
        attend(nc, g, alloc)
        att.close()
        last_layers(nc, g, alloc)


def prepare(nc, g, alloc):
    (x, w_cq, q_scale, w_qn, w_qr, w_ckv, kv_scale, w_kn, w_kr, cond, w_mod, ident_in, mask_in, cos_k, sin_k) = (
        g[k] for k in ("x", "w_cq", "q_scale", "w_qn", "w_qr", "w_ckv", "kv_scale", "w_kn", "w_kr", "cond",
                       "w_mod", "ident_in", "mask_in", "cos_k", "sin_k"))
    ident, identb, maskb, mod, eps, kvs = (g[k] for k in ("ident", "identb", "maskb", "mod", "eps", "kvs"))
    SA, CA = g["SA"], g["CA"]
    k_hi, k_lo, nq_hi, nq_lo, vals = (g[k] for k in ("k_hi", "k_lo", "nq_hi", "nq_lo", "vals"))
    wq_hi, wq_lo, lsum = g["wq_hi"], g["wq_lo"], g["lsum"]

    with ExitStack() as ctx:
        def sb(name, shape, dt=F32):
            return alloc(ctx, name, shape, dt)

        def sem(name):
            return ctx.enter_context(nc.semaphore(name))

        xs = sb("xs", [P, NT, D])
        xn = sb("xn", [P, NT, D])
        st = sb("st", [P, NT, 6])
        mv = sb("mv", [P, NT, 2])
        sd = sb("sd", [P, NT])
        rstd = sb("rstd", [P, NT])
        early = g["wgi"][:, :, :, :].bitcast(F32).rearrange("p a m n -> p (a m n)")
        h32 = early[:, 0:2 * DF * CH].rearrange("p (a f n) -> p a f n", a=2, f=DF)
        wqr = early[:, 2 * DF * CH:].rearrange("p (h i e) -> p h i e", h=NH, e=2)
        wkT = g["wdi"][:, :, :].bitcast(F32).rearrange("p f n -> p (f n)")[:, 0:NH * KVR].rearrange(
            "p (h r) -> p h r", h=NH)
        wvT = wkT
        h_hi = sb("h_hi", [P, 2, DF, CH], F32R)
        h_lo = sb("h_lo", [P, 2, DF, CH], F32R)
        wx = sb("wx", [P, DF, D])
        wkr = sb("wkr", [P, DF, ROPE])
        wx_hi = sb("wx_hi", [P, DF, D], F32R)
        wx_lo = sb("wx_lo", [P, DF, D], F32R)
        z = sb("z", [P, NT, D])
        ss = sb("ss", [P, 2, NT])
        sdz = sb("sdz", [P, 2, NT])
        rz = sb("rz", [P, 2, NT])
        sq, nqn = xs[:, :, 0:P], xs[:, :, P:D]
        kk = sb("kk", [P, NT, P])
        ck = sb("ck", [P, NT, HALF])
        sk = sb("sk", [P, NT, HALF])
        wqn, wqT = (z[:, 8 * k:8 * k + 8, :].rearrange("p t (a n) -> p (t a) n", n=P) for k in range(2))
        wkn = kk[0:KVR, :, :]
        sqk = kk[:, :, 0:KVR]
        wv = g["cosr"][0:KVR, :].rearrange("r (h n) -> r h n", h=NH)
        wo = xn[:, :, :]
        wqa = sb("wqa", [P, NH, P])
        r1 = sb("r1", [P, 4, TPC, HALF])
        qs = sb("qs", [P, 1])
        cs = sb("cs", [P, 2])
        wm = [wqa[:, :, :].rearrange("p h n -> p (h n)")[:, 0:6 * D], sb("wm", [P, 6 * D])[:, :]]
        sc = sb("sc", [P, 2])
        mk32 = sb("mk32", [P, P])
        gt = sb("gt", [P, 2, 4])
        banks = [ctx.enter_context(nc.psum_tensor(f"prep{b}", [P, CH], F32)) for b in range(8)]

        jobs = [("wqT", k) for k in range(4)] + [("wkT", k) for k in range(2)]
        jobs += [("mod", 0)]
        for c in range(2):
            jobs += [("xT", c, f) for f in range(DF)] + [("A", c)]
        for c in range(2, NC):
            jobs += [("z", c - 2, k) for k in range(2)] + [("xT", c, f) for f in range(DF)]
        jobs += [("vT", k) for k in range(2)]
        jobs += [("z", 2, k) for k in range(2)] + [("nT", 0), ("kT", 0)]
        jobs += [("z", 3, k) for k in range(2)]
        jobs += [("B", 0), ("B", 1), ("nT", 1), ("kT", 1), ("B", 2), ("B", 3)]
        jobs += [("nT", 2), ("kT", 2), ("nT", 3), ("kT", 3)]
        index = {j: n for n, j in enumerate(jobs)}

        pe_done = sem("pe_done")
        freed = [sem(f"freed{b}") for b in range(8)]
        dve_chain, pool_steps = sem("dve_chain"), sem("pool_steps")
        s_small, s_wqk, s_wx, s_wm, s_tab = sem("s_small"), sem("s_wqk"), sem("s_wx"), sem("s_wm"), sem("s_tab")
        s_wv, s_wo = sem("s_wv"), sem("s_wo")
        s_x = [sem(f"s_x{c}") for c in range(NC)]
        consts_ready = sem("consts_ready")
        wkn_ready = sem("wkn_ready")
        var_ready = sem("var_ready")
        sd_ready = sem("sd_ready")
        wqa_ready, wq_hi_ready = sem("wqa_ready"), sem("wq_hi_ready")
        sq_ready = sem("sq_ready")
        rot_ready = sem("rot_ready")
        xn_ready = sem("xn_ready")
        silu_ready = sem("silu_ready")
        mod_ready = sem("mod_ready")
        wx_ready = sem("wx_ready")
        h_high = sem("h_high")
        h_split = sem("h_split")
        ss_ready = sem("ss_ready")
        sdz_ready = sem("sdz_ready")
        nk_ready = sem("nk_ready")
        b_hi_ready = sem("b_hi_ready")
        hi_ready = sem("hi_ready")

        def bank(job):
            return banks[index[job] % 8]

        def job_done(eng, job):
            eng.wait_ge(pe_done, index[job] + 1)

        def taken(eng, job):
            eng.wait_ge(freed[index[job] % 8], index[job] // 8 + 1)

        class Order:

            def __init__(self, eng, chain):
                self.eng, self.chain, self.count, self.last = eng, chain, {}, None

            def did(self, ins, signal=None):
                s = signal if signal is not None else self.chain
                self.count[id(s)] = self.count.get(id(s), 0) + 1
                ins.then_inc(s, 1)
                self.last = (s, self.count[id(s)])

            def own(self):
                self.eng.wait_ge(*self.last)

        def free(ins, job):
            ins.then_inc(freed[index[job] % 8], 1)

        block = ctx.enter_context(nc.Block())

        @block.sync
        def _(sp):
            sp.dma_start(ident[:, :], ident_in).then_inc(s_small, 16)
            sp.dma_start(mk32[:, :], mask_in).then_inc(s_small, 16)
            sp.dma_start(qs[:, :], q_scale.rearrange("(p a) -> p a", a=1)).then_inc(s_small, 16)
            for r in (0, KVR):
                sp.dma_start(kvs[r:r + KVR, :], kv_scale.rearrange("(p a) -> p a", a=1)).then_inc(s_small, 16)
            for k in range(2):
                sp.dma_start(cs[:, k:k + 1], cond[0, k * P:(k + 1) * P].rearrange("(p a) -> p a", a=1)).then_inc(s_small, 16)
            for k in range(2):
                sp.dma_start(wm[k], w_mod[k * P:(k + 1) * P, :]).then_inc(s_wm, 16)
            xv = x.rearrange("a (t p) d -> p (a t) d", p=P)
            for c in range(NC):
                sp.dma_start(xs[:, c * TPC:(c + 1) * TPC, :], xv[:, c * TPC:(c + 1) * TPC, :]).then_inc(s_x[c], 16)
            sp.dma_start(g["cosr"][KVR:P, :], g["cos_q"]).then_inc(g["s_rot"], 16)
            sp.dma_start(g["sinr"][KVR:P, :], g["sin_q"]).then_inc(g["s_rot"], 16)
            sp.dma_start(wv[:, :, :], g["w_v"].rearrange("r (h n) -> r h n", h=NH)).then_inc(s_wv, 16)
            job_done(sp, ("xT", NC - 1, DF - 1))
            sp.dma_start(wo[:, :, :], g["w_o"].rearrange("(h n) m -> n h m", h=NH)).then_inc(s_wo, 16)

        @block.gpsimd
        def _(pool):
            pool.dma_start(wkn[:, :, :], w_kn.rearrange("r (h n) -> r h n", h=NH)).then_inc(s_wqk, 16)
            pool.dma_start(wqn[:, :, :], w_qn.rearrange("r (h n) -> r h n", h=NH)).then_inc(s_wqk, 16)
            pool.dma_start(wqr[:, :, :, :], w_qr.rearrange("r (h i e) -> r h i e", h=NH, e=2)).then_inc(s_wqk, 16)
            pool.dma_start(wx[:, :, 0:QR], w_cq.rearrange("(k p) n -> p k n", p=P)).then_inc(s_wx, 16)
            pool.dma_start(wx[:, :, QR:QR + KVR], w_ckv.rearrange("(k p) n -> p k n", p=P)).then_inc(s_wx, 16)
            pool.dma_start(wkr[:, :, :], w_kr.rearrange("(k p) n -> p k n", p=P)).then_inc(s_wx, 16)
            pool.dma_start(ck[:, :, :], cos_k.rearrange("(t p) i -> p t i", p=P)).then_inc(s_tab, 16)
            pool.dma_start(sk[:, :, :], sin_k.rearrange("(t p) i -> p t i", p=P)).then_inc(s_tab, 16)
            for c in range(NC):
                t = slice(c * TPC, (c + 1) * TPC)
                for k in range(2):
                    taken(pool, ("z", c, k))
                pool.tensor_tensor(sq[:, t, :], z[:, t, 0:QR], z[:, t, 0:QR], ALU.mult).then_inc(pool_steps, 1)
                pool.tensor_tensor(sqk[:, t, :], z[:, t, QR:QR + KVR], z[:, t, QR:QR + KVR],
                                   ALU.mult).then_inc(sq_ready, 1)
                if c == 0:
                    pool.wait_ge(s_tab, 32)
                else:
                    pool.wait_ge(pool_steps, 6 * c)
                    pool.wait_ge(rot_ready, c)
                even, odd = z[:, t, QR + KVR:QR + KVR + HALF], z[:, t, QR + KVR + HALF:D]
                for k, (a, b) in enumerate(((even, ck), (odd, sk), (even, sk), (odd, ck))):
                    pool.tensor_tensor(r1[:, k, :, :], a, b[:, t, :], ALU.mult).then_inc(pool_steps, 1)
                pool.wait_ge(pool_steps, 6 * (c + 1) - 1)
                pool.tensor_tensor(kk[:, t, KVR:KVR + HALF], r1[:, 0, :, :], r1[:, 1, :, :],
                                   ALU.subtract).then_inc(pool_steps, 1)
                pool.tensor_tensor(kk[:, t, KVR + HALF:P], r1[:, 2, :, :], r1[:, 3, :, :],
                                   ALU.add).then_inc(rot_ready, 1)

        @block.vector
        def _(dve):
            o = Order(dve, dve_chain)
            did, own = o.did, o.own
            dve.memset(eps[:, 0:1], LN_EPS).then_inc(g["pv_done"], 2)
            dve.memset(eps[:, 1:2], RMS_EPS).then_inc(g["o_taken"], 1)
            dve.memset(lsum[:, :, :], 0.0).then_inc(g["on_ready"], NC)
            did(dve.memset(wq_hi[:, NH:NH + 1, :].bitcast(mybir.dt.uint32), 0))
            did(dve.memset(wq_lo[:, NH:NH + 1, :].bitcast(mybir.dt.uint32), 0))
            dve.wait_ge(s_small, 16 * 7)
            did(dve.tensor_copy(identb[:, :], ident[:, :]))
            did(dve.tensor_copy(maskb[:, :], mk32[:, :]), consts_ready)
            did(dve.tensor_scalar(qs[:, :], qs[:, :], SCORE_SCALE, None, ALU.mult))
            dve.wait_ge(s_wqk, 48)
            did(dve.tensor_scalar(wkn[:, :, :], wkn[:, :, :], kvs[0:KVR, 0:1], None, ALU.mult), wkn_ready)

            def statistics(c):
                dve.wait_ge(s_x[c], 16)
                for t in range(c * TPC, (c + 1) * TPC):
                    did(dve.bn_stats(st[:, t, :], xs[:, t, :]))
                own()
                for t in range(c * TPC, (c + 1) * TPC):
                    did(dve.bn_aggr(mv[:, t, :], st[:, t, :]), var_ready)

            def norm(c):
                dve.wait_ge(sd_ready, c + 1)
                did(dve.reciprocal(rstd[:, c * TPC:(c + 1) * TPC], sd[:, c * TPC:(c + 1) * TPC]))
                own()
                for t in range(c * TPC, (c + 1) * TPC):
                    did(dve.tensor_scalar(xn[:, t, :], xs[:, t, :], mv[:, t, 0:1], rstd[:, t:t + 1],
                                          ALU.subtract, ALU.mult), xn_ready if t % TPC == TPC - 1 else None)

            def input_weights():
                dve.wait_ge(s_wx, 48)
                did(dve.tensor_copy(wx[:, :, QR + KVR:QR + KVR + HALF], wkr[:, :, 0::2]))
                did(dve.tensor_copy(wx[:, :, QR + KVR + HALF:D], wkr[:, :, 1::2]))
                own()
                did(dve.tensor_copy(wx_hi[:, :, :], wx[:, :, :]))
                own()
                did(dve.tensor_tensor(wx_lo[:, :, :], wx[:, :, :], wx_hi[:, :, :].bitcast(F32), ALU.subtract), wx_ready)

            statistics(0)
            statistics(1)
            norm(0)
            statistics(2)
            norm(1)
            input_weights()
            job_done(dve, ("mod", 0))
            free(dve.tensor_copy(mod[:, :], bank(("mod", 0))[:, 0:12]), ("mod", 0))
            taken(dve, ("mod", 0))
            gates = mod[:, :].rearrange("p (s k f) -> p s k f", s=2, k=3)[:, :, 2, :]
            sign, size = gt[:, :, 0:2], gt[:, :, 2:4]
            did(dve.tensor_scalar(sign, gates, 0.0, 2.0, ALU.is_ge, ALU.mult))
            did(dve.tensor_scalar(size, gates, -1.0, None, ALU.mult))
            own()
            did(dve.tensor_scalar(sign, sign, -1.0, None, ALU.add))
            did(dve.tensor_tensor(size, gates, size, ALU.max))
            own()
            did(dve.tensor_scalar(size, size, 0.25, None, ALU.max))
            for base in (2, 8):
                did(dve.tensor_scalar(mod[:, base:base + 2], mod[:, base:base + 2], 1.0, None, ALU.add))
            own()
            did(dve.tensor_tensor(gates, sign, size, ALU.mult), mod_ready)
            statistics(3)
            norm(2)
            norm(3)
            def split(c):
                if c >= 2:
                    job_done(dve, ("z", c - 2, 1))
                for f in range(DF):
                    dve.wait_ge(h_high, 2 * c + f + 1)
                    taken(dve, ("xT", c, f))
                    did(dve.tensor_tensor(h_lo[:, c % 2, f, :], h32[:, c % 2, f, :],
                                          h_hi[:, c % 2, f, :].bitcast(F32), ALU.subtract), h_split)

            def absorbed(k):
                job_done(dve, ("A", k))
                free(dve.tensor_scalar(wqa[:, 8 * k:8 * k + 8, 0:KVR],
                                       bank(("A", k))[:, :].rearrange("p (h j) -> p h j", h=8),
                                       qs[:, 0:1], None, ALU.mult), ("A", k))

            def squares_summed(c):
                t = slice(c * TPC, (c + 1) * TPC)
                dve.wait_ge(sq_ready, c + 1)
                did(dve.tensor_reduce(ss[:, 0, t], sq[:, t, :], AX_X, ALU.add))
                did(dve.tensor_reduce(ss[:, 1, t], sqk[:, t, :], AX_X, ALU.add), ss_ready)

            def latents(c):
                cols = slice(c * TPC, (c + 1) * TPC)
                dve.wait_ge(sdz_ready, 2 * (c + 1))
                did(dve.reciprocal(rz[:, :, cols], sdz[:, :, cols]))
                own()
                for t in range(c * TPC, (c + 1) * TPC):
                    did(dve.tensor_scalar(nqn[:, t, :], z[:, t, 0:QR], rz[:, 0, t:t + 1], None, ALU.mult))
                    did(dve.tensor_scalar(kk[:, t, 0:KVR], z[:, t, QR:QR + KVR], rz[:, 1, t:t + 1], None, ALU.mult),
                        nk_ready if t % TPC == TPC - 1 else None)
                own()
                did(dve.tensor_copy(vals[:, cols, 0:KVR], kk[:, cols, 0:KVR]))
                own()
                did(dve.tensor_tensor(vals[:, cols, KVR:2 * KVR], kk[:, cols, 0:KVR], vals[:, cols, 0:KVR],
                                      ALU.subtract))

            def low_parts(c):
                for k, (kind, hi, lo) in enumerate((("nT", nq_hi, nq_lo), ("kT", k_hi, k_lo))):
                    cols = slice(c * CH, (c + 1) * CH)
                    dve.wait_ge(hi_ready, 2 * c + k + 1)
                    free(dve.tensor_tensor(lo[:, cols], bank((kind, c))[:, :], hi[:, cols].bitcast(F32),
                                           ALU.subtract), (kind, c))

            def values_low(k):
                hi, lo = (g[n][:, 2 * k:2 * k + 2, :].rearrange("p a n -> p (a n)") for n in ("b_hi", "b_lo"))
                dve.wait_ge(b_hi_ready, k + 1)
                free(dve.scalar_tensor_tensor(out=lo, in0=bank(("B", k))[:, :], scalar=kvs[:, 0:1], in1=hi.bitcast(F32),
                                              op0=ALU.mult, op1=ALU.subtract), ("B", k))

            split(0)
            absorbed(0)
            split(1)
            absorbed(1)
            for e in range(2):
                did(dve.tensor_scalar(wqa[:, :, KVR + HALF * e:KVR + HALF * e + HALF], wqr[:, :, :, e],
                                      qs[:, 0:1], None, ALU.mult), wqa_ready)
            dve.wait_ge(wq_hi_ready, 1)
            did(dve.tensor_tensor(wq_lo[:, 0:NH, :], wqa[:, :, :], wq_hi[:, 0:NH, :].bitcast(F32), ALU.subtract))
            split(2)
            squares_summed(0)
            split(3)
            latents(0)
            squares_summed(1)
            latents(1)
            low_parts(0)
            squares_summed(2)
            latents(2)
            values_low(0)
            values_low(1)
            low_parts(1)
            squares_summed(3)
            latents(3)
            values_low(2)
            values_low(3)
            low_parts(2)
            low_parts(3)

        @block.scalar
        def _(act):
            act.wait_ge(s_small, 16 * 7)
            act.activation(sc[:, :], cs[:, :], ACT.Silu).then_inc(silu_ready, 1)
            for k in range(4):
                job_done(act, ("wqT", k))
                free(act.activation(wqT[:, 4 * k:4 * k + 4, :].rearrange("p h n -> p (h n)"),
                                    bank(("wqT", k))[:, :], ACT.Copy), ("wqT", k))
            for k in range(2):
                job_done(act, ("wkT", k))
                free(act.activation(wkT[:, 8 * k:8 * k + 8, :].rearrange("p h n -> p (h n)"),
                                    bank(("wkT", k))[:, :], ACT.Copy), ("wkT", k))
            for c in range(NC):
                cols = slice(c * TPC, (c + 1) * TPC)
                act.wait_ge(var_ready, TPC * (c + 1))
                act.activation(sd[:, cols], mv[:, cols, 1], ACT.Sqrt, bias=eps[:, 0:1]).then_inc(sd_ready, 1)
            act.wait_ge(mod_ready, 1)

            def modulate(c):
                if c >= 2:
                    job_done(act, ("z", c - 2, 1))
                for f in range(DF):
                    job_done(act, ("xT", c, f))
                    if c >= 2:
                        act.wait_ge(h_split, 2 * (c - 2) + f + 1)
                    act.activation(h_hi[:, c % 2, f, :], bank(("xT", c, f))[:, :], ACT.Identity,
                                   bias=SA[:, f:f + 1], scale=CA[:, f:f + 1]).then_inc(h_high, 1)
                    free(act.activation(h32[:, c % 2, f, :], bank(("xT", c, f))[:, :], ACT.Identity,
                                        bias=SA[:, f:f + 1], scale=CA[:, f:f + 1]), ("xT", c, f))

            def take_z(c):
                for k in range(2):
                    job_done(act, ("z", c, k))
                    t = c * TPC + 2 * k
                    free(act.activation(z[:, t:t + 2, :].rearrange("p t n -> p (t n)"), bank(("z", c, k))[:, :],
                                        ACT.Copy), ("z", c, k))

            def latent_deviation(c):
                act.wait_ge(ss_ready, c + 1)
                for k, rank in enumerate((QR, KVR)):
                    cols = slice(c * TPC, (c + 1) * TPC)
                    act.activation(sdz[:, k, cols], ss[:, k, cols], ACT.Sqrt, bias=eps[:, 1:2],
                                   scale=1.0 / rank).then_inc(sdz_ready, 1)

            def high_parts(c):
                for kind, hi in (("nT", nq_hi), ("kT", k_hi)):
                    job_done(act, (kind, c))
                    act.activation(hi[:, c * CH:(c + 1) * CH], bank((kind, c))[:, :], ACT.Copy).then_inc(hi_ready, 1)

            def absorbed_values(k):
                job_done(act, ("B", k))
                act.activation(g["b_hi"][:, 2 * k:2 * k + 2, :].rearrange("p a n -> p (a n)"), bank(("B", k))[:, :],
                               ACT.Copy, scale=kvs[:, 0:1]).then_inc(b_hi_ready, 1)

            modulate(0)
            modulate(1)
            for k in range(2):
                taken(act, ("A", k))
            act.wait_ge(wqa_ready, 2)
            act.activation(wq_hi[:, 0:NH, :], wqa[:, :, :], ACT.Copy).then_inc(wq_hi_ready, 1)
            take_z(0)
            modulate(2)
            take_z(1)
            modulate(3)
            for k in range(2):
                job_done(act, ("vT", k))
                free(act.activation(wvT[:, 8 * k:8 * k + 8, :].rearrange("p h n -> p (h n)"),
                                    bank(("vT", k))[:, :], ACT.Copy), ("vT", k))
            latent_deviation(0)
            take_z(2)
            high_parts(0)
            latent_deviation(1)
            take_z(3)
            absorbed_values(0)
            absorbed_values(1)
            high_parts(1)
            latent_deviation(2)
            absorbed_values(2)
            absorbed_values(3)
            high_parts(2)
            latent_deviation(3)
            high_parts(3)

        @block.tensor
        def _(pe):
            pe.wait_ge(s_small, 16 * 7)
            for n, job in enumerate(jobs):
                kind, b = job[0], bank(job)
                if n >= 8:
                    pe.wait_ge(freed[n % 8], n // 8)
                if kind == "wqT":
                    pe.wait_ge(s_wqk, 48)
                    for k in range(4):
                        last = pe.transpose(b[:, k * P:(k + 1) * P], wqn[:, 4 * job[1] + k, :], ident[:, :])
                elif kind == "wkT":
                    pe.wait_ge(wkn_ready, 1)
                    for k in range(8):
                        last = pe.transpose(b[:, k * KVR:(k + 1) * KVR], wkn[:, 8 * job[1] + k, :], ident[0:KVR, 0:KVR])
                elif kind == "mod":
                    pe.wait_ge(s_wm, 32)
                    pe.wait_ge(silu_ready, 1)
                    for m in range(12):
                        for k in range(2):
                            last = pe.matmul(b[:, m:m + 1], wm[k][:, m * P:(m + 1) * P], sc[:, k:k + 1],
                                             start=(k == 0), stop=(k == 1))
                elif kind == "A":
                    if job[1] == 0:
                        for k in range(2):
                            taken(pe, ("wkT", k))
                        for k in range(4):
                            taken(pe, ("wqT", k))
                    for k in range(8):
                        h = 8 * job[1] + k
                        last = pe.matmul(b[:, k * KVR:(k + 1) * KVR], wqT[:, h, :], wkT[:, h, :], start=True, stop=True)
                elif kind == "vT":
                    pe.wait_ge(s_wv, 16)
                    for k in range(8):
                        last = pe.transpose(b[:, k * KVR:(k + 1) * KVR], wv[:, 8 * job[1] + k, :], ident[0:KVR, 0:KVR])
                elif kind == "B":
                    if job[1] == 0:
                        pe.wait_ge(s_wo, 16)
                        for k in range(2):
                            taken(pe, ("vT", k))
                    for k in range(4):
                        h = 4 * job[1] + k
                        r = (h % 2) * KVR
                        last = pe.matmul(b[r:r + KVR, (k // 2) * D:(k // 2 + 1) * D], wvT[:, h, :], wo[:, h, :],
                                         start=True, stop=True)
                elif kind == "xT":
                    c, f = job[1:]
                    pe.wait_ge(xn_ready, c + 1)
                    for k in range(TPC):
                        last = pe.transpose(b[:, k * P:(k + 1) * P], xn[:, c * TPC + k, f * P:(f + 1) * P], ident[:, :])
                elif kind == "z":
                    c, half = job[1:]
                    pe.wait_ge(h_split, 2 * c + 2)
                    pe.wait_ge(wx_ready, 1)
                    for k in range(2):
                        tok = slice((2 * half + k) * P, (2 * half + k + 1) * P)
                        passes = [(a, w, f) for f in range(DF) for a, w in ((h_hi, wx_hi), (h_hi, wx_lo), (h_lo, wx_hi))]
                        for q, (a, w, f) in enumerate(passes):
                            last = pe.matmul(b[:, k * D:(k + 1) * D], a[:, c % 2, f, tok], w[:, f, :],
                                             start=(q == 0), stop=(q == len(passes) - 1))
                else:
                    c = job[1]
                    pe.wait_ge(nk_ready if kind == "nT" else rot_ready, c + 1)
                    src = nqn if kind == "nT" else kk
                    for k in range(TPC):
                        last = pe.transpose(b[:, k * P:(k + 1) * P], src[:, c * TPC + k, :], ident[:, :])
                last.then_inc(pe_done, 1)


def attend(nc, g, alloc):
    k_hi, k_lo, nq_hi, nq_lo, vals = (g[k] for k in ("k_hi", "k_lo", "nq_hi", "nq_lo", "vals"))
    wq_hi, wq_lo, lsum = g["wq_hi"], g["wq_lo"], g["lsum"]
    ident, identb, maskb = g["ident"], g["identb"], g["maskb"]
    cosr, sinr, s_rot, rl_dram, ot_dram = g["cosr"], g["sinr"], g["s_rot"], g["rl_dram"], g["ot_dram"]
    pv_done, o_taken, on_ready, ot_stored = (g[k] for k in ("pv_done", "o_taken", "on_ready", "ot_stored"))

    with ExitStack() as ctx:
        def sb(name, shape, dt=F32):
            return alloc(ctx, name, shape, dt)

        def sem(name):
            return ctx.enter_context(nc.semaphore(name))

        wh_hi = sb("wh_hi", [P, P], F32R)
        wh_lo = sb("wh_lo", [P, P], F32R)
        q_hi = sb("q_hi", [P, S], F32R)
        q_lo = sb("q_lo", [P, S], F32R)
        y = sb("y", [P, CH])
        yc = sb("yc", [P, CH])
        ys = sb("ys", [P, CH])
        zeros = sb("zeros", [P, CH])
        rb, on = cosr[0:KVR, :], sinr[0:KVR, :]
        oraw = sb("oraw", [KVR, S])
        tmp = sb("tmp", [KVR, CH])
        prob = sb("prob", [P, SBANKS, CH])
        pt = [[sb(f"pt{b}{part}", [P, n, CH], F16) for part in ("hi", "lo")] for b, n in ((0, 12), (1, 16))]
        mx = sb("mx", [P, NT, 4])
        nm = sb("nm", [P, NT])
        l = sb("l", [P, NT])
        rl = sb("rl", [P, 32])
        rlT = sb("rlT", [P, 32])
        sbank = [ctx.enter_context(nc.psum_tensor(f"scores{b}", [P, CH], F32)) for b in range(SBANKS)]
        wbank = [ctx.enter_context(nc.psum_tensor(f"work{b}", [P, CH], F32)) for b in range(WBANKS)]

        wh_ready = sem("wh_ready")
        qp_done = sem("qp_done")
        q_taken = sem("q_taken")
        q_ready = sem("q_ready")
        pool_chain, dve_chain = sem("pool_chain"), sem("dve_chain2")
        scored = sem("scored")
        unit_max = sem("unit_max")
        max_ready = sem("max_ready")
        exp_done = sem("exp_done")
        turned = sem("turned")
        hi_ready = sem("pthi_ready")
        lo_ready = sem("ptlo_ready")
        tmp_ready = sem("tmp_ready")
        l_chain = sem("l_chain")
        rl_ready = sem("rl_ready")
        rl_stored = sem("rl_stored")
        rb_loaded = sem("rb_loaded")

        def after(h, per_head, k):
            return h * per_head + k

        def transposed(v, part):
            i, n = TILE_OF[v % NU], width(v) // P
            j0, r = (v % NU - FIRST[i]) * TPC, i % TPC
            return pt[(i // TPC) % 2][part][:, j0:j0 + n, r * P:(r + 1) * P]

        def turned_bank(v):
            return wbank[BANK[("t", v)]][:, 0:width(v)].rearrange("p (j q) -> p j q", q=P)

        parked = [pt[0][part][:, TPC:12, :].rearrange("p (k e) n -> p k (e n)", e=2).bitcast(F32)
                  for part in range(2)]
        first_y = [y] + [parked[0][:, k, :] for k in range(3)]

        def parts(eng, chain, c, taken, base, y=y, yc=yc, ys=ys, before=None):
            cols = slice(c * CH, (c + 1) * CH)
            rot, e, o = slice(KVR, P), slice(KVR, KVR + HALF), slice(KVR + HALF, P)
            eng.wait_ge(q_taken, taken)
            eng.tensor_tensor(yc[rot, :], y[rot, :], cosr[rot, cols], ALU.mult).then_inc(chain, 1)
            eng.wait_ge(chain, base + 1)
            eng.tensor_tensor(ys[e, :], y[o, :], sinr[o, cols], ALU.mult).then_inc(chain, 1)
            eng.wait_ge(chain, base + 2)
            eng.tensor_tensor(ys[o, :], y[e, :], sinr[e, cols], ALU.mult).then_inc(chain, 1)
            eng.wait_ge(chain, base + 3)
            eng.tensor_tensor(y[rot, :], yc[rot, :], ys[rot, :], ALU.add).then_inc(chain, 1)
            eng.wait_ge(chain, base + 4)
            eng.tensor_tensor(q_hi[:, cols], y[:, :], zeros[:, :], ALU.add).then_inc(chain, 1)
            eng.wait_ge(chain, base + 5)
            if before is not None:
                eng.wait_ge(q_ready, before)
            eng.tensor_tensor(q_lo[:, cols], y[:, :], q_hi[:, cols].bitcast(F32), ALU.subtract).then_inc(q_ready, 1)

        def outputs(c):
            return wbank[BANK[("o", c)]]

        ident_in = g["ident_in"]
        wgi, wdi, sg, sdn, s_ffn = (g[k] for k in ("wgi", "wdi", "sg", "sdn", "s_ffn"))
        block = ctx.enter_context(nc.Block())

        @block.tensor
        def _(pe):
            def bank_free(h, use, last=False):
                kind, n = BEFORE[use]
                if last and (kind == "q" or kind == "t" and n >= NU):
                    return
                if kind == "t":
                    pe.wait_ge(lo_ready, after(h, NU, n + 1))
                elif kind == "q":
                    pe.wait_ge(q_taken, after(h, NC, NC + n + 1))
                else:
                    pe.wait_ge(o_taken, after(h, NC, 1 + n + 1))

            def project(b, c, wh_hi=wh_hi, wh_lo=wh_lo):
                cols = slice(c * CH, (c + 1) * CH)
                pe.matmul(b[:, :], wh_hi[:, :], nq_hi[:, cols], start=True, stop=False)
                pe.matmul(b[:, :], wh_hi[:, :], nq_lo[:, cols], start=False, stop=False)
                pe.matmul(b[:, :], wh_lo[:, :], nq_hi[:, cols], start=False, stop=True).then_inc(qp_done, 1)

            def score(h, v):
                u, n = v % NU, width(v)
                i = TILE_OF[u]
                if starts_chunk(v):
                    pe.wait_ge(q_ready, after(h, NC, chunk_of(v) + 1))
                if v >= SBANKS:
                    pe.wait_ge(exp_done, after(h, NU, v - SBANKS + 1))
                b, k0 = sbank[u % SBANKS], (u - FIRST[i]) * CH
                q, k = slice(i * P, (i + 1) * P), slice(k0, k0 + n)
                pe.matmul(b[:, 0:n], q_hi[:, q], k_hi[:, k], start=True, stop=False)
                pe.matmul(b[:, 0:n], q_hi[:, q], k_lo[:, k], start=False, stop=False)
                if u == FIRST[i] + UNITS[i] - 1:
                    pe.matmul(b[:, n - P:n], identb[:, :], maskb[:, :], start=False, stop=False)
                pe.matmul(b[:, 0:n], q_lo[:, q], k_hi[:, k], start=False, stop=True).then_inc(scored, 1)

            def values(h, c, at_end=False):
                last = FIRST[TPC * c + 3] + UNITS[TPC * c + 3] - 1
                pe.wait_ge(lo_ready, after(h, NU, last + 1))
                bank_free(h, ("o", c), at_end)
                for j in range(TPC * (c + 1)):
                    q0 = max(0, j - TPC * c) * P
                    for part in range(2):
                        ins = pe.matmul(outputs(c)[:, q0:CH], vals[:, j, :], pt[c % 2][part][:, j, q0:CH],
                                        start=(j == 0 and part == 0), stop=(j == TPC * c + TPC - 1 and part == 1))
                ins.then_inc(pv_done, 1)

            def step(h, v, last=False):
                if v >= START and v in PV_BEFORE:
                    values(h, PV_BEFORE[v], last)
                if last and v >= NU:
                    return
                pe.wait_ge(exp_done, after(h, NU, v + 1))
                bank_free(h, ("t", v), last)
                for k in range(width(v) // P):
                    ins = pe.transpose(wbank[BANK[("t", v)]][:, k * P:(k + 1) * P],
                                       prob[:, v % SBANKS, k * P:(k + 1) * P], ident[:, :])
                ins.then_inc(turned, 1)
                for n in ahead(LEAD_S, v, last):
                    score(h, n)
                if v >= START and v in QP_AFTER and not last:
                    c = QP_AFTER[v]
                    if c == 0:
                        pe.wait_ge(wh_ready, after(h, 1, 1))
                    bank_free(h, ("q", c))
                    project(wbank[BANK[("q", c)]], c)

            for c in range(NC):
                if c >= WBANKS:
                    pe.wait_ge(q_taken, c - WBANKS + 1)
                project(wbank[c % WBANKS], c, wq_hi[:, 0, :], wq_lo[:, 0, :])
            for v in range(reached(LEAD_S, -1) + 1):
                score(0, v)
            for v in range(START):
                step(0, v)
            with pe.Fori(0, NH - 1) as h:
                for v in range(START, START + NU):
                    step(h, v)
            for v in range(START, START + NU):
                step(NH - 1, v, last=True)

        @block.vector
        def _(dve):
            def maximum(h, v):
                i, n = TILE_OF[v % NU], width(v)
                k, b = v % NU - FIRST[i], sbank[v % SBANKS][:, 0:n]
                dve.wait_ge(scored, after(h, NU, v + 1))
                if UNITS[i] == 1:
                    dve.tensor_reduce(nm[:, i:i + 1], b, AX_X, ALU.max, negate=True).then_inc(max_ready, 1)
                    return
                dve.tensor_reduce(mx[:, i, k:k + 1], b, AX_X, ALU.max).then_inc(unit_max, 1)
                if k == UNITS[i] - 1:
                    dve.wait_ge(unit_max, after(h, MULTI, multi_before(v)))
                    dve.tensor_reduce(nm[:, i:i + 1], mx[:, i, 0:UNITS[i]], AX_X, ALU.max,
                                      negate=True).then_inc(max_ready, 1)

            def low_parts(h, v):
                dve.wait_ge(hi_ready, after(h, NU, v + 1))
                dve.scalar_tensor_tensor(out=transposed(v, 1), in0=turned_bank(v), scalar=PSCALE,
                                         in1=transposed(v, 0), op0=ALU.mult, op1=ALU.subtract).then_inc(lo_ready, 1)

            def take_outputs(h, c):
                dve.wait_ge(on_ready, after(h, NC, c + 1))
                dve.wait_ge(tmp_ready, after(h, NC, c + 1))
                dve.scalar_tensor_tensor(out=oraw[:, c * CH:(c + 1) * CH], in0=outputs(c)[0:KVR, :], scalar=1.0 / PSCALE,
                                         in1=tmp[:, :], op0=ALU.mult, op1=ALU.add).then_inc(o_taken, 1)

            def step(h, v, last=False):
                if v == SUMS_EARLY:
                    dve.wait_ge(exp_done, after(h, NU, FIRST[12]))
                    dve.tensor_reduce(l[:, 0:12], lsum[:, 0:12, :], AX_X, ALU.add).then_inc(l_chain, 1)
                maxima_last = place(v)[1] in MAXIMA_LAST.get(place(v)[0], [])
                if maxima_last and not (last and v >= NU):
                    low_parts(h, v)
                for n in ahead(LEAD_M, v, last):
                    maximum(h, n)
                if not maxima_last and not (last and v >= NU):
                    low_parts(h, v)
                if v == SUMS_LATE:
                    dve.wait_ge(exp_done, after(h, NU, NU))
                    dve.tensor_reduce(l[:, 12:NT], lsum[:, 12:NT, :], AX_X, ALU.add).then_inc(l_chain, 1)
                    dve.wait_ge(l_chain, after(h, 3, 3))
                    dve.reciprocal(rl[:, 0:NT], l[:, :]).then_inc(l_chain, 1)
                    dve.wait_ge(l_chain, after(h, 3, 4))
                    dve.wait_ge(ot_stored, after(h, 16, 16))
                    dve.transpose(rlT[:, :], rl[:, :]).then_inc(rl_ready, 1)
                if v >= START and v in PV_BEFORE:
                    take_outputs(h, PV_BEFORE[v])

            dve.memset(rl[:, :], 0.0).then_inc(l_chain, 1)
            dve.wait_ge(s_rot, 32)
            dve.wait_ge(pool_chain, 1)
            for c in range(DVE_CHUNKS):
                parts(dve, dve_chain, c, c + 1, 5 * c, first_y[c])
            for v in range(reached(LEAD_M, -1) + 1):
                maximum(0, v)
            for v in range(START):
                step(0, v)
            with dve.Fori(0, NH - 1) as h:
                for v in range(START, START + NU):
                    step(h, v)
            for v in range(START, START + NU):
                step(NH - 1, v, last=True)
            dve.wait_ge(rb_loaded, 16 * NH)
            for c in range(NC - 2, NC):
                cols = slice(c * CH, (c + 1) * CH)
                dve.wait_ge(o_taken, NC * (NH - 1) + 1 + c + 1)
                dve.tensor_tensor(on[:, cols], oraw[:, cols], rb[:, cols], ALU.mult).then_inc(on_ready, 1)

        @block.scalar
        def _(act):
            def exponentials(h, v):
                i, n = TILE_OF[v % NU], width(v)
                k = v % NU - FIRST[i]
                if k == 0:
                    act.wait_ge(max_ready, after(h, NT, i + 1 + NT * (v // NU)))
                act.activation(prob[:, v % SBANKS, 0:n], sbank[v % SBANKS][:, 0:n], ACT.Exp, bias=nm[:, i:i + 1],
                               accum_out=lsum[:, i, k:k + 1]).then_inc(exp_done, 1)

            def low_rows(h, c):
                act.wait_ge(pv_done, after(h, NC, 2 + c + 1))
                act.wait_ge(o_taken, after(h, NC, 1 + c))
                act.activation(tmp[:, :], outputs(c)[KVR:P, :], ACT.Copy, scale=1.0 / PSCALE).then_inc(tmp_ready, 1)

            def high_parts(h, v):
                act.wait_ge(turned, after(h, NU, v + 1))
                if starts_chunk(v):
                    act.wait_ge(pv_done, after(h, NC, chunk_of(v) + 1))
                act.activation(transposed(v, 0), turned_bank(v), ACT.Copy, scale=PSCALE).then_inc(hi_ready, 1)

            def step(h, v, last=False):
                if v < NU or not last:
                    high_parts(h, v)
                if v >= START and v in QP_AFTER and not last:
                    c = QP_AFTER[v]
                    act.wait_ge(qp_done, after(h, NC, NC + c + 1))
                    act.wait_ge(q_ready, after(h, NC, NC + c))
                    act.activation(y[:, :], wbank[BANK[("q", c)]][:, :], ACT.Copy).then_inc(q_taken, 1)
                if v >= START and v in PV_BEFORE:
                    low_rows(h, PV_BEFORE[v])
                for n in ahead(LEAD_E, v, last):
                    exponentials(h, n)

            for c in range(NC):
                act.wait_ge(qp_done, c + 1)
                act.activation(first_y[c][:, :], wbank[c % WBANKS][:, :], ACT.Copy).then_inc(q_taken, 1)
            for v in range(reached(LEAD_E, -1) + 1):
                exponentials(0, v)
            for v in range(START):
                step(0, v)
            with act.Fori(0, NH - 1) as h:
                for v in range(START, START + NU):
                    step(h, v)
            for v in range(START, START + NU):
                step(NH - 1, v, last=True)

        @block.gpsimd
        def _(pool):
            def load_weights(h):
                pool.tensor_copy(wh_hi[:, :], wq_hi[:, h, :]).then_inc(pool_chain, 1)
                pool.tensor_copy(wh_lo[:, :], wq_lo[:, h, :]).then_inc(wh_ready, 1)

            chain = 5 * NC + 1
            pool.memset(zeros[:, :], 0.0).then_inc(pool_chain, 1)
            pool.wait_ge(s_rot, 32)
            for c in range(DVE_CHUNKS, NC):
                if c == DVE_CHUNKS:
                    pool.wait_ge(pool_chain, 1)
                else:
                    pool.wait_ge(q_ready, c)
                parts(pool, pool_chain, c, c + 1, 1 + 5 * (c - DVE_CHUNKS), first_y[c],
                      parked[1][:, 0, :], parked[1][:, 1, :], c)
            load_weights(1)
            def norm_outputs(h, chunks):
                pool.wait_ge(rb_loaded, after(h, 16, 16))
                for c in chunks:
                    cols = slice(c * CH, (c + 1) * CH)
                    pool.wait_ge(o_taken, after(h, NC, 1 + c + 1))
                    pool.tensor_tensor(on[:, cols], oraw[:, cols], rb[:, cols], ALU.mult).then_inc(on_ready, 1)

            with pool.Fori(0, NH - 1) as h:
                for c in range(NC):
                    parts(pool, pool_chain, c, after(h, NC, NC + c + 1),
                          after(h, chain, 2 + 5 * (NC - DVE_CHUNKS) + 5 * c))
                load_weights(h + 2)
                norm_outputs(h, range(NC))
            norm_outputs(NH - 1, range(NC - 2))

        @block.sync
        def _(sp):
            sp.dma_start(rlT[:, :], ident_in[:, 0:32]).then_inc(ot_stored, 16)
            full = HID // P
            for a, (wq, s) in enumerate(((g["wq_gate"], g["s_gate"]), (g["wq_up"], g["s_up"]))):
                sp.dma_start(wgi[:, a, 0:full, :], wq[0:full * P, :].rearrange("(m p) d -> p m d", p=P)).then_inc(s_ffn, 16)
                sp.dma_start(wgi[0:HID - full * P, a, full, :], wq[full * P:HID, :]).then_inc(s_ffn, 16)
                for m in range(HT):
                    rows = min(P, HID - m * P)
                    sp.dma_start(sg[0:rows, a, m:m + 1], s[m * P:m * P + rows].rearrange("(p a) -> p a", a=1)).then_inc(s_ffn, 16)
            sp.dma_start(wdi[:, :, :], g["wq_down"].rearrange("(f p) n -> p f n", p=P)).then_inc(s_ffn, 16)
            for f in range(DF):
                sp.dma_start(sdn[:, f:f + 1], g["s_down"][f * P:(f + 1) * P].rearrange("(p a) -> p a", a=1)).then_inc(s_ffn, 16)
            with sp.Fori(0, NH) as h:
                row = sp.snap(h * KVR)
                sp.wait_ge(rl_ready, after(h, 1, 1))
                for a in range(4):
                    sp.dma_start(rl_dram.rearrange("(t p) -> t p", p=P)[:, 32 * a:32 * a + 32],
                                 rlT[32 * a:32 * a + NT, :]).then_inc(rl_stored, 16)
                sp.wait_ge(rl_stored, after(h, 64, 64))
                sp.wait_ge(ot_stored, after(h, 16, 16))
                sp.dma_start(rb, rl_dram.rearrange("(a s) -> a s", a=1).to_broadcast([KVR, S])).then_inc(rb_loaded, 16)
                sp.wait_ge(on_ready, after(h, NC, 2 * NC))
                sp.dma_start(ot_dram[bass.ds(row, KVR), :], on).then_inc(ot_stored, 16)


def last_layers(nc, g, alloc):
    x, out, ot_dram, ident, eps, ot_stored = (g[k] for k in ("x", "out", "ot_dram", "ident", "eps", "ot_stored"))
    GA, SB, CB, GB = g["GA"], g["SB"], g["CB"], g["GB"]
    b_hi, b_lo, wgi, wdi, sg, sdn, s_ffn = (g[k] for k in ("b_hi", "b_lo", "wgi", "wdi", "sg", "sdn", "s_ffn"))
    NP = NH // 2
    full = HID // P
    rest = HID - full * P

    jobs = [("gu", a, f, k) for a in range(2) for f in range(DF) for k in range(2)] + [("dn", k) for k in range(3)]

    events = []
    for c in range(NC):
        for m in range(HT):
            events.append(("GU", c, m))
            if m == 1 and c:
                events.append(("O", c - 1))
            if m == 2 and c + 1 < NC:
                events.append(("X", c + 1))
            if m == 3 and c + 1 < NC:
                events.append(("T", c + 1))
            if m or c:
                events.append(("DN", c, m - 1) if m else ("DN", c - 1, HT - 1))
    events += [("DN", NC - 1, HT - 1), ("O", NC - 1)]

    with ExitStack() as ctx:
        def sb(name, shape, dt=F32):
            return alloc(ctx, name, shape, dt)

        def sem(name):
            return ctx.enter_context(nc.semaphore(name))

        xs = sb("x1", [P, NT, D])
        st, mv, sd, rstd = sb("st2", [P, NT, 6]), sb("mv2", [P, NT, 2]), sb("sd2", [P, NT]), sb("rstd2", [P, NT])
        dn_hi = sb("dn_hi", [P, HT, D], F32R)
        dn_lo = sb("dn_lo", [P, HT, D], F32R)
        gu_hi = sb("gu_hi", [P, 2, DF, HIDP], F32R)
        gu_lo = sb("gu_lo", [P, 2, DF, HIDP], F32R)
        h_hi, h_lo = sb("h2_hi", [P, 2, DF, CH], F32R), sb("h2_lo", [P, 2, DF, CH], F32R)
        xn = sb("xn2", [P, TPC, D])
        h32 = sb("h2", [P, DF, CH])
        half = ExitStack()
        ot = alloc(half, "ot", [P, 2, NP, CH], F32)
        o_hi = alloc(half, "o_hi", [P, NP, CH], F32R)
        o_lo = alloc(half, "o_lo", [P, NP, CH], F32R)
        yT = alloc(half, "yT", [P, 2, DF, CH], F32)
        wg = alloc(half, "wg", [P, 2, HT, D], F32)
        wd = alloc(half, "wd", [P, DF, HIDP], F32)
        banks = [ctx.enter_context(nc.psum_tensor(f"ll{b}", [P, CH], F32)) for b in range(8)]
        dest = [[x[:, a, f, k * CH:min(k * CH + CH, HIDP)] for x in (gu_hi, gu_lo)] for _, a, f, k in jobs[:-3]]
        dest += [[x[:, 2 * k:2 * k + 2, :].rearrange("p a n -> p (a n)") for x in (dn_hi, dn_lo)] for k in range(3)]

        PARTS = 4
        PER = NP // PARTS
        s_ot = [[sem(f"s_ot{c}_{k}") for k in range(PARTS)] for c in range(NC)]
        s_x = sem("s_x1")
        JOB_LEAD = 4
        JOB_BEHIND = {1 + 2 * k: k for k in range(len(jobs))}
        hi_done, o_split, pair_used = sem("o_hi_done"), sem("o_split"), sem("pair_used")
        y_ready, y_turned, x1_ready = sem("y_ready"), sem("y_turned"), sem("x1_ready")
        st_ready, mv_ready, sd2_ready = sem("st_ready"), sem("mv_ready"), sem("sd2_ready")
        rstd_ready = sem("rstd_ready")
        xn_ready, t_done, t_taken, h_hi_done, h_split = (sem(n) for n in ("x2n", "x2t", "x2taken", "h2hi", "h2split"))
        zeroed, w_ready = sem("zeroed"), sem("w_ready")
        w_turned, w_hi, w_taken = sem("w_turned"), sem("w_hi"), sem("w_taken")

        def residual(dve, c):
            for f in range(DF):
                dve.wait_ge(y_turned, 2 * c + f + 1)
                cols = xs[:, TPC * c:TPC * (c + 1), f * P:(f + 1) * P]
                dve.tensor_tensor(cols, banks[4 + f][:, :].rearrange("p (t n) -> p t n", n=P), cols,
                                  ALU.add).then_inc(x1_ready, 1)

        def statistics(dve, c):
            dve.wait_ge(x1_ready, 2 * (c + 1))
            for t in range(TPC * c, TPC * (c + 1)):
                dve.bn_stats(st[:, t, :], xs[:, t, :]).then_inc(st_ready, 1)
            dve.wait_ge(st_ready, TPC * (c + 1))
            for t in range(TPC * c, TPC * (c + 1)):
                dve.bn_aggr(mv[:, t, :], st[:, t, :]).then_inc(mv_ready, 1)

        def deviation(act, c):
            cols = slice(TPC * c, TPC * (c + 1))
            act.wait_ge(mv_ready, TPC * (c + 1))
            act.activation(sd[:, cols], mv[:, cols, 1], ACT.Sqrt, bias=eps[:, 0:1]).then_inc(sd2_ready, 1)

        def norm(dve, c):
            cols = slice(TPC * c, TPC * (c + 1))
            dve.wait_ge(sd2_ready, c + 1)
            dve.reciprocal(rstd[:, cols], sd[:, cols]).then_inc(rstd_ready, 1)
            dve.wait_ge(rstd_ready, c + 1)
            if c:
                dve.wait_ge(t_done, 2 * c)
            for k in range(TPC):
                t = TPC * c + k
                dve.tensor_scalar(xn[:, k, :], xs[:, t, :], mv[:, t, 0:1], rstd[:, t:t + 1],
                                  ALU.subtract, ALU.mult).then_inc(xn_ready, 1)

        def norm_bank(c, f):
            return banks[(4 if c else 6) + f]

        def turn_norm(pe, c):
            pe.wait_ge(xn_ready, TPC * (c + 1))
            for f in range(DF):
                for k in range(TPC):
                    last = pe.transpose(norm_bank(c, f)[:, k * P:(k + 1) * P], xn[:, k, f * P:(f + 1) * P], ident[:, :])
                last.then_inc(t_done, 1)

        def modulate(act, c):
            for f in range(DF):
                act.wait_ge(t_done, 2 * c + f + 1)
                if c:
                    act.wait_ge(h_split, 2 * (c - 1) + f + 1)
                act.activation(h32[:, f, :], norm_bank(c, f)[:, :], ACT.Identity, bias=SB[:, f:f + 1],
                               scale=CB[:, f:f + 1]).then_inc(t_taken, 1)

        def split(dve, c):
            for f in range(DF):
                dve.wait_ge(t_taken, 2 * c + f + 1)
                dve.tensor_copy(h_hi[:, c % 2, f, :], h32[:, f, :]).then_inc(h_hi_done, 1)
                dve.wait_ge(h_hi_done, 2 * c + f + 1)
                dve.tensor_tensor(h_lo[:, c % 2, f, :], h32[:, f, :], h_hi[:, c % 2, f, :].bitcast(F32),
                                  ALU.subtract).then_inc(h_split, 1)

        with nc.Block() as block:
            @block.sync
            def _(sp):
                src = ot_dram.rearrange("(a p) s -> p a s", p=P)
                for c in range(NC):
                    for k in range(PARTS):
                        if c >= 2:
                            sp.wait_ge(o_split, NP * (c - 2) + PER * (k + 1))
                        if c == 0:
                            sp.wait_ge(ot_stored, 16 * (2 * PER * (k + 1) + 1))
                        sp.dma_start(ot[:, c % 2, PER * k:PER * (k + 1), :],
                                     src[:, PER * k:PER * (k + 1), c * CH:(c + 1) * CH]).then_inc(s_ot[c][k], 16)
                    if c == 0:
                        sp.dma_start(xs[:, :, :], x.rearrange("a (t p) d -> p (a t) d", p=P)).then_inc(s_x, 16)

            @block.scalar
            def _(act):
                def turned_outputs(c):
                    if c >= 2:
                        act.wait_ge(y_turned, 2 * (c - 1))
                    for f in range(DF):
                        act.activation(yT[:, c % 2, f, :], banks[2 * (c % 2) + f][:, :], ACT.Copy,
                                       scale=GA[:, f:f + 1]).then_inc(y_ready, 1)

                for c in range(NC):
                    for a in range(NP):
                        n = NP * c + a
                        if a % PER == 0:
                            act.wait_ge(s_ot[c][a // PER], 16)
                        if c:
                            act.wait_ge(pair_used, NP * (c - 1) + a + 1)
                        act.activation(o_hi[:, a, :], ot[:, c % 2, a, :], ACT.Copy).then_inc(hi_done, 1)
                        if n in JOB_BEHIND:
                            k = JOB_BEHIND[n]
                            act.wait_ge(w_turned, k + 1)
                            hi = dest[k][0]
                            act.activation(hi, banks[6 + k % 2][:, 0:hi.shape[-1]], ACT.Copy).then_inc(w_hi, 1)
                        if a == 3 and c:
                            act.wait_ge(pair_used, NP * c)
                            turned_outputs(c - 1)
                        if c >= 2 and a == 1:
                            deviation(act, c - 2)
                modulate(act, 0)
                act.wait_ge(pair_used, NP * NC)
                turned_outputs(NC - 1)

            @block.vector
            def _(dve):
                dve.memset(wg[:, :, full, :], 0.0).then_inc(zeroed, 1)
                dve.memset(wd[:, :, HID:HIDP], 0.0).then_inc(zeroed, 1)
                dve.wait_ge(s_ffn, 16 * (2 * (2 + HT) + 1 + DF))
                dve.wait_ge(zeroed, 2)

                for a in range(2):
                    for m in range(HT):
                        rows = P if m < full else rest
                        dve.tensor_scalar(wg[0:rows, a, m, :], wgi[0:rows, a, m, :], ZERO_POINT, sg[0:rows, a, m:m + 1],
                                          ALU.subtract, ALU.mult).then_inc(w_ready, 1)
                for f in range(DF):
                    dve.tensor_scalar(wd[:, f, 0:HID], wdi[:, f, :], ZERO_POINT, sdn[:, f:f + 1],
                                      ALU.subtract, ALU.mult).then_inc(w_ready, 1)
                for c in range(NC):
                    for a in range(NP):
                        n = NP * c + a
                        dve.wait_ge(hi_done, n + 1)
                        dve.tensor_tensor(o_lo[:, a, :], ot[:, c % 2, a, :], o_hi[:, a, :].bitcast(F32),
                                          ALU.subtract).then_inc(o_split, 1)
                        if n in JOB_BEHIND:
                            k = JOB_BEHIND[n]
                            dve.wait_ge(w_hi, k + 1)
                            hi, lo = dest[k]
                            dve.tensor_tensor(lo, banks[6 + k % 2][:, 0:hi.shape[-1]], hi.bitcast(F32),
                                              ALU.subtract).then_inc(w_taken, 1)
                        if c and a == 7:
                            if c == 1:
                                dve.wait_ge(s_x, 16)
                            residual(dve, c - 1)
                            if c < NC - 1:
                                statistics(dve, c - 1)
                        if n == NP * (NC - 1) + 1:
                            norm(dve, 0)
                split(dve, 0)

            @block.tensor
            def _(pe):
                def turn(c):
                    for f in range(DF):
                        pe.wait_ge(y_ready, 2 * c + f + 1)
                        if c:
                            pe.wait_ge(x1_ready, 2 * (c - 1) + f + 1)
                        for k in range(TPC):
                            last = pe.transpose(banks[4 + f][:, k * P:(k + 1) * P],
                                                yT[:, c % 2, f, k * P:(k + 1) * P], ident[:, :])
                        last.then_inc(y_turned, 1)

                def turn_weights(k):
                    pe.wait_ge(w_ready, HT * (jobs[k][1] + 1) if jobs[k][0] == "gu" else 2 * HT + DF)
                    if k >= 2:
                        pe.wait_ge(w_taken, k - 1)
                    b, job = banks[6 + k % 2], jobs[k]
                    if job[0] == "gu":
                        _, a, f, part = job
                        for m in range(4 * part, min(4 * part + 4, HT)):
                            last = pe.transpose(b[:, (m - 4 * part) * P:(m - 4 * part + 1) * P],
                                                wg[:, a, m, f * P:(f + 1) * P], ident[:, :])
                    else:
                        for q in range(4):
                            m, f = 2 * job[1] + q // 2, q % 2
                            last = pe.transpose(b[:, q * P:(q + 1) * P], wd[:, f, m * P:(m + 1) * P], ident[:, :])
                    last.then_inc(w_turned, 1)

                for n in range(JOB_LEAD):
                    if n in JOB_BEHIND:
                        turn_weights(JOB_BEHIND[n])
                for c in range(NC):
                    if c >= 2:
                        pe.wait_ge(y_ready, 2 * (c - 1))
                    for a in range(NP):
                        if NP * c + a + JOB_LEAD in JOB_BEHIND:
                            turn_weights(JOB_BEHIND[NP * c + a + JOB_LEAD])
                        pe.wait_ge(o_split, NP * c + a + 1)
                        for q, (w, o) in enumerate(((b_hi, o_hi), (b_hi, o_lo), (b_lo, o_hi))):
                            for f in range(DF):
                                last = pe.matmul(banks[2 * (c % 2) + f][:, :], w[:, a, f * P:(f + 1) * P], o[:, a, :],
                                                 start=(a == 0 and q == 0), stop=(a == NP - 1 and q == 2))
                        last.then_inc(pair_used, 1)
                        if c and a == 4:
                            turn(c - 1)
                        if c == NC - 1 and a == 5:
                            pe.wait_ge(w_taken, len(jobs))
                            turn_norm(pe, 0)
                turn(NC - 1)
        half.close()

        sl = sb("sl", [P, 2, CH])
        a32 = sb("a32", [P, 2, CH])
        a_hi, a_lo = sb("a_hi", [P, 2, CH], F32R), sb("a_lo", [P, 2, CH], F32R)
        fT = sb("fT", [P, DF, CH])
        res = sb("res", [P, 2, TPC, D])

        gu_done, silu_done, prod_done, a_hi_done, a_split = (sem(n) for n in ("gud", "silud", "prodd", "ahid", "asplit"))
        dn_done, f_taken, o_turned, o_added = (sem(n) for n in ("dnd", "ftaken", "oturned", "oadded"))
        stored = [sem(f"stored{c}") for c in range(NC)]

        with nc.Block() as block:
            @block.sync
            def _(sp):
                for c in range(NC):
                    sp.wait_ge(o_added, 2 * (c + 1))
                    sp.dma_start(out[0, c * CH:(c + 1) * CH, :].rearrange("(t p) d -> p t d", p=P),
                                 res[:, c % 2, :, :]).then_inc(stored[c], 16)
                for c in range(NC):
                    sp.wait_ge(stored[c], 16)

            @block.vector
            def _(dve):
                statistics(dve, NC - 2)
                residual(dve, NC - 1)
                for e in events:
                    kind, c = e[0], e[1]
                    if e == ("GU", 0, 1):
                        statistics(dve, NC - 1)
                    if kind == "X":
                        norm(dve, c)
                    elif kind == "T":
                        if c >= 2:
                            dve.wait_ge(gu_done, HT * (c - 1))
                        split(dve, c)
                    elif kind == "GU":
                        n = HT * c + e[2]
                        dve.wait_ge(silu_done, n + 1)
                        if n >= 2:
                            dve.wait_ge(a_split, n - 1)
                        dve.tensor_tensor(a32[:, n % 2, :], banks[2 * (n % 2) + 1][:, :], sl[:, n % 2, :],
                                          ALU.mult).then_inc(prod_done, 1)
                        if n >= 2:
                            dve.wait_ge(dn_done, n - 1)
                        dve.wait_ge(prod_done, n + 1)
                        dve.tensor_copy(a_hi[:, n % 2, :], a32[:, n % 2, :]).then_inc(a_hi_done, 1)
                        dve.wait_ge(a_hi_done, n + 1)
                        dve.tensor_tensor(a_lo[:, n % 2, :], a32[:, n % 2, :], a_hi[:, n % 2, :].bitcast(F32),
                                          ALU.subtract).then_inc(a_split, 1)
                    elif kind == "O":
                        if c >= 2:
                            dve.wait_ge(stored[c - 2], 16)
                        for f in range(DF):
                            dve.wait_ge(o_turned, 2 * c + f + 1)
                            cols = slice(f * P, (f + 1) * P)
                            dve.tensor_tensor(res[:, c % 2, :, cols],
                                              banks[4 + f][:, :].rearrange("p (t n) -> p t n", n=P),
                                              xs[:, TPC * c:TPC * (c + 1), cols], ALU.add).then_inc(o_added, 1)

            @block.scalar
            def _(act):
                for e in events:
                    kind, c = e[0], e[1]
                    if e == ("GU", 0, 2):
                        deviation(act, NC - 2)
                        deviation(act, NC - 1)
                    if kind == "T":
                        modulate(act, c)
                    elif kind == "GU":
                        n = HT * c + e[2]
                        act.wait_ge(gu_done, n + 1)
                        if n >= 2:
                            act.wait_ge(prod_done, n - 1)
                        act.activation(sl[:, n % 2, :], banks[2 * (n % 2)][:, :], ACT.Silu).then_inc(silu_done, 1)
                    elif kind == "DN" and e[2] == HT - 1:
                        act.wait_ge(dn_done, HT * (c + 1))
                        if c:
                            act.wait_ge(o_turned, 2 * c)
                        for f in range(DF):
                            act.activation(fT[:, f, :], banks[6 + f][:, :], ACT.Copy, scale=GB[:, f:f + 1]).then_inc(f_taken, 1)

            @block.tensor
            def _(pe):
                for at, e in enumerate(events):
                    kind, c = e[0], e[1]
                    if kind == "T":
                        if c >= 2:
                            pe.wait_ge(o_added, 2 * (c - 1))
                        else:
                            pe.wait_ge(x1_ready, 2 * NC)
                        turn_norm(pe, c)
                    elif kind == "O":
                        pe.wait_ge(f_taken, 2 * (c + 1))
                        pe.wait_ge(t_taken, 2 * min(c + 2, NC))
                        for f in range(DF):
                            if c == NC - 1:
                                pe.wait_ge(o_added, 2 * c)
                            for k in range(TPC):
                                last = pe.transpose(banks[4 + f][:, k * P:(k + 1) * P], fT[:, f, k * P:(k + 1) * P],
                                                    ident[:, :])
                            last.then_inc(o_turned, 1)
                    elif kind == "GU":
                        n = HT * c + e[2]
                        if e[2] == 0:
                            pe.wait_ge(h_split, 2 * (c + 1))
                        if n >= 2:
                            pe.wait_ge(prod_done, n - 1)
                        cols = slice(e[2] * P, (e[2] + 1) * P)
                        for a in range(2):
                            passes = [(w, h, f) for f in range(DF)
                                      for w, h in ((gu_hi, h_hi), (gu_hi, h_lo), (gu_lo, h_hi))]
                            for q, (w, h, f) in enumerate(passes):
                                last = pe.matmul(banks[2 * (n % 2) + a][:, :], w[:, a, f, cols], h[:, c % 2, f, :],
                                                 start=(q == 0), stop=(q == len(passes) - 1))
                        last.then_inc(gu_done, 1)
                    elif kind == "DN":
                        n = HT * c + e[2]
                        pe.wait_ge(a_split, n + 1)
                        if e[2] == 0 and c:
                            pe.wait_ge(f_taken, 2 * c)
                        for f in range(DF):
                            cols = slice(f * P, (f + 1) * P)
                            for q, (w, a) in enumerate(((dn_hi, a_hi), (dn_hi, a_lo), (dn_lo, a_hi))):
                                last = pe.matmul(banks[6 + f][:, :], w[:, e[2], cols], a[:, n % 2, :],
                                                 start=(e[2] == 0 and q == 0), stop=(e[2] == HT - 1 and q == 2))
                        last.then_inc(dn_done, 1)


_INS = ["L0_attn_x", "L0_attn_W_cq", "L0_attn_q_scale", "L0_attn_W_dq_nope", "L0_attn_W_dq_rope", "L0_attn_W_ckv",
        "L0_attn_kv_scale", "L0_attn_W_dk_nope", "L0_attn_W_dv", "L0_attn_W_krope", "L0_attn_W_o",
        "L0_ffn_wq_gate", "L0_ffn_s_gate", "L0_ffn_wq_up", "L0_ffn_s_up", "L0_ffn_wq_down", "L0_ffn_s_down",
        "L0_c", "L0_wmod"]


def shape_constants():
    f = np.float32
    inv = (f(1.0) / np.power(f(10000.0), np.arange(HALF, dtype=f) * f(2.0) / f(ROPE))).astype(f)
    ang = np.arange(S, dtype=f)[:, None] * inv[None, :]
    cos, sin = np.cos(ang).astype(f), np.sin(ang).astype(f)
    return {
        "ident": np.eye(P, dtype=f),
        "mask": np.where(np.arange(P)[None, :] > np.arange(P)[:, None], f(MASKED), f(0)).astype(f),
        "cos_q": np.ascontiguousarray(np.concatenate([cos.T, cos.T])),
        "sin_q": np.ascontiguousarray(np.concatenate([sin.T, -sin.T])),
        "cos_k": cos / f(NH),
        "sin_k": sin / f(NH),
    }


def kernel(**inputs):
    import concourse.bacc as _bacc
    from concourse.bass_utils import run_bass_kernel_spmd as _run

    nc = _bacc.Bacc("TRN2", target_bir_lowering=False, num_devices=1)
    arrays, args = {}, []
    given = {n: np.ascontiguousarray(inputs[n]) for n in _INS} | shape_constants()
    for name, a in given.items():
        arrays[f"in_{name}_dram"] = a
        args.append(nc.dram_tensor(f"in_{name}_dram", a.shape, mybir.dt.from_np(a.dtype), kind="ExternalInput").ap())
    out = nc.dram_tensor("out_dram", (1, S, D), F32, kind="ExternalOutput").ap()
    adaln_block(nc, *args, out)
    r = _run(nc, [arrays], core_ids=[0])
    return r.results[0]["out_dram"]
```
